# Optimizing a Trainium2 kernel written in Bass

```python
import numpy as np
import jax
import jax.numpy as jnp

def _softmax(x, axis=-1):
    return jax.nn.softmax(x, axis=axis)

def _gelu(x):
    return jax.nn.gelu(x, approximate=True)

def _silu(x):
    return jax.nn.silu(x)

def _sigmoid(x):
    return jax.nn.sigmoid(x)

def _layernorm(x, axis=-1, eps=1e-05):
    m = jnp.mean(x, axis=axis, keepdims=True)
    v = jnp.var(x, axis=axis, keepdims=True)
    return (x - m) / jnp.sqrt(v + eps)

def _scatter_add(tgt, idx, src, axis=0):
    return tgt.at[idx].add(src)

def _segment_sum(src, seg, n):
    return jax.ops.segment_sum(src, seg, n)
kernel_name = 'mk_adj_ffn_d1_adj_r2_b6ed41'

def setup_inputs(seed: int=0):
    np.random.seed(seed)
    _w = jnp.asarray

    def _rec_inputs():
        import jax
        import jax.numpy as jnp
        _gk = jax.random.key(seed)
        x = -0.0002928 + 1 * jax.random.normal(jax.random.fold_in(_gk, 1), (16, 512, 128), jnp.float32)
        _a = jax.random.bernoulli(jax.random.fold_in(_gk, 2), 0.03125, (16, 512, 512))
        adj = _a.astype(jnp.int32)
        return (x, adj)
    x, adj = _rec_inputs()

    def _L0_gnn_setup():
        import jax, jax.numpy as jnp
        import numpy as np
        key = jax.random.key(seed)
        k1, k2, k3, k4 = jax.random.split(key, 4)
        B, N, F, U = (8, 1024, 128, 128)
        x = jax.random.normal(k1, (B, N, F), dtype=jnp.float32)
        adj = jax.random.randint(k2, (B, N, N), 0, 2, dtype=jnp.int32)
        W_msg = jax.random.normal(k3, (F, U), dtype=jnp.float32) / np.sqrt(F)
        W_upd = jax.random.normal(k4, (F, U), dtype=jnp.float32) / np.sqrt(F)
        bias = jnp.zeros((U,), dtype=jnp.float32)
        return {'x': x, 'adj': adj, 'W_msg': W_msg, 'W_upd': W_upd, 'bias': bias}
    _L0_gnn_all = _L0_gnn_setup()
    _L0_gnn_in = {k: v for k, v in _L0_gnn_all.items() if k in ('W_msg', 'W_upd', 'bias')}
    del _L0_gnn_all

    def _L0_ffn_setup():
        import jax, jax.numpy as jnp
        import numpy as np
        B, S, H, NH, NE = (4, 512, 128, 4, 4)
        D = H // NH
        EPS = 1e-08

        def layernorm(x, g, b):
            m = jnp.mean(x, axis=-1, keepdims=True)
            v = jnp.mean((x - m) ** 2, axis=-1, keepdims=True)
            return (x - m) / jnp.sqrt(v + EPS) * g + b
        key = jax.random.key(seed)
        ks = jax.random.split(key, 18)
        sc = 0.05
        return {'x': jax.random.normal(ks[0], (B, S, H), jnp.float32), 'hl_w': jax.random.normal(ks[1], (NH, D, H), jnp.float32) * sc, 'hl_b': jax.random.normal(ks[2], (NH, D), jnp.float32) * sc, 'wq': jax.random.normal(ks[3], (NH, NE, D, D), jnp.float32) * sc, 'wk': jax.random.normal(ks[4], (NH, D, D), jnp.float32) * sc, 'wv': jax.random.normal(ks[5], (NH, D, D), jnp.float32) * sc, 'gate_w': jax.random.normal(ks[6], (NH, NE, NE * D), jnp.float32) * sc, 'gate_b': jax.random.normal(ks[7], (NH, NE), jnp.float32) * sc, 'ln_g': jnp.ones((D,), jnp.float32), 'ln_b': jnp.zeros((D,), jnp.float32), 'fc1_w': jax.random.normal(ks[8], (D, D), jnp.float32) * sc, 'fc1_b': jax.random.normal(ks[9], (D,), jnp.float32) * sc, 'fc2_w': jax.random.normal(ks[10], (D, D), jnp.float32) * sc, 'fc2_b': jax.random.normal(ks[11], (D,), jnp.float32) * sc, 'fnorm_g': jnp.ones((D,), jnp.float32), 'fnorm_b': jnp.zeros((D,), jnp.float32), 'fgate_w': jax.random.normal(ks[12], (NH, H), jnp.float32) * sc}
    _L0_ffn_all = _L0_ffn_setup()
    _L0_ffn_in = {k: v for k, v in _L0_ffn_all.items() if k in ('hl_w', 'hl_b', 'wq', 'wk', 'wv', 'gate_w', 'gate_b', 'ln_g', 'ln_b', 'fc1_w', 'fc1_b', 'fc2_w', 'fc2_b', 'fnorm_g', 'fnorm_b', 'fgate_w')}
    del _L0_ffn_all
    return {'x': x, 'adj': adj, 'L0_gnn_W_msg': _L0_gnn_in['W_msg'], 'L0_gnn_W_upd': _L0_gnn_in['W_upd'], 'L0_gnn_bias': _L0_gnn_in['bias'], 'L0_ffn_hl_w': _L0_ffn_in['hl_w'], 'L0_ffn_hl_b': _L0_ffn_in['hl_b'], 'L0_ffn_wq': _L0_ffn_in['wq'], 'L0_ffn_wk': _L0_ffn_in['wk'], 'L0_ffn_wv': _L0_ffn_in['wv'], 'L0_ffn_gate_w': _L0_ffn_in['gate_w'], 'L0_ffn_gate_b': _L0_ffn_in['gate_b'], 'L0_ffn_ln_g': _L0_ffn_in['ln_g'], 'L0_ffn_ln_b': _L0_ffn_in['ln_b'], 'L0_ffn_fc1_w': _L0_ffn_in['fc1_w'], 'L0_ffn_fc1_b': _L0_ffn_in['fc1_b'], 'L0_ffn_fc2_w': _L0_ffn_in['fc2_w'], 'L0_ffn_fc2_b': _L0_ffn_in['fc2_b'], 'L0_ffn_fnorm_g': _L0_ffn_in['fnorm_g'], 'L0_ffn_fnorm_b': _L0_ffn_in['fnorm_b'], 'L0_ffn_fgate_w': _L0_ffn_in['fgate_w']}

def reference(x, adj, L0_gnn_W_msg, L0_gnn_W_upd, L0_gnn_bias, L0_ffn_hl_w, L0_ffn_hl_b, L0_ffn_wq, L0_ffn_wk, L0_ffn_wv, L0_ffn_gate_w, L0_ffn_gate_b, L0_ffn_ln_g, L0_ffn_ln_b, L0_ffn_fc1_w, L0_ffn_fc1_b, L0_ffn_fc2_w, L0_ffn_fc2_b, L0_ffn_fnorm_g, L0_ffn_fnorm_b, L0_ffn_fgate_w):
    import jax
    import jax.numpy as jnp

    def _L0_gnn_ref(x, adj, W_msg, W_upd, bias):
        import jax, jax.numpy as jnp
        import numpy as np
        a = adj.astype(x.dtype)
        h = jnp.einsum('bnf,fu->bnu', x, W_msg)
        msg_sum = jnp.einsum('bij,biu->bju', a, h)
        deg = jnp.sum(a, axis=1)
        messages = jnp.where(deg[..., None] > 0, msg_sum / jnp.maximum(deg, 1.0)[..., None], 0.0)
        out = jnp.einsum('bnf,fu->bnu', x, W_upd) + messages + bias
        return jax.nn.relu(out)

    def _L0_ffn_ref(x, hl_w, hl_b, wq, wk, wv, gate_w, gate_b, ln_g, ln_b, fc1_w, fc1_b, fc2_w, fc2_b, fnorm_g, fnorm_b, fgate_w):
        import jax, jax.numpy as jnp
        import numpy as np
        B, S, H, NH, NE = (4, 512, 128, 4, 4)
        D = H // NH
        EPS = 1e-08

        def layernorm(x, g, b):
            m = jnp.mean(x, axis=-1, keepdims=True)
            v = jnp.mean((x - m) ** 2, axis=-1, keepdims=True)
            return (x - m) / jnp.sqrt(v + EPS) * g + b
        b, s, h = x.shape
        nh, d, _ = wk.shape
        ne = wq.shape[1]
        sx = jnp.einsum('bsh,ndh->bnsd', x, hl_w) + hl_b[None, :, None, :]
        pad = sx == 0
        q = jnp.einsum('bnsd,neod->bneso', sx, wq)
        k = jnp.einsum('bnsd,nod->bnso', sx, wk)
        v = jnp.einsum('bnsd,nod->bnso', sx, wv)
        causal = jnp.where(jnp.tril(jnp.ones((s, s), bool)), 0.0, -jnp.inf).astype(x.dtype)
        scores = jnp.einsum('bnesd,bntd->bnest', q, k) * d ** 0.5 + causal
        att = jax.nn.softmax(scores, axis=-1)
        qkv = jnp.einsum('bnest,bntd->bnesd', att, v)
        qkv = jnp.where(pad[:, :, None], 0.0, qkv)
        out = jnp.transpose(qkv, (0, 1, 3, 2, 4)).reshape(b, nh, s, ne * d)
        gs = jax.nn.softmax(jnp.einsum('bnsf,nef->bnse', out, gate_w) + gate_b[None, :, None, :], axis=-1)
        mixed = jnp.einsum('bnsed,bnse->bnsd', out.reshape(b, nh, s, ne, d), gs)
        resid = sx[jnp.arange(nh), jnp.arange(nh)]
        hn = layernorm(mixed + resid, ln_g, ln_b)
        f_n = jnp.transpose(hn, (0, 2, 1, 3)).reshape(b, s, h)
        fx = f_n.reshape(b, s, nh, d)
        pm = fx == 0
        hx = jnp.where(pm, 0.0, fx @ fc1_w.T + fc1_b)
        hx = jax.nn.relu(hx)
        hx = jnp.where(pm, 0.0, hx @ fc2_w.T + fc2_b)
        hx = layernorm(hx + fx, fnorm_g, fnorm_b)
        fout = hx.reshape(b, s, h)
        fg = jax.nn.softmax(fout @ fgate_w.T, axis=-1)
        return (fout.reshape(b, s, nh, d) * fg[..., None]).reshape(b, s, h)
    x = x + _L0_gnn_ref(_layernorm(x, axis=-1), adj, L0_gnn_W_msg, L0_gnn_W_upd, L0_gnn_bias)
    x = x + _L0_ffn_ref(_layernorm(x, axis=-1), L0_ffn_hl_w, L0_ffn_hl_b, L0_ffn_wq, L0_ffn_wk, L0_ffn_wv, L0_ffn_gate_w, L0_ffn_gate_b, L0_ffn_ln_g, L0_ffn_ln_b, L0_ffn_fc1_w, L0_ffn_fc1_b, L0_ffn_fc2_w, L0_ffn_fc2_b, L0_ffn_fnorm_g, L0_ffn_fnorm_b, L0_ffn_fgate_w)
    return x

_drawn_inputs = setup_inputs


def setup_inputs(seed=0):
    import zlib

    import numpy as np

    out = dict(_drawn_inputs(seed))
    spreads = {'L0_gnn_bias': (0.0, 0.1),
     'L0_ffn_ln_g': (1.0, 0.2),
     'L0_ffn_ln_b': (0.0, 0.34),
     'L0_ffn_fnorm_g': (1.0, 0.2),
     'L0_ffn_fnorm_b': (0.0, 0.412)}
    factors = {'L0_ffn_wq': 7.608,
     'L0_ffn_wk': 7.498,
     'L0_ffn_wv': 4.353,
     'L0_ffn_gate_w': 8.0,
     'L0_ffn_gate_b': 8.0,
     'L0_ffn_fc1_w': 4.862,
     'L0_ffn_fc1_b': 8.0,
     'L0_ffn_fc2_w': 4.225,
     'L0_ffn_fc2_b': 4.781}
    for name, (base, spread) in spreads.items():
        noise = np.random.default_rng([zlib.crc32(name.encode()), seed]).standard_normal(out[name].shape)
        drawn = base * np.exp(spread * noise) if base else spread * noise
        out[name] = jnp.asarray(drawn.astype(out[name].dtype))
    for name, factor in factors.items():
        out[name] = (out[name] * factor).astype(out[name].dtype)
    return out
```

```python
from contextlib import ExitStack

import numpy as np
import concourse.bass as bass
from concourse import mybir

ALU = mybir.AluOpType
ACT = mybir.ActivationFunctionType
AX = mybir.AxisListType
F32 = mybir.dt.float32
F16 = mybir.dt.float16
BF16 = mybir.dt.bfloat16
I32 = mybir.dt.int32

B, S, H = 16, 512, 128
NH, NE = 4, 4
D = H // NH
P = 128
C = S // P
J = NE * C
EPS_GNN, EPS_FFN = 1e-5, 1e-8
SCALE = float(D) ** 0.5
MSCALE = 64.0
BIG = -1e30
NATW = P + NE * NE
TAIL_LAG = 3
RING = 8

SLOTS = 8
MAX_TILES = [(C * (pos // 4) + (0, 3, 1, 2)[pos % 4], pos) for pos in range(J)]
CHUNKS = [(0, e, 1) for e in range(4)] + [(1, e, 1) for e in range(4)] + [(2, 0, 2), (2, 2, 2), (3, 0, 4)]
CHUNK_SLOT = [0, 0, 1, 2, 2, 3, 4, 5, 5, 6, 7]
PT_OFF = [0, 2048, 3584, 4608]
PT_W = 5120
LAST_CHUNK = [3, 7, 9, 10]
AV_SLOT = {(0, 0): 4, (0, 1): 5, (1, 0): 6, (1, 1): 7, (2, 0): 8, (2, 1): 8, (3, 0): 9, (3, 1): 9}

USES = [
    ("mT", 0, 1), ("q", 0, 2), ("nat0", 0, 3), ("xnT", 0, 3), ("nat1", 0, 4), ("LT", 0, 4), ("hu0", 0, 5), ("hu1", 0, 6),
    ("msg0", 1, 0), ("mT", 1, 1), ("msg1", 1, 1), ("q", 1, 2), ("nat0", 1, 3), ("nat1", 1, 4), ("LT", 1, 4), ("fxT", 1, 4),
    ("h1T", 1, 5),
    ("h2", 2, 0), ("mT", 2, 1), ("q", 2, 2), ("xn2T", 2, 2), ("nat0", 2, 3), ("nat1", 2, 4), ("LT", 2, 4),
    ("sxT", 3, 0), ("mT", 3, 1), ("kT", 3, 1), ("q", 3, 2), ("nat0", 3, 3), ("v", 3, 3), ("nat1", 3, 4), ("LT", 3, 4), ("sxn", 3, 5),
    ("foT", 3, 5), ("fg", 3, 6),
]
BANK = {}
for _u, (_name, _k, _s) in enumerate(USES):
    BANK[_name, _k] = _u % 2


class Phase:

    def __init__(self, v0, count):
        self.v0, self.count = v0, count
        v = v0
        self.att = 0 <= v < B
        self.prep = v + 1 < B
        self.load = v + 2 < B
        self.prev = 1 <= v <= B
        self.tail = TAIL_LAG <= v < B + TAIL_LAG
        self.resid = v + 1 < NH
        self.uses = [(n, k) for n, k, _ in USES if self.has(n, k)]

    def has(self, name, k):
        if name in ("xnT", "hu0", "hu1", "msg0", "msg1", "xn2T", "sxT", "kT", "v"):
            return self.prep
        if name == "sxn":
            return self.prep and self.resid
        if name in ("fxT", "h1T", "h2", "foT", "fg"):
            return self.tail
        return {"q": self.query(k), "mT": self.block(k, 1), "nat0": self.block(k, 3), "nat1": self.block(k, 3),
                "LT": self.block(k, 3)}[name]

    def query(self, k):
        return self.att if k < 3 else self.prep

    def block(self, k, lag):
        return self.att if k >= lag else self.prev


PHASES = [Phase(-1, 1), Phase(0, 1), Phase(1, 1), Phase(2, 1), Phase(3, B - 5), Phase(B - 2, 1), Phase(B - 1, 1), Phase(B, 1),
          Phase(B + 1, 1), Phase(B + 2, 1)]


def use_count(ph, v, name, k):
    bank = BANK[name, k]
    base = 0
    for q in PHASES:
        mine = [u for u in q.uses if BANK[u] == bank]
        if q is ph:
            at = base + mine.index((name, k))
            return bank, (at if isinstance(v, int) else (v - ph.v0) * len(mine) + at)
        base += q.count * len(mine)


def use_before(ph, v, name, k):
    if k > 0:
        if not ph.has(name, k - 1):
            return None
        bank, c = use_count(ph, v, name, k - 1)
        return bank, c + 1
    if ph is PHASES[0] or not PHASES[PHASES.index(ph) - 1].has(name, 3):
        return None
    return BANK[name, 3], iteration_start(ph, v, BANK[name, 3])


def iteration_start(ph, v, bank):
    base = 0
    for q in PHASES:
        mine = len([u for u in q.uses if BANK[u] == bank])
        if q is ph:
            return base if isinstance(v, int) else (v - ph.v0) * mine + base
        base += q.count * mine


class Steps:

    def __init__(self, sem, names):
        self.sem, self.names = sem, names

    def after(self, b, name):
        return b * len(self.names) + self.names.index(name) + 1


def wait(eng, sem, value):
    if not isinstance(value, int) or value > 0:
        eng.wait_ge(sem, value)


def head(v, k, lag):
    return (v, k - lag) if k >= lag else (v - 1, k - lag + 4)


def build(nc, x, adj, w_mu, gnn_b, hlwT, hlb, wq, wk, wv, gw, gb, ln_g, ln_b, fc1, fc1_b, fc2, fc2_b, fn_g, fn_b, fgT,
          out):
    ctx = ExitStack()
    with ctx:
        def sb(name, shape, dt=F32):
            return ctx.enter_context(nc.sbuf_tensor(name, shape, dt))

        def sem(name):
            return ctx.enter_context(nc.semaphore(name))

        ident = sb("ident", [P, P])
        ident16 = sb("ident16", [P, P], F16)
        identb = sb("identb", [P, P], BF16)
        maskneg = sb("maskneg", [P, P], BF16)
        masknegT = sb("masknegT", [P, NE, P], BF16)
        ones = sb("ones", [P, D])
        mhalf = sb("mhalf", [P, 16])
        w_mu_s = sb("w_mu_s", [P, 2 * H])
        gnnb_s = sb("gnnb_s", [P, H])
        hlwT_s = sb("hlwT_s", [P, H])
        hlb_s = sb("hlb_s", [P, 1])
        wq_s = sb("wq_s", [P, NH, NE * D])
        wk_s = sb("wk_s", [P, H])
        wv_s = sb("wv_s", [P, H])
        nat_w = sb("nat_w", [P, NH, NATW])
        gb_s = sb("gb_s", [P, NH, NE])
        lng_s = sb("lng_s", [P, D])
        lnb_s = sb("lnb_s", [P, D])
        fc1_s = sb("fc1_s", [P, H])
        fc1b_s = sb("fc1b_s", [P, 1])
        fc2_s = sb("fc2_s", [P, H])
        fc2b_s = sb("fc2b_s", [P, D])
        fng_s = sb("fng_s", [P, D])
        fnb_s = sb("fnb_s", [P, D])
        fgT_s = sb("fgT_s", [P, NH])

        xin = sb("xin", [P, C, H])
        adj_i = sb("adj_i", [P, C, S], I32)
        adj_f = sb("adj_f", [P, C, S])
        bst = sb("bst", [P, C, 6])
        mv = sb("mv", [P, C, 2])
        ve = sb("ve", [P, C])
        rs = sb("rs", [P, C])
        xn = sb("xn", [P, C, H])
        xnT = sb("xnT", [P, S])
        hS = sb("hS", [P, C, 132])
        upd = sb("upd", [P, C, H])
        dmax = sb("dmax", [P, 2])
        drec = sb("drec", [P, 2])
        dgs = sb("dgs", [P, 2])
        agg = sb("agg", [P, C, H])
        x2 = sb("x2", [P, C, H])
        sxT = sb("sxT", [P, S])
        nzT = sb("nzT", [P, S], BF16)
        khi = sb("khi", [P, S], F16)
        klo = sb("klo", [P, S], F16)
        vnew = sb("vnew", [P, C, H])
        resid = sb("resid", [P, C, NH, D])
        x2ring = sb("x2ring", [P, RING, C * H])
        mixring = sb("mixring", [P, RING, C * H])

        qhi = sb("qhi", [P, S], F16)
        qlo = sb("qlo", [P, S], F16)
        QT = sb("QT", [98, NH, NE, S], F16)
        KT = sb("KT", [98, NH, S], F16)
        V = sb("V", [P, NH, C, D])
        mx = sb("mx", [P, 2, J])
        m2 = sb("m2", [P, 2 * J], F16)
        mT = sb("mT", [2 * J, P], F16)
        PT = sb("PT", [P, 2, PT_W])
        mrep = sb("mrep", [P, NH, S], BF16)
        Om = sb("Om", [P, S])
        Lsb = sb("Lsb", [P, S])
        nat = sb("nat", [P, NH, C, NATW])
        rL = sb("rL", [P, NH, C, NE])

        G16 = NH * C
        zr = sb("zr", [P, G16, NE, NE])
        lg = sb("lg", [P, G16, NE])
        lgb = sb("lgb", [P, G16, NE])
        lmax = sb("lmax", [P, G16])
        lsub = sb("lsub", [P, G16, NE])
        lex = sb("lex", [P, G16, NE])
        lsum = sb("lsum", [P, G16])
        lrec = sb("lrec", [P, G16])
        lw = sb("lw", [P, G16, NE])
        lw2 = sb("lw2", [P, G16, NE])
        prod = sb("prod", [P, 2, C, NE, D])
        half = sb("half", [P, 2, C, 2, D])
        mixed = sb("mixed", [P, C, NH, D])

        ty = sb("ty", [P, G16, D])
        tsum = sb("tsum", [P, G16])
        tmean = sb("tmean", [P, G16])
        txc = sb("txc", [P, G16, D])
        tsq = sb("tsq", [P, G16, D])
        tvs = sb("tvs", [P, G16])
        tve = sb("tve", [P, G16])
        trs = sb("trs", [P, G16])
        txs = sb("txs", [P, G16, D])
        tg = sb("tg", [P, G16, D])
        fx = sb("fx", [P, G16, D])
        fxT = sb("fxT", [P, S])
        nzf = sb("nzf", [P, S])
        h1r = sb("h1r", [P, S])
        h1m = sb("h1m", [P, S])
        u2 = sb("u2", [P, G16, D])
        w2 = sb("w2", [P, G16, D])
        fo = sb("fo", [P, G16, D])
        foT = sb("foT", [P, S])
        fmax = sb("fmax", [P, C])
        fsub = sb("fsub", [P, C, NH])
        fex = sb("fex", [P, C, NH])
        fsum = sb("fsum", [P, C])
        frec = sb("frec", [P, C])
        fgs = sb("fgs", [P, C, NH])
        fmul = sb("fmul", [P, G16, D])
        outb = sb("outb", [P, C * H])

        MX = ctx.enter_context(nc.psum_tensor("MX", [P, 2, 512], F32))
        ST = ctx.enter_context(nc.psum_tensor("ST", [P, 2, 512], F32))
        O = ctx.enter_context(nc.psum_tensor("O", [P, 512], F32))
        L = ctx.enter_context(nc.psum_tensor("L", [P, 512], F32))
        SH = ctx.enter_context(nc.psum_tensor("SH", [P, 2, 512], F32))

        w_in = sem("weights_loaded")
        zero_done = sem("weights_zeroed")
        c_done = sem("constants_built")
        k_rows = sem("key_rows_set")
        passed = sem("waits_passed")
        x_in = sem("x_loaded")
        adj_in = sem("adj_loaded")
        x2_kept = sem("x2_kept")
        mix_kept = sem("mixed_kept")
        out_done = sem("out_stored")
        q_in = [sem(f"q_loaded{n}") for n in range(NH)]
        k_in = [sem(f"k_loaded{n}") for n in range(NH)]
        m_in = [sem(f"max_loaded{n}") for n in range(NH)]
        mask_in = [sem(f"mask_loaded{n}") for n in range(NH)]
        sh_full = [sem(f"shared_full{i}") for i in range(2)]
        sh_free = [sem(f"shared_free{i}") for i in range(2)]
        mx_full = sem("max_scores_full")
        mx_free = sem("max_scores_reduced")
        st_full = sem("scores_full")
        exp_done = sem("exp_done")
        av_done = sem("av_done")
        adjf_free = sem("adj_multiplied")
        m2_done = sem("max_split")
        v_copied = sem("v_copied")
        om_done = sem("outputs_masked")
        ls_done = sem("sums_copied")
        qhi_done = sem("q_high")
        khi_done = sem("k_high")
        g_dve = Steps(sem("prep_vector"), ("stats", "aggr", "var", "xn", "adj", "deg0", "rec0", "gs0", "agg0", "deg1", "rec1",
                                           "gs1", "agg1", "x2", "stats2", "aggr2", "var2", "xn2", "nz"))
        g_act = Steps(sem("prep_scalar"), ("h0", "h1"))
        g_pool = Steps(sem("prep_pool"), ("rs", "rs2"))
        x_dve = Steps(sem("mix_vector"), ("zr", "lg", "lgb", "lmax", "lsub", "lsum", "lrec", "lw", "lw2"))
        x_act = Steps(sem("mix_scalar"), ("lex",))
        x_pool = Steps(sem("mix_pool"), tuple(f"{w}{n}" for n in range(NH) for w in ("prod", "half", "mixed")))
        t_dve = Steps(sem("tail_vector"), ("y", "sum", "mean", "xc", "vs", "ve", "xs", "nzf", "u", "w", "y2", "sum2", "mean2",
                                           "xc2", "vs2", "ve2", "xs2", "fmax", "fsub", "fsum", "frec", "fgs", "out"))
        t_act = Steps(sem("tail_scalar"), ("sq", "sq2", "fex"))
        t_pool = Steps(sem("tail_pool"), ("rs", "g", "fx", "h1m", "rs2", "g2", "fo", "fmul"))

        block = ctx.enter_context(nc.Block())

        def held(eng):
            eng.sem_inc(passed, 1)

        def run(eng, body):
            for ph in PHASES:
                if ph.count == 1:
                    body(ph, ph.v0)
                else:
                    with eng.Fori(ph.v0, ph.v0 + ph.count) as v:
                        body(ph, v)

        def bcast(ap, n):
            return ap.unsqueeze(0).to_broadcast([n] + list(ap.shape)) if False else ap.partition_broadcast(n)

        @block.sync
        def _(sp):
            def ready(sem, value):
                if not isinstance(value, int) or value > 0:
                    sp.wait_ge(sem, value)
                    held(sp)

            def loads(b):
                if isinstance(b, int):
                    xb, ab = x[b], adj[b]
                else:
                    xb, ab = x[bass.ds(b, 1)].rearrange("a s f -> (a s) f"), adj[bass.ds(b, 1)].rearrange("a s f -> (a s) f")
                ready(g_dve.sem, g_dve.after(b - 1, "x2"))
                sp.dma_start(xin[:], xb.rearrange("(c p) f -> p c f", p=P)).then_inc(x_in, 16)
                ready(g_dve.sem, g_dve.after(b - 1, "adj"))
                sp.dma_start(adj_i[:], ab.rearrange("(c p) j -> p c j", p=P)).then_inc(adj_in, 16)

            loads(0)
            sp.dma_start(w_mu_s[:, 0:H], w_mu[0]).then_inc(w_in, 16)
            sp.dma_start(w_mu_s[:, H:2 * H], w_mu[1]).then_inc(w_in, 16)
            sp.dma_start(hlwT_s[:], hlwT).then_inc(w_in, 16)
            sp.dma_start(hlb_s[:], hlb).then_inc(w_in, 16)
            sp.dma_start(fgT_s[:], fgT).then_inc(w_in, 16)
            for dst, src in ((gnnb_s[:], gnn_b), (gb_s[:].rearrange("p n e -> p (n e)"), gb), (lng_s[:], ln_g),
                             (lnb_s[:], ln_b), (fc2b_s[:], fc2_b), (fng_s[:], fn_g), (fnb_s[:], fn_b)):
                sp.dma_start(dst, src.to_broadcast([P, src.shape[1]])).then_inc(w_in, 16)
            sp.wait_ge(zero_done, 1)
            for n in range(NH):
                r = slice(D * n, D * n + D)
                sp.dma_start(wq_s[r, n, :], wq[n]).then_inc(w_in, 16)
                sp.dma_start(wk_s[r, r], wk[n]).then_inc(w_in, 16)
                sp.dma_start(wv_s[r, r], wv[n]).then_inc(w_in, 16)
                sp.dma_start(fc1_s[r, r], fc1).then_inc(w_in, 16)
                sp.dma_start(fc2_s[r, r], fc2).then_inc(w_in, 16)
                sp.dma_start(fc1b_s[r, :], fc1_b).then_inc(w_in, 16)
            for n in range(NH):
                for e in range(NE):
                    sp.dma_start(nat_w[D * e:D * e + D, n, P + NE * e:P + NE * e + NE], gw[n, e]).then_inc(w_in, 16)

            def body(ph, v):
                for k in range(4):
                    if k < 3 and ph.att:
                        load_keys(v, k + 1)
                    if ph.att:
                        load_mask(v, k)
                    if ph.block(k, 1):
                        b, n = head(v, k, 1)
                        bank, c = use_count(ph, v, "mT", k)
                        ready(sh_free[bank], c + 1)
                        sp.dma_start(QT[96:98, n].rearrange("r e (c s) -> r (e c) s", s=P), mT[:]).then_inc(m_in[n], 16)
                    if ph.query(k):
                        b, n = (v, k + 1) if k < 3 else (v + 1, 0)
                        bank, c = use_count(ph, v, "q", k)
                        ready(sh_free[bank], c + 1)
                        ready(st_full, (b - 1) * 44 + (n + 1) * 11)
                        for e in range(NE):
                            r = slice(D * e, D * e + D)
                            sp.dma_start(QT[0:D, n, e, :], qhi[r, :]).then_inc(q_in[n], 16)
                            sp.dma_start(QT[D:2 * D, n, e, :], qhi[r, :]).then_inc(q_in[n], 16)
                            sp.dma_start(QT[2 * D:3 * D, n, e, :], qlo[r, :]).then_inc(q_in[n], 16)
                    if k == 1 and ph.prep:
                        ready(g_dve.sem, g_dve.after(v + 1, "x2"))
                        keep(x2ring, v + 1, x2[:].rearrange("p c f -> p (c f)"), x2_kept)
                        if ph.load:
                            loads(v + 2)
                    if k == 3 and ph.prep:
                        load_keys(v + 1, 0)
                    if k == 3 and ph.prev:
                        ready(x_pool.sem, x_pool.after(v - 1, "mixed3"))
                        keep(mixring, v - 1, mixed[:].rearrange("p c n d -> p (c n d)"), mix_kept)
                    if k == 3 and ph.tail:
                        b = v - TAIL_LAG
                        ready(t_dve.sem, t_dve.after(b, "out"))
                        ob = out[b] if isinstance(b, int) else out[bass.ds(b, 1)].rearrange("a s f -> (a s) f")
                        sp.dma_start(ob.rearrange("(c p) f -> p c f", p=P),
                                     outb[:].rearrange("p (c f) -> p c f", c=C)).then_inc(out_done, 16)

            def keep(ring, b, src, done):
                dst = ring[:, b % RING] if isinstance(b, int) else ring[:, bass.ds(b % RING, 1)].rearrange("p a f -> p (a f)")
                sp.dma_start(dst, src).then_inc(done, 16)

            def load_keys(b, n):
                ready(khi_done, (b + 1) * 2)
                ready(st_full, (b - 1) * 44 + (n + 1) * 11)
                r = slice(D * n, D * n + D)
                sp.dma_start(KT[0:D, n, :], khi[r, :]).then_inc(k_in[n], 16)
                sp.dma_start(KT[D:2 * D, n, :], klo[r, :]).then_inc(k_in[n], 16)
                sp.dma_start(KT[2 * D:3 * D, n, :], khi[r, :]).then_inc(k_in[n], 16)

            def load_mask(b, n):
                ready(g_dve.sem, g_dve.after(b, "nz"))
                ready(om_done, (b - 1) * 4 + n + 1)
                for e in range(NE):
                    sp.dma_start(mrep[D * e:D * e + D, n, :], nzT[D * n:D * n + D, :]).then_inc(mask_in[n], 16)

            run(sp, body)
            sp.wait_ge(out_done, 16 * B)

        N_W = 12 + 6 * NH + NH * NE

        @block.gpsimd
        def _(pool):
            for t in (wk_s, wv_s, fc1_s, fc2_s):
                pool.memset(t[:], 0.0)
            pool.memset(nat_w[:], 0.0)
            pool.memset(wq_s[:], 0.0).then_inc(zero_done, 1)
            for t in (ident, ident16, identb):
                pool.memset(t[:], 0.0)
            pool.memset(maskneg[:], 0.0)
            pool.memset(masknegT[:], 0.0)
            pool.memset(ones[:], 1.0)
            pool.memset(mhalf[:], -0.5)
            pool.memset(hS[:, :, H:H + 1], 1.0)
            pool.memset(hS[:, :, H + 1:132], 0.0).then_inc(c_done, 1)
            pool.wait_ge(c_done, 1)
            for t in (ident, ident16, identb):
                pool.affine_select(out=t[:], in_=t[:], compare_op=ALU.not_equal, fill=1.0, base=0, pattern=[[-1, P]],
                                   channel_multiplier=1)
            for n in range(NH):
                pool.affine_select(out=nat_w[:, n, 0:P], in_=nat_w[:, n, 0:P], compare_op=ALU.not_equal, fill=1.0, base=0,
                                   pattern=[[-1, P]], channel_multiplier=1)
            pool.affine_select(out=masknegT[:], in_=masknegT[:], compare_op=ALU.is_ge, fill=BIG, base=0,
                               pattern=[[0, NE], [1, P]], channel_multiplier=-1)
            pool.affine_select(out=maskneg[:], in_=maskneg[:], compare_op=ALU.is_ge, fill=BIG, base=0, pattern=[[-1, P]],
                               channel_multiplier=1).then_inc(c_done, 1)
            pool.wait_ge(c_done, 2)

            def power(steps, b, name, dst, src):
                pool.tensor_tensor(dst, src, mhalf[:, 0:src.shape[-1]], ALU.pow).then_inc(steps.sem, 1)

            def body(ph, v):
                for k in range(4):
                    for s in range(SLOTS):
                        at = (k, s)
                        if ph.prep and at == (0, 0):
                            pool.wait_ge(g_dve.sem, g_dve.after(v + 1, "var"))
                            power(g_pool, v + 1, "rs", rs[:], ve[:])
                        if ph.prep and at == (1, 6):
                            pool.wait_ge(g_dve.sem, g_dve.after(v + 1, "var2"))
                            power(g_pool, v + 1, "rs2", rs[:], ve[:])
                        if ph.prev and at in ((2, 7), (3, 1), (3, 3), (3, 5)):
                            mix(v - 1, {(2, 7): 0, (3, 1): 1, (3, 3): 2, (3, 5): 3}[at])
                        if ph.tail:
                            tail(ph, v, v - TAIL_LAG, at)

            def mix(b, n):
                if n == 0:
                    pool.wait_ge(x_dve.sem, x_dve.after(b, "lw2"))
                if n >= 2:
                    pool.wait_ge(x_pool.sem, x_pool.after(b, f"half{n - 2}"))
                else:
                    wait(pool, x_pool.sem, x_pool.after(b - 1, f"half{n + 2}"))
                w = lw2[:, n * C:n * C + C, :].unsqueeze(3).to_broadcast([P, C, NE, D])
                pool.tensor_tensor(prod[:, n % 2], nat[:, n, :, 0:P].rearrange("p c (e d) -> p c e d", d=D), w,
                                   ALU.mult).then_inc(x_pool.sem, 1)
                pool.wait_ge(x_pool.sem, x_pool.after(b, f"prod{n}"))
                pool.tensor_tensor(half[:, n % 2], prod[:, n % 2, :, 0:2, :], prod[:, n % 2, :, 2:4, :],
                                   ALU.add).then_inc(x_pool.sem, 1)
                pool.wait_ge(x_pool.sem, x_pool.after(b, f"half{n}"))
                if n == 0:
                    wait(pool, mix_kept, b * 16)
                pool.tensor_tensor(mixed[:, :, n, :], half[:, n % 2, :, 0, :], half[:, n % 2, :, 1, :],
                                   ALU.add).then_inc(x_pool.sem, 1)

            def tail(ph, v, b, at):
                gbc = lng_s[:].unsqueeze(1).to_broadcast([P, G16, D])
                bbc = lnb_s[:].unsqueeze(1).to_broadcast([P, G16, D])
                gbc2 = fng_s[:].unsqueeze(1).to_broadcast([P, G16, D])
                bbc2 = fnb_s[:].unsqueeze(1).to_broadcast([P, G16, D])
                if at == (0, 6):
                    pool.wait_ge(t_dve.sem, t_dve.after(b, "ve"))
                    power(t_pool, b, "rs", trs[:], tve[:])
                if at == (1, 0):
                    pool.wait_ge(t_dve.sem, t_dve.after(b, "xs"))
                    pool.tensor_tensor(tg[:], txs[:], gbc, ALU.mult).then_inc(t_pool.sem, 1)
                if at == (1, 1):
                    pool.wait_ge(t_pool.sem, t_pool.after(b, "g"))
                    pool.tensor_tensor(fx[:], tg[:], bbc, ALU.add).then_inc(t_pool.sem, 1)
                if at == (1, 6):
                    bank, c = use_count(ph, v, "h1T", 1)
                    pool.wait_ge(sh_free[bank], c + 1)
                    pool.wait_ge(t_dve.sem, t_dve.after(b, "nzf"))
                    pool.tensor_tensor(h1m[:], h1r[:], nzf[:], ALU.mult).then_inc(t_pool.sem, 1)
                if at == (2, 5):
                    pool.wait_ge(t_dve.sem, t_dve.after(b, "ve2"))
                    power(t_pool, b, "rs2", trs[:], tve[:])
                if at == (2, 6):
                    pool.wait_ge(t_dve.sem, t_dve.after(b, "xs2"))
                    pool.tensor_tensor(tg[:], txs[:], gbc2, ALU.mult).then_inc(t_pool.sem, 1)
                if at == (3, 0):
                    pool.wait_ge(t_pool.sem, t_pool.after(b, "g2"))
                    pool.tensor_tensor(fo[:], tg[:], bbc2, ALU.add).then_inc(t_pool.sem, 1)
                if at == (3, 7):
                    pool.wait_ge(t_dve.sem, t_dve.after(b, "fgs"))
                    g = fgs[:].rearrange("p c n -> p (c n)").unsqueeze(2).to_broadcast([P, G16, D])
                    pool.tensor_tensor(fmul[:], fo[:], g, ALU.mult).then_inc(t_pool.sem, 1)

            pool.wait_ge(w_in, 16 * N_W)
            run(pool, body)

        @block.tensor
        def _(pe):
            pe.wait_ge(c_done, 2)
            pe.wait_ge(k_rows, 1)
            pe.wait_ge(w_in, 16 * N_W)

            def body(ph, v):
                def shared(name, k):
                    bank, c = use_count(ph, v, name, k)
                    wait(pe, sh_free[bank], c)
                    return SH[:, bank], sh_full[bank]

                def done(name, k, lag_v=0):
                    bank, c = use_count(ph, v, name, k)
                    pe.wait_ge(sh_free[bank], c + 1)

                def maxima(b, n, j, pos):
                    g = (b * 4 + n) * J + pos
                    if pos == 0:
                        pe.wait_ge(q_in[n], (b + 1) * 16 * 12)
                        pe.wait_ge(k_in[n], (b + 1) * 16 * 3)
                    wait(pe, mx_free, g - 1)
                    bank = MX[:, pos % 2]
                    e, c = j // C, j % C
                    nc.tensor.matmul(bank[:, 0:P * (c + 1)], QT[0:96, n, e, P * c:P * c + P], KT[0:96, n, 0:P * (c + 1)],
                                     start=True, stop=False)
                    nc.tensor.matmul(bank[:, P * c:P * c + P], identb[:], maskneg[:], start=False, stop=True).then_inc(mx_full, 1)

                def scores(b, n, c):
                    t, e0, ne = CHUNKS[c]
                    g = (b * 4 + n) * 11 + c
                    if c == 0:
                        pe.wait_ge(m_in[n], (b + 1) * 16)
                    wait(pe, exp_done, g - 1)
                    w = S - P * t
                    for i in range(ne):
                        nc.tensor.matmul(ST[:, (11 * n + c) % 2, i * w:i * w + w], KT[:, n, P * t:P * t + P],
                                         QT[:, n, e0 + i, P * t:S], start=(i == 0), stop=False)
                    diag = ST[:, (11 * n + c) % 2, 0:ne * w].rearrange("p (e s) -> p e s", e=ne)[:, :, 0:P]
                    nc.tensor.matmul(diag, identb[:], masknegT[:, 0:ne, :], start=False, stop=True).then_inc(st_full, 1)

                def values(b, n, t, what):
                    if what == 0:
                        pe.wait_ge(exp_done, (b * 4 + n) * 11 + LAST_CHUNK[t] + 1)
                        if t == 0:
                            pe.wait_ge(v_copied, b * 4 + n + 1)
                            wait(pe, om_done, b * 4 + n)
                    elif t == 0:
                        wait(pe, ls_done, b * 4 + n)
                    w = S - P * t
                    for e in range(NE):
                        a = PT_OFF[t] + e * w
                        mm = nc.tensor.matmul((L if what else O)[D * e:D * e + D, P * t:S], ones[:] if what else V[:, n, t, :],
                                              PT[:, n % 2, a:a + w], start=(t == 0), stop=(t == C - 1))
                    if t == C - 1 and what == 1:
                        mm.then_inc(av_done, 1)

                def transposes(dst, src, full):
                    for c in range(C):
                        mm = nc.tensor.transpose(dst[:, c * P:c * P + P], src[:, c, :], ident[:])
                    mm.then_inc(full, 1)

                def side(k, s):
                    for name, uk, us in USES:
                        if (uk, us) != (k, s) or not ph.has(name, k):
                            continue
                        shared_use(name, k)

                def shared_use(name, k):
                    if name == "mT":
                        b, n = head(v, k, 1)
                        pe.wait_ge(m2_done, (b * 4 + n + 1) * 2)
                        dst, full = shared(name, k)
                        nc.tensor.transpose(dst.bitcast(F16)[0:2 * J, 0:P], m2[:], ident16[:]).then_inc(full, 1)
                    elif name == "q":
                        n = (k + 1) % 4
                        if k == 3:
                            done("sxT", 3)
                        dst, full = shared(name, k)
                        nc.tensor.matmul(dst, wq_s[:, n, :], sxT[:], start=True, stop=True).then_inc(full, 1)
                    elif name in ("nat0", "nat1"):
                        b, n = head(v, k, 3)
                        if name == "nat0":
                            pe.wait_ge(om_done, b * 4 + n + 1)
                        dst, full = shared(name, k)
                        for i in range(2):
                            c = 2 * int(name[3]) + i
                            mm = nc.tensor.matmul(dst[:, i * NATW:i * NATW + NATW], Om[:, c * P:c * P + P], nat_w[:, n, :],
                                                  start=True, stop=True)
                        mm.then_inc(full, 1)
                    elif name == "LT":
                        b, n = head(v, k, 3)
                        pe.wait_ge(ls_done, b * 4 + n + 1)
                        dst, full = shared(name, k)
                        transposes(dst, Lsb[:].rearrange("p (c s) -> p c s", c=C), full)
                    elif name == "xnT":
                        pe.wait_ge(g_dve.sem, g_dve.after(v + 1, "xn"))
                        dst, full = shared(name, k)
                        transposes(dst, xn, full)
                    elif name in ("hu0", "hu1"):
                        done("xnT", 0)
                        dst, full = shared(name, k)
                        for i in range(2):
                            c = 2 * int(name[2]) + i
                            mm = nc.tensor.matmul(dst[:, i * 256:i * 256 + 256], xnT[:, c * P:c * P + P], w_mu_s[:],
                                                  start=True, stop=True)
                        mm.then_inc(full, 1)
                    elif name in ("msg0", "msg1"):
                        if name == "msg0":
                            pe.wait_ge(g_act.sem, g_act.after(v + 1, "h1"))
                            pe.wait_ge(g_dve.sem, g_dve.after(v + 1, "adj"))
                        dst, full = shared(name, k)
                        for i in range(2):
                            jc = 2 * int(name[3]) + i
                            for ic in range(C):
                                mm = nc.tensor.matmul(dst[:, i * 130:i * 130 + 130], adj_f[:, ic, jc * P:jc * P + P],
                                                      hS[:, ic, 0:130], start=(ic == 0), stop=(ic == C - 1))
                        mm.then_inc(full, 1)
                    elif name == "xn2T":
                        pe.wait_ge(g_dve.sem, g_dve.after(v + 1, "xn2"))
                        dst, full = shared(name, k)
                        transposes(dst, xn, full)
                    elif name == "sxT":
                        done("xn2T", 2)
                        dst, full = shared(name, k)
                        nc.tensor.matmul(dst, hlwT_s[:], xnT[:], start=True, stop=True).then_inc(full, 1)
                    elif name == "kT":
                        done("sxT", 3)
                        dst, full = shared(name, k)
                        nc.tensor.matmul(dst, wk_s[:], sxT[:], start=True, stop=True).then_inc(full, 1)
                    elif name == "v":
                        dst, full = shared(name, k)
                        for c in range(C):
                            mm = nc.tensor.matmul(dst[:, c * P:c * P + P], sxT[:, c * P:c * P + P], wv_s[:],
                                                  start=True, stop=True)
                        mm.then_inc(full, 1)
                    elif name == "sxn":
                        dst, full = shared(name, k)
                        transposes(dst, sxT[:].rearrange("p (c s) -> p c s", c=C), full)
                    elif name == "fxT":
                        pe.wait_ge(t_pool.sem, t_pool.after(v - TAIL_LAG, "fx"))
                        dst, full = shared(name, k)
                        transposes(dst, fx[:].rearrange("p (c n) d -> p c (n d)", c=C), full)
                    elif name == "h1T":
                        done("fxT", 1)
                        dst, full = shared(name, k)
                        nc.tensor.matmul(dst, fc1_s[:], fxT[:], start=True, stop=True).then_inc(full, 1)
                    elif name == "h2":
                        pe.wait_ge(t_pool.sem, t_pool.after(v - TAIL_LAG, "h1m"))
                        dst, full = shared(name, k)
                        for c in range(C):
                            mm = nc.tensor.matmul(dst[:, c * P:c * P + P], h1m[:, c * P:c * P + P], fc2_s[:],
                                                  start=True, stop=True)
                        mm.then_inc(full, 1)
                    elif name == "foT":
                        pe.wait_ge(t_pool.sem, t_pool.after(v - TAIL_LAG, "fo"))
                        dst, full = shared(name, k)
                        transposes(dst, fo[:].rearrange("p (c n) d -> p c (n d)", c=C), full)
                    elif name == "fg":
                        done("foT", 3)
                        dst, full = shared(name, k)
                        for c in range(C):
                            mm = nc.tensor.matmul(dst[:, c * NH:c * NH + NH], foT[:, c * P:c * P + P], fgT_s[:],
                                                  start=True, stop=True)
                        mm.then_inc(full, 1)

                for k in range(4):
                    for s in range(SLOTS):
                        if ph.block(k, 2):
                            b, n = head(v, k, 2)
                            for c in range(11):
                                if CHUNK_SLOT[c] == s:
                                    scores(b, n, c)
                        if ph.att:
                            maxima(v, k, *MAX_TILES[2 * s])
                            maxima(v, k, *MAX_TILES[2 * s + 1])
                        for (t, what), at in AV_SLOT.items():
                            lag = 2 + at // SLOTS
                            if at % SLOTS == s and ph.block(k, lag):
                                values(*head(v, k, lag), t, what)
                        side(k, s)

            run(pe, body)

        @block.scalar
        def _(act):
            act.wait_ge(w_in, 16 * N_W)

            def body(ph, v):
                def full(name, k):
                    bank, c = use_count(ph, v, name, k)
                    act.wait_ge(sh_full[bank], c + 1)
                    return SH[:, bank], sh_free[bank]

                def exps(b, n, c):
                    t, e0, ne = CHUNKS[c]
                    g = (b * 4 + n) * 11 + c
                    if c == 0:
                        wait(act, av_done, b * 4 + n - 1)
                    act.wait_ge(st_full, g + 1)
                    w = S - P * t
                    a = PT_OFF[t] + e0 * w
                    nc.scalar.activation(PT[:, n % 2, a:a + ne * w], ST[:, (11 * n + c) % 2, 0:ne * w], ACT.Exp,
                                         scale=SCALE).then_inc(exp_done, 1)

                def side(k, s):
                    for name, uk, us in USES:
                        if (uk, us) != (k, s) or not ph.has(name, k):
                            continue
                        read(name, k)

                def read(name, k):
                    if name == "mT":
                        b, n = head(v, k, 1)
                        src, free = full(name, k)
                        for m in range(NH):
                            if m == (n - 1) % 4:
                                wait(act, m_in[m], (b + 1) * 16 if n else b * 16)
                        nc.scalar.copy(mT[:], src.bitcast(F16)[0:2 * J, 0:P]).then_inc(free, 1)
                    elif name == "q":
                        b, n = (v, k + 1) if k < 3 else (v + 1, 0)
                        src, _ = full(name, k)
                        m = (n - 1) % 4
                        wait(act, q_in[m], ((b + 1) if n else b) * 16 * 12)
                        nc.scalar.copy(qhi[:], src).then_inc(qhi_done, 1)
                    elif name in ("nat0", "nat1"):
                        b, n = head(v, k, 3)
                        i = 2 * int(name[3])
                        src, free = full(name, k)
                        wait(act, x_pool.sem, x_pool.after(b - 1, f"prod{n}"))
                        nc.scalar.copy(nat[:, n, i:i + 2, :], src[:, 0:2 * NATW].rearrange("p (c w) -> p c w", c=2)).then_inc(free, 1)
                    elif name in ("xnT", "xn2T"):
                        src, free = full(name, k)
                        nc.scalar.copy(xnT[:], src).then_inc(free, 1)
                    elif name in ("hu0", "hu1"):
                        i = 2 * int(name[2])
                        src, _ = full(name, k)
                        nc.scalar.copy(hS[:, i:i + 2, 0:H], src.rearrange("p (c w) -> p c w", c=2)[:, :, 0:H]).then_inc(g_act.sem, 1)
                    elif name == "sxT":
                        src, free = full(name, k)
                        nc.scalar.activation(sxT[:], src, ACT.Identity, bias=hlb_s[:]).then_inc(free, 1)
                    elif name == "kT":
                        src, _ = full(name, k)
                        wait(act, k_in[3], (v + 1) * 48)
                        nc.scalar.copy(khi[:], src).then_inc(khi_done, 1)
                    elif name == "v":
                        src, free = full(name, k)
                        wait(act, v_copied, 4 * (v + 1))
                        nc.scalar.copy(vnew[:].rearrange("p c f -> p (c f)"), src).then_inc(free, 1)
                    elif name == "fxT":
                        src, free = full(name, k)
                        nc.scalar.copy(fxT[:], src).then_inc(free, 1)
                    elif name == "h1T":
                        src, free = full(name, k)
                        nc.scalar.activation(h1r[:], src, ACT.Relu, bias=fc1b_s[:]).then_inc(free, 1)
                    elif name == "foT":
                        src, free = full(name, k)
                        nc.scalar.copy(foT[:], src).then_inc(free, 1)

                for k in range(4):
                    for s in range(SLOTS):
                        if ph.block(k, 2):
                            b, n = head(v, k, 2)
                            for c in range(11):
                                if CHUNK_SLOT[c] == s:
                                    exps(b, n, c)
                        if ph.block(k, 3) and s == 2:
                            b, n = head(v, k, 3)
                            act.wait_ge(av_done, b * 4 + n + 1)
                            before = use_before(ph, v, "LT", k)
                            if before:
                                act.wait_ge(sh_full[before[0]], before[1])
                            nc.scalar.copy(Lsb[:], L[:]).then_inc(ls_done, 1)
                        side(k, s)
                        at = (k, s)
                        if ph.prev and at == (2, 6):
                            b = v - 1
                            act.wait_ge(x_dve.sem, x_dve.after(b, "lsub"))
                            nc.scalar.activation(lex[:], lsub[:], ACT.Exp).then_inc(x_act.sem, 1)
                        if ph.tail:
                            b = v - TAIL_LAG
                            if at == (0, 4):
                                act.wait_ge(t_dve.sem, t_dve.after(b, "xc"))
                                nc.scalar.activation(tsq[:], txc[:], ACT.Square).then_inc(t_act.sem, 1)
                            if at == (2, 3):
                                act.wait_ge(t_dve.sem, t_dve.after(b, "xc2"))
                                nc.scalar.activation(tsq[:], txc[:], ACT.Square).then_inc(t_act.sem, 1)
                            if at == (3, 6):
                                act.wait_ge(t_dve.sem, t_dve.after(b, "fsub"))
                                nc.scalar.activation(fex[:], fsub[:], ACT.Exp).then_inc(t_act.sem, 1)

            run(act, body)

        @block.vector
        def _(dve):
            nc.vector.memset(KT[96:98], -MSCALE).then_inc(k_rows, 1)
            dve.wait_ge(w_in, 16 * N_W)
            dve.wait_ge(c_done, 2)

            def body(ph, v):
                def full(name, k):
                    bank, c = use_count(ph, v, name, k)
                    dve.wait_ge(sh_full[bank], c + 1)
                    return SH[:, bank], sh_free[bank]

                def done(name, k):
                    bank, c = use_count(ph, v, name, k)
                    dve.wait_ge(sh_free[bank], c + 1)

                def reduce_max(b, n, j, pos):
                    dve.wait_ge(mx_full, (b * 4 + n) * J + pos + 1)
                    if pos == 0:
                        wait(dve, m2_done, (b * 4 + n - 1) * 2)
                    nc.vector.tensor_reduce(mx[:, n % 2, j:j + 1], MX[:, pos % 2, 0:P * (j % C + 1)], AX.X,
                                            ALU.max).then_inc(mx_free, 1)

                def layernorm_stats(b, src, two):
                    for c in range(C):
                        st = nc.vector.bn_stats(bst[:, c, :], src[:, c, :])
                    st.then_inc(g_dve.sem, 1)
                    dve.wait_ge(g_dve.sem, g_dve.after(b, "stats" + two))
                    held(dve)
                    for c in range(C):
                        st = nc.vector.bn_aggr(mv[:, c, :], bst[:, c, :])
                    st.then_inc(g_dve.sem, 1)
                    dve.wait_ge(g_dve.sem, g_dve.after(b, "aggr" + two))
                    nc.vector.tensor_scalar(ve[:], mv[:, :, 1], EPS_GNN, None, ALU.add).then_inc(g_dve.sem, 1)

                def normalise(b, src, two):
                    dve.wait_ge(g_pool.sem, g_pool.after(b, "rs" + two))
                    for c in range(C):
                        i = nc.vector.tensor_scalar(xn[:, c, :], src[:, c, :], mv[:, c, 0:1], rs[:, c:c + 1],
                                                    ALU.subtract, ALU.mult)
                    i.then_inc(g_dve.sem, 1)

                def aggregate(b, i):
                    src, free = full(f"msg{i}", 1)
                    m = src[:, 0:260].rearrange("p (c w) -> p c w", c=2)
                    nc.vector.tensor_scalar(dmax[:], m[:, :, H], 1.0, None, ALU.max).then_inc(g_dve.sem, 1)
                    dve.wait_ge(g_dve.sem, g_dve.after(b, f"deg{i}"))
                    nc.vector.reciprocal(drec[:], dmax[:]).then_inc(g_dve.sem, 1)
                    dve.wait_ge(g_dve.sem, g_dve.after(b, f"rec{i}"))
                    nc.vector.scalar_tensor_tensor(out=dgs[:], in0=m[:, :, H], scalar=0.0, in1=drec[:], op0=ALU.is_gt,
                                                   op1=ALU.mult).then_inc(g_dve.sem, 1)
                    dve.wait_ge(g_dve.sem, g_dve.after(b, f"gs{i}"))
                    c = 2 * i
                    nc.vector.scalar_tensor_tensor(out=agg[:, c, :], in0=m[:, 0, 0:H], scalar=dgs[:, 0:1], in1=upd[:, c, :],
                                                   op0=ALU.mult, op1=ALU.add).then_inc(g_dve.sem, 1)
                    nc.vector.scalar_tensor_tensor(out=agg[:, c + 1, :], in0=m[:, 1, 0:H], scalar=dgs[:, 1:2],
                                                   in1=upd[:, c + 1, :], op0=ALU.mult, op1=ALU.add).then_inc(free, 1)

                def prep(b, at):
                    if at == (0, 0):
                        dve.wait_ge(x_in, (b + 1) * 16)
                        layernorm_stats(b, xin, "")
                    if at == (0, 2):
                        normalise(b, xin, "")
                    if at == (0, 4):
                        dve.wait_ge(adj_in, (b + 1) * 16)
                        nc.vector.tensor_copy(adj_f[:], adj_i[:]).then_inc(g_dve.sem, 1)
                    if at in ((0, 5), (0, 6)):
                        i = at[1] - 5
                        src, free = full(f"hu{i}", 0)
                        dve.wait_ge(g_act.sem, g_act.after(b, f"h{i}"))
                        nc.vector.tensor_tensor(upd[:, 2 * i:2 * i + 2, :], src.rearrange("p (c w) -> p c w", c=2)[:, :, H:2 * H],
                                                gnnb_s[:].unsqueeze(1).to_broadcast([P, 2, H]), ALU.add).then_inc(free, 1)
                    if at == (1, 1):
                        aggregate(b, 0)
                    if at == (1, 3):
                        aggregate(b, 1)
                    if at == (1, 4):
                        done("msg0", 1)
                        done("msg1", 1)
                        wait(dve, x2_kept, 16 * b)
                        nc.vector.scalar_tensor_tensor(out=x2[:], in0=agg[:], scalar=0.0, in1=xin[:], op0=ALU.max,
                                                       op1=ALU.add).then_inc(g_dve.sem, 1)
                    if at == (1, 5):
                        dve.wait_ge(g_dve.sem, g_dve.after(b, "x2"))
                        layernorm_stats(b, x2, "2")
                    if at == (1, 7):
                        normalise(b, x2, "2")
                    if at == (3, 5):
                        done("sxT", 3)
                        for m in range(NH):
                            wait(dve, mask_in[m], b * 64)
                        nc.vector.tensor_scalar(nzT[:], sxT[:], 0.0, None, ALU.not_equal).then_inc(g_dve.sem, 1)

                def read(name, k):
                    if name == "q":
                        b, n = (v, k + 1) if k < 3 else (v + 1, 0)
                        src, free = full(name, k)
                        dve.wait_ge(qhi_done, b * 4 + n + 1)
                        nc.vector.tensor_tensor(qlo[:], src, qhi[:], ALU.subtract).then_inc(free, 1)
                    elif name == "kT":
                        src, free = full(name, k)
                        dve.wait_ge(khi_done, (v + 1) * 2 + 1)
                        nc.vector.tensor_tensor(klo[:], src, khi[:], ALU.subtract).then_inc(free, 1)
                        dve.wait_ge(free, use_count(ph, v, name, k)[1] + 1)
                        dve.sem_inc(khi_done, 1)
                    elif name == "LT":
                        b, n = head(v, k, 3)
                        src, free = full(name, k)
                        wait(dve, x_dve.sem, x_dve.after(b - 1, "lw2"))
                        nc.vector.reciprocal(rL[:, n], src.rearrange("p (c e r) -> p c e r", c=C, e=NE)[:, :, :, 0]).then_inc(free, 1)
                    elif name == "sxn":
                        b = v + 1
                        src, free = full(name, k)
                        nc.vector.tensor_copy(resid[:, :, b, :], src.rearrange("p (c n d) -> p c n d", c=C, n=NH)[:, :, b, :]).then_inc(free, 1)

                def mix(b, at):
                    if at != (2, 6):
                        return
                    z = nat[:].rearrange("p n c w -> p (n c) w")[:, :, P:NATW].rearrange("p g (f e) -> p g e f", f=NE)
                    r = rL[:].rearrange("p n c e -> p (n c) e")
                    bank, c = use_count(ph, v, "LT", 2)
                    dve.wait_ge(sh_free[bank], c + 1)
                    bank, c = use_count(ph, v, "nat1", 2)
                    dve.wait_ge(sh_free[bank], c + 1)
                    done("nat0", 2)

                    def step(name, ins):
                        ins.then_inc(x_dve.sem, 1)
                        dve.wait_ge(x_dve.sem, x_dve.after(b, name))
                    wait(dve, x_pool.sem, x_pool.after(b - 1, "prod3"))
                    step("zr", nc.vector.tensor_tensor(zr[:], z, r.unsqueeze(2).to_broadcast([P, G16, NE, NE]), ALU.mult))
                    step("lg", nc.vector.tensor_reduce(lg[:], zr[:], AX.X, ALU.add))
                    step("lgb", nc.vector.tensor_tensor(lgb[:].rearrange("p (n c) e -> p n c e", n=NH),
                                                        lg[:].rearrange("p (n c) e -> p n c e", n=NH),
                                                        gb_s[:].unsqueeze(2).to_broadcast([P, NH, C, NE]), ALU.add))
                    step("lmax", nc.vector.tensor_reduce(lmax[:], lgb[:], AX.X, ALU.max))
                    step("lsub", nc.vector.tensor_tensor(lsub[:], lgb[:], lmax[:].unsqueeze(2).to_broadcast([P, G16, NE]), ALU.subtract))
                    dve.wait_ge(x_act.sem, x_act.after(b, "lex"))
                    step("lsum", nc.vector.tensor_reduce(lsum[:], lex[:], AX.X, ALU.add))
                    step("lrec", nc.vector.reciprocal(lrec[:], lsum[:]))
                    step("lw", nc.vector.tensor_tensor(lw[:], lex[:], lrec[:].unsqueeze(2).to_broadcast([P, G16, NE]), ALU.mult))
                    step("lw2", nc.vector.tensor_tensor(lw2[:], lw[:], r, ALU.mult))

                def tail(b, at):
                    def step(name, ins, last=False):
                        ins.then_inc(t_dve.sem, 1)
                        dve.wait_ge(t_dve.sem, t_dve.after(b, name))

                    def slot(ring):
                        return ring[:, b % RING] if isinstance(b, int) else ring[:, bass.ds(b % RING, 1)].rearrange("p a f -> p (a f)")

                    def mean(two):
                        step("sum" + two, nc.vector.tensor_reduce(tsum[:], ty[:], AX.X, ALU.add))
                        step("mean" + two, nc.vector.tensor_scalar(tmean[:], tsum[:], 1.0 / D, None, ALU.mult))

                    def centre(two):
                        step("xc" + two, nc.vector.tensor_tensor(txc[:], ty[:], tmean[:].unsqueeze(2).to_broadcast([P, G16, D]),
                                                                 ALU.subtract))

                    def variance(two):
                        dve.wait_ge(t_act.sem, t_act.after(b, "sq" + two))
                        step("vs" + two, nc.vector.tensor_reduce(tvs[:], tsq[:], AX.X, ALU.add))
                        step("ve" + two, nc.vector.tensor_scalar(tve[:], tvs[:], 1.0 / D, EPS_FFN, ALU.mult, ALU.add))

                    def scaled(two):
                        dve.wait_ge(t_pool.sem, t_pool.after(b, "rs" + two))
                        step("xs" + two, nc.vector.tensor_tensor(txs[:], txc[:], trs[:].unsqueeze(2).to_broadcast([P, G16, D]),
                                                                 ALU.mult))

                    if at == (0, 1):
                        dve.wait_ge(mix_kept, (b + 1) * 16)
                        step("y", nc.vector.tensor_tensor(ty[:].rearrange("p g d -> p (g d)"), slot(mixring),
                                                          resid[:].rearrange("p c n d -> p (c n d)"), ALU.add))
                        mean("")
                    if at == (0, 3):
                        centre("")
                    if at == (0, 5):
                        variance("")
                    if at == (0, 7):
                        scaled("")
                    if at == (1, 5):
                        done("fxT", 1)
                        step("nzf", nc.vector.tensor_scalar(nzf[:], fxT[:], 0.0, None, ALU.not_equal))
                    if at == (2, 1):
                        src, free = full("h2", 2)
                        step("u", nc.vector.tensor_tensor(u2[:], src.rearrange("p (g d) -> p g d", d=D),
                                                          fc2b_s[:].unsqueeze(1).to_broadcast([P, G16, D]), ALU.add))
                        dve.sem_inc(free, 1)
                        step("w", nc.vector.scalar_tensor_tensor(out=w2[:], in0=fx[:], scalar=0.0, in1=u2[:], op0=ALU.not_equal,
                                                                 op1=ALU.mult))
                        step("y2", nc.vector.tensor_tensor(ty[:], w2[:], fx[:], ALU.add))
                    if at == (2, 2):
                        mean("2")
                    if at == (2, 3):
                        centre("2")
                    if at == (2, 4):
                        variance("2")
                    if at == (2, 7):
                        pass
                    if at == (2, 5):
                        scaled("2")
                    if at == (3, 6):
                        src, free = full("fg", 3)
                        l4 = src[:, 0:C * NH].rearrange("p (c n) -> p c n", c=C)
                        step("fmax", nc.vector.tensor_reduce(fmax[:], l4, AX.X, ALU.max))
                        step("fsub", nc.vector.tensor_tensor(fsub[:], l4, fmax[:].unsqueeze(2).to_broadcast([P, C, NH]), ALU.subtract))
                        dve.sem_inc(free, 1)
                        dve.wait_ge(t_act.sem, t_act.after(b, "fex"))
                        step("fsum", nc.vector.tensor_reduce(fsum[:], fex[:], AX.X, ALU.add))
                        step("frec", nc.vector.reciprocal(frec[:], fsum[:]))
                        step("fgs", nc.vector.tensor_tensor(fgs[:], fex[:], frec[:].unsqueeze(2).to_broadcast([P, C, NH]), ALU.mult))
                    if at == (3, 7):
                        dve.wait_ge(t_pool.sem, t_pool.after(b, "fmul"))
                        dve.wait_ge(x2_kept, (b + 1) * 16)
                        wait(dve, out_done, b * 16)
                        step("out", nc.vector.tensor_tensor(outb[:], slot(x2ring), fmul[:].rearrange("p g d -> p (g d)"), ALU.add))

                for k in range(4):
                    for s in range(SLOTS):
                        at = (k, s)
                        if ph.block(k, 1) and s == 0:
                            b, n = head(v, k, 1)
                            i = b * 4 + n
                            before = use_before(ph, v, "mT", k)
                            if before:
                                dve.wait_ge(sh_full[before[0]], before[1])
                            dve.wait_ge(mx_free, (i + 1) * J)
                            nc.vector.tensor_scalar(m2[:, 0:J], mx[:, n % 2, :], 1.0 / MSCALE, None, ALU.mult).then_inc(m2_done, 1)
                            dve.wait_ge(m2_done, i * 2 + 1)
                            nc.vector.scalar_tensor_tensor(out=m2[:, J:2 * J], in0=mx[:, n % 2, :], scalar=1.0 / MSCALE,
                                                           in1=m2[:, 0:J], op0=ALU.mult, op1=ALU.subtract).then_inc(m2_done, 1)
                        if ph.att and s == 1:
                            wait(dve, av_done, (v - 1) * 4 + k + 1)
                            if k == 0:
                                dve.wait_ge(sh_free[BANK["v", 3]], iteration_start(ph, v, BANK["v", 3]))
                            nc.vector.tensor_copy(V[:, k], vnew[:, :, D * k:D * k + D]).then_inc(v_copied, 1)
                        if ph.att:
                            reduce_max(v, k, *MAX_TILES[2 * s])
                            reduce_max(v, k, *MAX_TILES[2 * s + 1])
                        if ph.block(k, 3) and s == 2:
                            b, n = head(v, k, 3)
                            dve.wait_ge(av_done, b * 4 + n + 1)
                            dve.wait_ge(mask_in[n], (b + 1) * 64)
                            before = use_before(ph, v, "nat1", k)
                            if before:
                                dve.wait_ge(sh_full[before[0]], before[1])
                            nc.vector.tensor_tensor(Om[:], O[:], mrep[:, n, :], ALU.mult).then_inc(om_done, 1)
                        for name, uk, us in USES:
                            if (uk, us) == at and ph.has(name, k):
                                read(name, k)
                        if ph.prep:
                            prep(v + 1, at)
                        if ph.prev:
                            mix(v - 1, at)
                        if ph.tail:
                            tail(v - TAIL_LAG, at)

            run(dve, body)


def kernel(x, adj, L0_gnn_W_msg, L0_gnn_W_upd, L0_gnn_bias, L0_ffn_hl_w, L0_ffn_hl_b, L0_ffn_wq, L0_ffn_wk, L0_ffn_wv,
           L0_ffn_gate_w, L0_ffn_gate_b, L0_ffn_ln_g, L0_ffn_ln_b, L0_ffn_fc1_w, L0_ffn_fc1_b, L0_ffn_fc2_w, L0_ffn_fc2_b,
           L0_ffn_fnorm_g, L0_ffn_fnorm_b, L0_ffn_fgate_w):
    import concourse.bacc as bacc
    from concourse.bass_utils import run_bass_kernel_spmd

    def lay(a, *shape, perm=None):
        a = np.asarray(a)
        if perm is not None:
            a = a.transpose(perm)
        return np.ascontiguousarray(a.reshape(shape) if shape else a)

    arrays = {
        "x": lay(x),
        "adj": lay(adj),
        "w_mu": np.stack([np.asarray(L0_gnn_W_msg), np.asarray(L0_gnn_W_upd)]),
        "gnn_b": lay(L0_gnn_bias, 1, H),
        "hlwT": lay(L0_ffn_hl_w, H, H, perm=(2, 0, 1)),
        "hlb": lay(L0_ffn_hl_b, H, 1),
        "wq": lay(L0_ffn_wq, NH, D, NE * D, perm=(0, 3, 1, 2)),
        "wk": lay(L0_ffn_wk, perm=(0, 2, 1)),
        "wv": lay(L0_ffn_wv, perm=(0, 2, 1)),
        "gw": np.ascontiguousarray(np.asarray(L0_ffn_gate_w).reshape(NH, NE, NE, D).transpose(0, 2, 3, 1)),
        "gb": lay(L0_ffn_gate_b, 1, NH * NE),
        "ln_g": lay(L0_ffn_ln_g, 1, D),
        "ln_b": lay(L0_ffn_ln_b, 1, D),
        "fc1": lay(L0_ffn_fc1_w, perm=(1, 0)),
        "fc1_b": lay(L0_ffn_fc1_b, D, 1),
        "fc2": lay(L0_ffn_fc2_w, perm=(1, 0)),
        "fc2_b": lay(L0_ffn_fc2_b, 1, D),
        "fn_g": lay(L0_ffn_fnorm_g, 1, D),
        "fn_b": lay(L0_ffn_fnorm_b, 1, D),
        "fgT": lay(L0_ffn_fgate_w, perm=(1, 0)),
    }
    nc = bacc.Bacc("TRN2", target_bir_lowering=False, num_devices=1)
    args = [nc.dram_tensor(name, a.shape, mybir.dt.from_np(a.dtype), kind="ExternalInput").ap() for name, a in arrays.items()]
    out = nc.dram_tensor("out", (B, S, H), F32, kind="ExternalOutput").ap()
    build(nc, *args, out)
    r = run_bass_kernel_spmd(nc, [arrays], core_ids=[0])
    return r.results[0]["out"]
```

```python
from contextlib import ExitStack

import numpy as np
import concourse.bass as bass
from concourse import mybir

ALU = mybir.AluOpType
ACT = mybir.ActivationFunctionType
AX = mybir.AxisListType
F32 = mybir.dt.float32
F16 = mybir.dt.float16
BF16 = mybir.dt.bfloat16
I32 = mybir.dt.int32

B, S, H = 16, 512, 128
NH, NE = 4, 4
D = H // NH
P = 128
C = S // P
J = NE * C
EPS_GNN, EPS_FFN = 1e-5, 1e-8
SCALE = float(D) ** 0.5
MSCALE = 64.0
BIG = -1e30
NATW = P + NE * NE
FGW = 96
TAIL_LAG = 3
X2_RING, MIX_RING = 8, 4

SLOTS = J
MX_BANKS = 3
MAX_TILES = [(C * (pos // 4) + (0, 3, 1, 2)[pos % 4], pos) for pos in range(J)]
CHUNKS = [(0, e, 1) for e in range(4)] + [(1, e, 1) for e in range(4)] + [(2, 0, 2), (2, 2, 2), (3, 0, 4)]
CHUNK_SLOT = [0, 1, 2, 3, 5, 7, 8, 8, 13, 14, 15]
PT_OFF = [0, 2048, 3584, 4608]
PT_W = 5120
LAST_CHUNK = [3, 7, 9, 10]
AV_SLOT = [6, 11, 15, 16]
ADD_SLOT = [8, 15, 17]

USES = [
    ("q", 0, 1), ("mT", 0, 4), ("nat0", 0, 4), ("xnT", 0, 5), ("nat1", 0, 5), ("L", 0, 7), ("LT", 0, 9),
    ("hu0", 0, 9), ("hu1", 0, 13),
    ("mT", 1, 1), ("q", 1, 2), ("msg0", 1, 3), ("msg1", 1, 3), ("nat0", 1, 3), ("L", 1, 7), ("LT", 1, 9),
    ("nat1", 1, 10), ("fxT", 1, 10), ("fxT_b", 1, 10), ("h1T", 1, 14), ("h1T_b", 1, 15),
    ("h2", 2, 2), ("h2_b", 2, 2), ("q", 2, 3), ("mT", 2, 5), ("nat0", 2, 7), ("L", 2, 7), ("nat1", 2, 9),
    ("LT", 2, 10), ("xn2T", 2, 11),
    ("sxT", 3, 0), ("mT", 3, 2), ("q", 3, 4), ("nat1", 3, 4), ("kT", 3, 6), ("L", 3, 7), ("v", 3, 8), ("nat0", 3, 9),
    ("foT_b", 3, 9), ("foT", 3, 9), ("fg", 3, 12), ("sxn", 3, 12), ("LT", 3, 13), ("fg_b", 3, 14),
]
SPLIT_SLOT, V_SLOT, OM_SLOT = 0, 7, 0
VECTOR_AT = {
    "stats": (0, 0), "xn": (0, 2), "adj": (0, 7), "upd0": (0, 9), "upd1": (0, 13), "agg0": (1, 2), "agg1": (1, 4),
    "x2": (1, 7), "stats2": (1, 9), "xn2": (2, 1), "nz": (3, 13), "gate": (2, 11), "gate2": (2, 15), "y": (0, 5),
    "xc": (0, 6), "var": (0, 12), "xs": (1, 1), "nzf": (1, 11), "y2": (2, 2), "mean2": (2, 3), "xc2": (2, 3),
    "var2": (2, 4), "xs2": (2, 11), "head": (3, 12), "head2": (3, 12), "out": (3, 15),
}
SCALAR_AT = {
    "lex": (2, 15), "sq": (0, 9), "sq2": (2, 5), "fex": (3, 12),
}
POOL_AT = {
    "rs": (0, 0), "rs2": (1, 9), "mix0": (2, 15), "mix1": (3, 3), "mix2": (3, 6), "mix3": (3, 10), "trs": (0, 10),
    "g": (1, 3), "fx": (1, 6), "h1m": (1, 12), "trs2": (2, 1), "g2": (2, 10), "fo": (2, 12), "fmul": (3, 8),
}
BANK = {}
for _u, (_name, _k, _s) in enumerate(USES):
    BANK[_name, _k] = _u % 2


def mx_bank(n, pos):
    return (n * J + pos) % MX_BANKS


def mx_before(n, pos):
    g = n * J + pos
    if g >= MX_BANKS:
        return g - MX_BANKS
    return max(i for i in range(NH * J) if i % MX_BANKS == g) - NH * J


class Phase:

    def __init__(self, v0, count):
        self.v0, self.count = v0, count
        v = v0
        self.att = 0 <= v < B
        self.prep = v + 1 < B
        self.load = v + 2 < B
        self.prev = 1 <= v <= B
        self.tail = TAIL_LAG <= v < B + TAIL_LAG
        self.resid = v + 1 < NH
        self.pair = v == B + 1
        self.uses = [(n, k) for n, k, _ in USES if self.has(n, k)]

    def has(self, name, k):
        if name in ("xnT", "hu0", "hu1", "msg0", "msg1", "xn2T", "sxT", "kT", "v"):
            return self.prep
        if name == "sxn":
            return self.prep and self.resid
        if name in ("fxT", "h1T", "h2", "foT", "fg"):
            return self.tail
        if name in ("fxT_b", "h1T_b", "h2_b", "foT_b", "fg_b"):
            return self.pair
        return {"q": self.query(k), "mT": self.block(k, 1), "nat0": self.block(k, 3), "nat1": self.block(k, 3),
                "L": self.block(k, 3), "LT": self.block(k, 3)}[name]

    def query(self, k):
        return self.att if k < 3 else self.prep

    def block(self, k, lag):
        return self.att if k >= lag else self.prev


PHASES = [Phase(-1, 1), Phase(0, 1), Phase(1, 1), Phase(2, 1), Phase(3, B - 5), Phase(B - 2, 1), Phase(B - 1, 1), Phase(B, 1),
          Phase(B + 1, 1)]


def use_count(ph, v, name, k):
    bank = BANK[name, k]
    base = 0
    for q in PHASES:
        mine = [u for u in q.uses if BANK[u] == bank]
        if q is ph:
            at = base + mine.index((name, k))
            return bank, (at if isinstance(v, int) else (v - ph.v0) * len(mine) + at)
        base += q.count * len(mine)


def use_before(ph, v, name, k):
    if k > 0:
        if not ph.has(name, k - 1):
            return None
        bank, c = use_count(ph, v, name, k - 1)
        return bank, c + 1
    if ph is PHASES[0] or not PHASES[PHASES.index(ph) - 1].has(name, 3):
        return None
    return BANK[name, 3], iteration_start(ph, v, BANK[name, 3])


def iteration_start(ph, v, bank):
    base = 0
    for q in PHASES:
        mine = len([u for u in q.uses if BANK[u] == bank])
        if q is ph:
            return base if isinstance(v, int) else (v - ph.v0) * mine + base
        base += q.count * mine


class Steps:

    def __init__(self, sem, names, first=0):
        self.sem, self.names, self.first = sem, names, first

    def after(self, b, name):
        return (b - self.first) * len(self.names) + self.names.index(name) + 1


class Tail:

    def __init__(self, first, sem, tile):
        self.first = first

        def groups(name):
            return tile(f"{name}_{first}", NH * C * D).rearrange("p (g d) -> p g d", d=D)

        def small(name):
            return tile(f"{name}_{first}", NH * C)

        self.y, self.xc, self.sq, self.xs, self.g = groups("ty"), groups("txc"), groups("tsq"), groups("txs"), groups("tg")
        self.fx, self.u, self.w, self.fo, self.mul = groups("fx"), groups("u2"), groups("w2"), groups("fo"), groups("fmul")
        self.sum, self.mean, self.vs, self.ve, self.rs = small("tsum"), small("tmean"), small("tvs"), small("tve"), small("trs")
        self.fxT, self.nzf, self.h1r, self.h1m, self.foT, self.out = [
            tile(f"{name}_{first}", S) for name in ("fxT", "nzf", "h1r", "h1m", "foT", "outb")]
        self.fsub, self.fex, self.fgs = [small(name).rearrange("p (c n) -> p c n", n=NH) for name in ("fsub", "fex", "fgs")]
        self.fmax, self.fsum, self.frec = [tile(f"{name}_{first}", C) for name in ("fmax", "fsum", "frec")]
        self.dve = Steps(sem(f"tail_vector_{first}"), ("y", "sum", "mean", "xc", "vs", "ve", "xs", "nzf", "u", "w", "y2", "sum2",
                                                       "mean2", "xc2", "vs2", "ve2", "xs2", "fmax", "fsub", "fsum", "frec", "fgs",
                                                       "out"), first)
        self.act = Steps(sem(f"tail_scalar_{first}"), ("sq", "sq2", "fex"), first)
        self.pool = Steps(sem(f"tail_pool_{first}"), ("rs", "g", "fx", "h1m", "rs2", "g2", "fo", "fmul"), first)

    def use(self, name):
        return name + "_b" if self.first else name


def wait(eng, sem, value):
    if not isinstance(value, int) or value > 0:
        eng.wait_ge(sem, value)


def head(v, k, lag):
    return (v, k - lag) if k >= lag else (v - 1, k - lag + 4)


def columns(*parts):
    at, cols = 0, {}
    for name, w in parts:
        cols[name] = slice(at, at + w)
        at += w
    return cols, at


WP, WP_W = columns(("hlwT", H), ("hlb", 1), ("wq", NE * D), ("wk", D), ("wv", D), ("gate", NH * NE), ("fgate", NH))
WD, WD_W = columns(("fc1", D), ("fc2", D), ("fc1_b", 1))
WR, WR_W = columns(("gnn_b", H), ("gate_b", NH * NE), ("ln_g", D), ("ln_b", D), ("fc2_b", D), ("fn_g", D), ("fn_b", D))


def tails(ph, v, a, b):
    return ([(a, v - TAIL_LAG)] if ph.tail else []) + ([(b, v - TAIL_LAG + 1)] if ph.pair else [])


def build(nc, x, adj, w_mu, w_p, w_d, w_r, out):
    ctx = ExitStack()
    with ctx:
        def sb(name, shape, dt=F32):
            return ctx.enter_context(nc.sbuf_tensor(name, shape, dt))

        def sem(name):
            return ctx.enter_context(nc.semaphore(name))

        ident = sb("ident", [P, P])
        ident16 = sb("ident16", [P, P], F16)
        identb = sb("identb", [P, P], BF16)
        maskneg = sb("maskneg", [P, P], BF16)
        masknegT = sb("masknegT", [P, NE, P], BF16)
        blocks = sb("blocks", [P, NH])
        ones = sb("ones", [P, D])
        mhalf = sb("mhalf", [P, 16])
        w_mu_s = sb("w_mu_s", [P, 2, H])
        wp_s = sb("wp_s", [P, WP_W])
        wd_s = sb("wd_s", [P, WD_W])
        wr_s = sb("wr_s", [P, WR_W])
        hlwT_s, hlb_s, fc1b_s = wp_s[:, WP["hlwT"]], wp_s[:, WP["hlb"]], wd_s[:, WD["fc1_b"]]
        gnnb_s, lng_s, lnb_s = wr_s[:, WR["gnn_b"]], wr_s[:, WR["ln_g"]], wr_s[:, WR["ln_b"]]
        fc2b_s, fng_s, fnb_s = wr_s[:, WR["fc2_b"]], wr_s[:, WR["fn_g"]], wr_s[:, WR["fn_b"]]
        gb_s = wr_s[:, WR["gate_b"]].rearrange("p (n e) -> p n e", n=NH)
        wq_s = sb("wq_s", [P, NH, NE * D])
        wk_s = sb("wk_s", [P, H])
        wv_s = sb("wv_s", [P, H])
        fc1_s = sb("fc1_s", [P, H])
        fc2_s = sb("fc2_s", [P, H])
        nat_w = sb("nat_w", [P, NH, NATW])
        fgT_s = sb("fgT_s", [P, FGW])

        xin = sb("xin", [P, C, H])
        adj_i = sb("adj_i", [P, C, S], I32)
        adj_f = sb("adj_f", [P, C, S])
        bst = sb("bst", [P, C, 6])
        mv = sb("mv", [P, C, 2])
        ve = sb("ve", [P, C])
        rs = sb("rs", [P, C])
        xn = sb("xn", [P, C, H])
        xnT = sb("xnT", [P, S])
        hS = sb("hS", [P, C, 132])
        upd = sb("upd", [P, C, H])
        dmax = sb("dmax", [P, 2])
        drec = sb("drec", [P, 2])
        dgs = sb("dgs", [P, 2])
        agg = sb("agg", [P, C, H])
        x2 = sb("x2", [P, C, H])
        sxT = sb("sxT", [P, S])
        nzT = sb("nzT", [P, S], BF16)
        khi = sb("khi", [P, S], F16)
        klo = sb("klo", [P, S], F16)
        vnew = sb("vnew", [P, C, H])
        resid = sb("resid", [P, C, NH, D])
        x2ring = sb("x2ring", [P, X2_RING, C * H])
        mixring = sb("mixring", [P, MIX_RING, C * H])

        qhi = sb("qhi", [P, S], F16)
        qlo = sb("qlo", [P, S], F16)
        QT = sb("QT", [P, NH, NE, S], F16)
        KT = sb("KT", [98, NH, S], F16)
        V = sb("V", [P, NH, C, D])
        mx = sb("mx", [P, 2, J])
        m2 = sb("m2", [P, 2 * J], F16)
        mT = sb("mT", [2 * J, P], F16)
        PT = sb("PT", [P, 2, PT_W])
        psum = sb("psum", [P, NE, S - P])
        mrep = sb("mrep", [P, NH, S], BF16)
        Om = sb("Om", [P, S])
        Lsb = sb("Lsb", [P, S])
        nat = sb("nat", [P, NH, C, NATW])
        rL = sb("rL", [P, NH, C, NE])

        G16 = NH * C
        zr = sb("zr", [P, G16, NE, NE])
        lg = sb("lg", [P, G16, NE])
        lgb = sb("lgb", [P, G16, NE])
        lmax = sb("lmax", [P, G16])
        lsub = sb("lsub", [P, G16, NE])
        lex = sb("lex", [P, G16, NE])
        lsum = sb("lsum", [P, G16])
        lrec = sb("lrec", [P, G16])
        lw = sb("lw", [P, G16, NE])
        lw2 = sb("lw2", [P, G16, NE])
        prod = sb("prod", [P, 2, C, NE, D])
        half = sb("half", [P, 2, C, 2, D])
        mixed = sb("mixed", [P, C, NH, D])

        tail_a = Tail(0, sem, lambda name, width: sb(name, [P, width])[:])
        spare = PT[:].rearrange("p a w -> p (a w)")
        taken = [0]

        def from_spare(name, width):
            taken[0] += width
            return spare[:, taken[0] - width:taken[0]]

        tail_b = Tail(B - 1, sem, from_spare)

        MX = ctx.enter_context(nc.psum_tensor("MX", [P, MX_BANKS, 512], F32))
        ST = ctx.enter_context(nc.psum_tensor("ST", [P, 2, 512], F32))
        O = ctx.enter_context(nc.psum_tensor("O", [P, 512], F32))
        SH = ctx.enter_context(nc.psum_tensor("SH", [P, 2, 512], F32))

        q_dram = nc.dram_tensor("q_scratch", (2, D, NE, S), F16, kind="Internal").ap()
        nz_dram = nc.dram_tensor("nonzero_scratch", (P, S), BF16, kind="Internal").ap()

        w_in = sem("weights_loaded")
        placed = sem("weights_placed")
        q_out = sem("q_in_scratch")
        nz_out = sem("nonzero_in_scratch")
        c_done = sem("constants_built")
        k_rows = sem("key_rows_set")
        passed = sem("waits_passed")
        x_in = sem("x_loaded")
        adj_in = sem("adj_loaded")
        x2_kept = sem("x2_kept")
        mix_kept = sem("mixed_kept")
        out_done = sem("out_stored")
        q_in = [sem(f"q_loaded{n}") for n in range(NH)]
        k_in = [sem(f"k_loaded{n}") for n in range(NH)]
        m_in = [sem(f"max_loaded{n}") for n in range(NH)]
        mask_in = [sem(f"mask_loaded{n}") for n in range(NH)]
        sh_full = [sem(f"shared_full{i}") for i in range(2)]
        sh_free = [sem(f"shared_free{i}") for i in range(2)]
        mx_full = sem("max_scores_full")
        mx_free = sem("max_scores_reduced")
        st_full = sem("scores_full")
        exp_done = sem("exp_done")
        added = sem("probabilities_added")
        o_done = sem("outputs_done")
        adjf_free = sem("adj_multiplied")
        m2_done = sem("max_split")
        v_copied = sem("v_copied")
        om_done = sem("outputs_masked")
        qhi_done = sem("q_high")
        khi_done = sem("k_high")
        g_dve = Steps(sem("prep_vector"), ("stats", "aggr", "var", "xn", "adj", "deg0", "rec0", "gs0", "agg0", "deg1", "rec1",
                                           "gs1", "agg1", "x2", "stats2", "aggr2", "var2", "xn2", "nz"))
        g_act = Steps(sem("prep_scalar"), ("h0", "h1"))
        g_pool = Steps(sem("prep_pool"), ("rs", "rs2"))
        x_dve = Steps(sem("mix_vector"), ("zr", "lg", "lgb", "lmax", "lsub", "lsum", "lrec", "lw", "lw2"))
        x_act = Steps(sem("mix_scalar"), ("lex",))
        x_pool = Steps(sem("mix_pool"), tuple(f"{w}{n}" for n in range(NH) for w in ("prod", "half", "mixed")))

        block = ctx.enter_context(nc.Block())

        def held(eng):
            eng.sem_inc(passed, 1)

        def run(eng, body):
            for ph in PHASES:
                if ph.count == 1:
                    body(ph, ph.v0)
                else:
                    with eng.Fori(ph.v0, ph.v0 + ph.count) as v:
                        body(ph, v)

        @block.sync
        def _(sp):
            def ready(sem, value):
                if not isinstance(value, int) or value > 0:
                    sp.wait_ge(sem, value)
                    held(sp)

            def loads(b):
                if isinstance(b, int):
                    xb, ab = x[b], adj[b]
                else:
                    xb, ab = x[bass.ds(b, 1)].rearrange("a s f -> (a s) f"), adj[bass.ds(b, 1)].rearrange("a s f -> (a s) f")
                ready(g_dve.sem, g_dve.after(b - 1, "x2"))
                sp.dma_start(xin[:], xb.rearrange("(c p) f -> p c f", p=P)).then_inc(x_in, 16)
                ready(g_dve.sem, g_dve.after(b - 1, "adj"))
                sp.dma_start(adj_i[:], ab.rearrange("(c p) j -> p c j", p=P)).then_inc(adj_in, 16)

            loads(0)
            sp.dma_start(w_mu_s[:], w_mu.rearrange("t p f -> p t f")).then_inc(w_in, 16)
            sp.dma_start(wr_s[:], w_r.to_broadcast([P, WR_W])).then_inc(w_in, 16)
            sp.dma_start(wp_s[:], w_p).then_inc(w_in, 16)
            sp.dma_start(wd_s[:], w_d.unsqueeze(0).to_broadcast([NH, D, WD_W])).then_inc(w_in, 16)

            def body(ph, v):
                for k in range(4):
                    if k < 3 and ph.att:
                        load_keys(v, k + 1)
                    if ph.att:
                        ready(nz_out, (v + 1) * 16)
                        ready(om_done, (v - 1) * 4 + k + 1)
                        sp.dma_start(mrep[:, k, :], nz_dram[D * k:D * k + D].unsqueeze(0).to_broadcast([NE, D, S])).then_inc(mask_in[k], 16)
                    if ph.block(k, 1):
                        b, n = head(v, k, 1)
                        bank, c = use_count(ph, v, "mT", k)
                        ready(sh_free[bank], c + 1)
                        sp.dma_start(QT[96:98, n].rearrange("r e (c s) -> r (e c) s", s=P), mT[:]).then_inc(m_in[n], 16)
                    if ph.query(k):
                        b, n = (v, k + 1) if k < 3 else (v + 1, 0)
                        bank, c = use_count(ph, v, "q", k)
                        ready(sh_free[bank], c + 1)
                        ready(st_full, (b - 1) * 44 + (n + 1) * 11)
                        for r, part in enumerate((qhi, qlo)):
                            sp.dma_start(q_dram[r].rearrange("d e s -> e d s"), part[:]).then_inc(q_out, 16)
                        ready(q_out, (b * 4 + n + 1) * 32)
                        sp.dma_start(QT[:, n].rearrange("p e s -> p (e s)"),
                                     q_dram.rearrange("r d e s -> (r d) (e s)").unsqueeze(0).to_broadcast([2, 2 * D, NE * S])
                                     ).then_inc(q_in[n], 16)
                    if k == 1 and ph.prep:
                        ready(g_dve.sem, g_dve.after(v + 1, "x2"))
                        keep(x2ring, v + 1, x2[:].rearrange("p c f -> p (c f)"), x2_kept)
                        if ph.load:
                            loads(v + 2)
                    if k == 3 and ph.prep:
                        load_keys(v + 1, 0)
                        ready(g_dve.sem, g_dve.after(v + 1, "nz"))
                        for m in range(NH):
                            ready(mask_in[m], (v + 1) * 16)
                        sp.dma_start(nz_dram, nzT[:]).then_inc(nz_out, 16)
                    if k == 3 and ph.prev:
                        ready(x_pool.sem, x_pool.after(v - 1, "mixed3"))
                        keep(mixring, v - 1, mixed[:].rearrange("p c n d -> p (c n d)"), mix_kept)
                    if k == 3:
                        for t, b in tails(ph, v, tail_a, tail_b):
                            ready(t.dve.sem, t.dve.after(b, "out"))
                            ob = out[b] if isinstance(b, int) else out[bass.ds(b, 1)].rearrange("a s f -> (a s) f")
                            sp.dma_start(ob.rearrange("(c p) f -> p c f", p=P), t.out.rearrange("p (c f) -> p c f", c=C)
                                         ).then_inc(out_done, 16)

            def keep(ring, b, src, done):
                size = ring.shape[1]
                dst = ring[:, b % size] if isinstance(b, int) else ring[:, bass.ds(b % size, 1)].rearrange("p a f -> p (a f)")
                sp.dma_start(dst, src).then_inc(done, 16)

            def load_keys(b, n):
                ready(khi_done, (b + 1) * 2)
                ready(st_full, (b - 1) * 44 + (n + 1) * 11)
                r = slice(D * n, D * n + D)
                sp.dma_start(KT[0:D, n, :], khi[r, :]).then_inc(k_in[n], 16)
                sp.dma_start(KT[D:2 * D, n, :], khi[r, :]).then_inc(k_in[n], 16)
                sp.dma_start(KT[2 * D:3 * D, n, :], klo[r, :]).then_inc(k_in[n], 16)

            run(sp, body)
            sp.wait_ge(out_done, 16 * B)

        N_W = 4

        @block.gpsimd
        def _(pool):
            pool.memset(mhalf[:], -0.5)
            for t in (ident, ident16, identb, maskneg):
                pool.memset(t[:], 0.0)
            pool.memset(masknegT[:], 0.0)
            pool.memset(blocks[:], 1.0)
            pool.memset(nat_w[:, :, 0:P], 0.0)
            pool.memset(fgT_s[:], 0.0)
            pool.memset(ones[:], 1.0)
            pool.memset(hS[:, :, H:H + 1], 1.0)
            pool.memset(hS[:, :, H + 1:132], 0.0).then_inc(c_done, 1)
            pool.wait_ge(c_done, 1)
            for t in (ident, ident16, identb):
                pool.affine_select(out=t[:], in_=t[:], compare_op=ALU.not_equal, fill=1.0, base=0, pattern=[[-1, P]],
                                   channel_multiplier=1)
            for n in range(NH):
                pool.affine_select(out=nat_w[:, n, 0:P], in_=nat_w[:, n, 0:P], compare_op=ALU.not_equal, fill=1.0, base=0,
                                   pattern=[[-1, P]], channel_multiplier=1)
            pool.affine_select(out=masknegT[:], in_=masknegT[:], compare_op=ALU.is_ge, fill=BIG, base=0,
                               pattern=[[0, NE], [1, P]], channel_multiplier=-1)
            pool.affine_select(out=blocks[:], in_=blocks[:], compare_op=ALU.is_ge, fill=0.0, base=0,
                               pattern=[[-D, NH]], channel_multiplier=1)
            pool.affine_select(out=maskneg[:], in_=maskneg[:], compare_op=ALU.is_ge, fill=BIG, base=0, pattern=[[-1, P]],
                               channel_multiplier=1).then_inc(c_done, 1)
            pool.wait_ge(c_done, 2)
            pool.affine_select(out=blocks[:], in_=blocks[:], compare_op=ALU.is_ge, fill=0.0, base=D - 1,
                               pattern=[[D, NH]], channel_multiplier=-1).then_inc(c_done, 1)

            def power(steps, dst, src):
                pool.tensor_tensor(dst, src, mhalf[:, 0:src.shape[-1]], ALU.pow).then_inc(steps.sem, 1)

            def body(ph, v):
                for k in range(4):
                    for s in range(SLOTS):
                        at = (k, s)
                        for t, slot in enumerate(ADD_SLOT):
                            lag = 2 + slot // SLOTS
                            if slot % SLOTS == s and ph.block(k, lag):
                                add(ph, v, k, *head(v, k, lag), t + 1)
                        if ph.prep and at == POOL_AT["rs"]:
                            pool.wait_ge(g_dve.sem, g_dve.after(v + 1, "var"))
                            power(g_pool, rs[:], ve[:])
                        if ph.prep and at == POOL_AT["rs2"]:
                            pool.wait_ge(g_dve.sem, g_dve.after(v + 1, "var2"))
                            power(g_pool, rs[:], ve[:])
                        for n in range(NH):
                            if ph.prev and at == POOL_AT[f"mix{n}"]:
                                mix(v - 1, n)
                        for t, b in tails(ph, v, tail_a, tail_b):
                            tail(ph, v, t, b, at)

            def add(ph, v, k, b, n, t):
                i = b * 4 + n
                pool.wait_ge(exp_done, i * 11 + LAST_CHUNK[t] + 1)
                w = S - P * t
                new = PT[:, n % 2, PT_OFF[t]:PT_OFF[t] + NE * w].rearrange("p (e s) -> p e s", e=NE)
                if t == 1:
                    if ph.has("L", k):
                        bank, c = use_count(ph, v, "L", k)
                        pool.wait_ge(sh_full[bank], c + 1)
                    old = PT[:, n % 2, 0:NE * S].rearrange("p (e s) -> p e s", e=NE)[:, :, P:S]
                else:
                    pool.wait_ge(added, i * 3 + t - 1)
                    old = psum[:, :, P * (t - 1):S - P]
                pool.tensor_tensor(psum[:, :, P * (t - 1):S - P], old, new, ALU.add).then_inc(added, 1)

            def mix(b, n):
                if n == 0:
                    pool.wait_ge(x_dve.sem, x_dve.after(b, "lw2"))
                if n >= 2:
                    pool.wait_ge(x_pool.sem, x_pool.after(b, f"half{n - 2}"))
                else:
                    wait(pool, x_pool.sem, x_pool.after(b - 1, f"half{n + 2}"))
                w = lw2[:, n * C:n * C + C, :].unsqueeze(3).to_broadcast([P, C, NE, D])
                pool.tensor_tensor(prod[:, n % 2], nat[:, n, :, 0:P].rearrange("p c (e d) -> p c e d", d=D), w,
                                   ALU.mult).then_inc(x_pool.sem, 1)
                pool.wait_ge(x_pool.sem, x_pool.after(b, f"prod{n}"))
                pool.tensor_tensor(half[:, n % 2], prod[:, n % 2, :, 0:2, :], prod[:, n % 2, :, 2:4, :],
                                   ALU.add).then_inc(x_pool.sem, 1)
                pool.wait_ge(x_pool.sem, x_pool.after(b, f"half{n}"))
                if n == 0:
                    wait(pool, mix_kept, b * 16)
                pool.tensor_tensor(mixed[:, :, n, :], half[:, n % 2, :, 0, :], half[:, n % 2, :, 1, :],
                                   ALU.add).then_inc(x_pool.sem, 1)

            def tail(ph, v, t, b, at):
                gbc = lng_s.unsqueeze(1).to_broadcast([P, G16, D])
                bbc = lnb_s.unsqueeze(1).to_broadcast([P, G16, D])
                gbc2 = fng_s.unsqueeze(1).to_broadcast([P, G16, D])
                bbc2 = fnb_s.unsqueeze(1).to_broadcast([P, G16, D])
                if at == POOL_AT["trs"]:
                    pool.wait_ge(t.dve.sem, t.dve.after(b, "ve"))
                    power(t.pool, t.rs, t.ve)
                if at == POOL_AT["g"]:
                    pool.wait_ge(t.dve.sem, t.dve.after(b, "xs"))
                    pool.tensor_tensor(t.g, t.xs, gbc, ALU.mult).then_inc(t.pool.sem, 1)
                if at == POOL_AT["fx"]:
                    pool.wait_ge(t.pool.sem, t.pool.after(b, "g"))
                    pool.tensor_tensor(t.fx, t.g, bbc, ALU.add).then_inc(t.pool.sem, 1)
                if at == POOL_AT["h1m"]:
                    bank, c = use_count(ph, v, t.use("h1T"), 1)
                    pool.wait_ge(sh_free[bank], c + 1)
                    pool.wait_ge(t.dve.sem, t.dve.after(b, "nzf"))
                    pool.tensor_tensor(t.h1m, t.h1r, t.nzf, ALU.mult).then_inc(t.pool.sem, 1)
                if at == POOL_AT["trs2"]:
                    pool.wait_ge(t.dve.sem, t.dve.after(b, "ve2"))
                    power(t.pool, t.rs, t.ve)
                if at == POOL_AT["g2"]:
                    pool.wait_ge(t.dve.sem, t.dve.after(b, "xs2"))
                    pool.tensor_tensor(t.g, t.xs, gbc2, ALU.mult).then_inc(t.pool.sem, 1)
                if at == POOL_AT["fo"]:
                    pool.wait_ge(t.pool.sem, t.pool.after(b, "g2"))
                    pool.tensor_tensor(t.fo, t.g, bbc2, ALU.add).then_inc(t.pool.sem, 1)
                if at == POOL_AT["fmul"]:
                    pool.wait_ge(t.dve.sem, t.dve.after(b, "fgs"))
                    g = t.fgs.rearrange("p c n -> p (c n)").unsqueeze(2).to_broadcast([P, G16, D])
                    pool.tensor_tensor(t.mul, t.fo, g, ALU.mult).then_inc(t.pool.sem, 1)

            pool.wait_ge(w_in, 16 * N_W)
            run(pool, body)

        @block.tensor
        def _(pe):
            pe.wait_ge(c_done, 2)
            pe.wait_ge(k_rows, 1)
            pe.wait_ge(w_in, 16 * N_W)

            def body(ph, v):
                def shared(name, k):
                    bank, c = use_count(ph, v, name, k)
                    wait(pe, sh_free[bank], c)
                    return SH[:, bank], sh_full[bank]

                def done(name, k):
                    bank, c = use_count(ph, v, name, k)
                    pe.wait_ge(sh_free[bank], c + 1)

                def maxima(b, n, j, pos):
                    if pos == 0:
                        pe.wait_ge(q_in[n], (b + 1) * 16)
                        pe.wait_ge(k_in[n], (b + 1) * 16 * 3)
                    wait(pe, mx_free, b * 4 * J + mx_before(n, pos) + 1)
                    bank = MX[:, mx_bank(n, pos)]
                    e, c = j // C, j % C
                    nc.tensor.matmul(bank[:, 0:P * (c + 1)], QT[0:96, n, e, P * c:P * c + P], KT[0:96, n, 0:P * (c + 1)],
                                     start=True, stop=False)
                    nc.tensor.matmul(bank[:, P * c:P * c + P], identb[:], maskneg[:], start=False, stop=True).then_inc(mx_full, 1)

                def scores(b, n, c):
                    t, e0, ne = CHUNKS[c]
                    g = (b * 4 + n) * 11 + c
                    if c == 0:
                        pe.wait_ge(m_in[n], (b + 1) * 16)
                    wait(pe, exp_done, g - 1)
                    w = S - P * t
                    bank = ST[:, (11 * n + c) % 2, 0:ne * w].rearrange("p (e s) -> p e s", e=ne)
                    nc.tensor.matmul(bank, KT[:, n, P * t:P * t + P], QT[0:98, n, e0:e0 + ne, P * t:S],
                                     start=True, stop=False)
                    nc.tensor.matmul(bank[:, :, 0:P], identb[:], masknegT[:, 0:ne, :], start=False, stop=True).then_inc(st_full, 1)

                def values(b, n, t):
                    pe.wait_ge(exp_done, (b * 4 + n) * 11 + LAST_CHUNK[t] + 1)
                    if t == 0:
                        pe.wait_ge(v_copied, b * 4 + n + 1)
                        wait(pe, om_done, b * 4 + n)
                    w = S - P * t
                    for e in range(NE):
                        a = PT_OFF[t] + e * w
                        mm = nc.tensor.matmul(O[D * e:D * e + D, P * t:S], V[:, n, t, :], PT[:, n % 2, a:a + w],
                                              start=(t == 0), stop=(t == C - 1))
                    if t == C - 1:
                        mm.then_inc(o_done, 1)

                def transposes(dst, src, full):
                    for c in range(C):
                        mm = nc.tensor.transpose(dst[:, c * P:c * P + P], src[:, c, :], ident[:])
                    mm.then_inc(full, 1)

                def side(k, s):
                    for name, uk, us in USES:
                        if (uk, us) != (k, s) or not ph.has(name, k):
                            continue
                        shared_use(name, k)

                def shared_use(name, k):
                    if name == "mT":
                        b, n = head(v, k, 1)
                        pe.wait_ge(m2_done, (b * 4 + n + 1) * 2)
                        dst, full = shared(name, k)
                        nc.tensor.transpose(dst.bitcast(F16)[0:2 * J, 0:P], m2[:], ident16[:]).then_inc(full, 1)
                    elif name == "q":
                        n = (k + 1) % 4
                        if k == 3:
                            done("sxT", 3)
                        dst, full = shared(name, k)
                        nc.tensor.matmul(dst, wq_s[:, n, :], sxT[:], start=True, stop=True).then_inc(full, 1)
                    elif name in ("nat0", "nat1"):
                        b, n = head(v, k, 3)
                        if name == "nat0":
                            pe.wait_ge(om_done, b * 4 + n + 1)
                        dst, full = shared(name, k)
                        for i in range(2):
                            c = 2 * int(name[3]) + i
                            mm = nc.tensor.matmul(dst[:, i * NATW:i * NATW + NATW], Om[:, c * P:c * P + P], nat_w[:, n, :],
                                                  start=True, stop=True)
                        mm.then_inc(full, 1)
                    elif name == "L":
                        b, n = head(v, k, 3)
                        dst, full = shared(name, k)
                        for e in range(NE):
                            nc.tensor.matmul(dst[D * e:D * e + D, 0:P], ones[:], PT[:, n % 2, e * S:e * S + P], start=True, stop=True)
                        pe.wait_ge(added, (b * 4 + n + 1) * 3)
                        for e in range(NE):
                            mm = nc.tensor.matmul(dst[D * e:D * e + D, P:S], ones[:], psum[:, e, :], start=True, stop=True)
                        mm.then_inc(full, 1)
                    elif name == "LT":
                        b, n = head(v, k, 3)
                        done("L", k)
                        dst, full = shared(name, k)
                        transposes(dst, Lsb[:].rearrange("p (c s) -> p c s", c=C), full)
                    elif name == "xnT":
                        pe.wait_ge(g_dve.sem, g_dve.after(v + 1, "xn"))
                        dst, full = shared(name, k)
                        transposes(dst, xn, full)
                    elif name in ("hu0", "hu1"):
                        done("xnT", 0)
                        dst, full = shared(name, k)
                        for i in range(2):
                            c = 2 * int(name[2]) + i
                            mm = nc.tensor.matmul(dst[:, i * 256:i * 256 + 256], xnT[:, c * P:c * P + P],
                                                  w_mu_s[:].rearrange("p t f -> p (t f)"),
                                                  start=True, stop=True)
                        mm.then_inc(full, 1)
                    elif name in ("msg0", "msg1"):
                        if name == "msg0":
                            pe.wait_ge(g_act.sem, g_act.after(v + 1, "h1"))
                            pe.wait_ge(g_dve.sem, g_dve.after(v + 1, "adj"))
                        dst, full = shared(name, k)
                        for i in range(2):
                            jc = 2 * int(name[3]) + i
                            for ic in range(C):
                                mm = nc.tensor.matmul(dst[:, i * 130:i * 130 + 130], adj_f[:, ic, jc * P:jc * P + P],
                                                      hS[:, ic, 0:130], start=(ic == 0), stop=(ic == C - 1))
                        mm.then_inc(full, 1)
                    elif name == "xn2T":
                        pe.wait_ge(g_dve.sem, g_dve.after(v + 1, "xn2"))
                        dst, full = shared(name, k)
                        transposes(dst, xn, full)
                    elif name == "sxT":
                        if ph is PHASES[0]:
                            pe.wait_ge(placed, 1)
                        done("xn2T", 2)
                        dst, full = shared(name, k)
                        nc.tensor.matmul(dst, hlwT_s, xnT[:], start=True, stop=True).then_inc(full, 1)
                    elif name == "kT":
                        done("sxT", 3)
                        dst, full = shared(name, k)
                        nc.tensor.matmul(dst, wk_s[:], sxT[:], start=True, stop=True).then_inc(full, 1)
                    elif name == "v":
                        dst, full = shared(name, k)
                        for c in range(C):
                            mm = nc.tensor.matmul(dst[:, c * P:c * P + P], sxT[:, c * P:c * P + P], wv_s[:],
                                                  start=True, stop=True)
                        mm.then_inc(full, 1)
                    elif name == "sxn":
                        dst, full = shared(name, k)
                        transposes(dst, sxT[:].rearrange("p (c s) -> p c s", c=C), full)
                    else:
                        t, b = tails(ph, v, tail_a, tail_b)[name.endswith("_b")]
                        tail_use(t, b, name.removesuffix("_b"), k)

                def tail_use(t, b, name, k):
                    if name == "fxT":
                        pe.wait_ge(t.pool.sem, t.pool.after(b, "fx"))
                        dst, full = shared(t.use(name), k)
                        transposes(dst, t.fx.rearrange("p (c n) d -> p c (n d)", c=C), full)
                    elif name == "h1T":
                        done(t.use("fxT"), 1)
                        dst, full = shared(t.use(name), k)
                        nc.tensor.matmul(dst, fc1_s[:], t.fxT, start=True, stop=True).then_inc(full, 1)
                    elif name == "h2":
                        pe.wait_ge(t.pool.sem, t.pool.after(b, "h1m"))
                        dst, full = shared(t.use(name), k)
                        for c in range(C):
                            mm = nc.tensor.matmul(dst[:, c * P:c * P + P], t.h1m[:, c * P:c * P + P], fc2_s[:],
                                                  start=True, stop=True)
                        mm.then_inc(full, 1)
                    elif name == "foT":
                        pe.wait_ge(t.pool.sem, t.pool.after(b, "fo"))
                        dst, full = shared(t.use(name), k)
                        transposes(dst, t.fo.rearrange("p (c n) d -> p c (n d)", c=C), full)
                    elif name == "fg":
                        done(t.use("foT"), 3)
                        dst, full = shared(t.use(name), k)
                        for c in range(C):
                            mm = nc.tensor.matmul(dst[:, c * FGW:c * FGW + FGW], t.foT[:, c * P:c * P + P], fgT_s[:],
                                                  start=True, stop=True)
                        mm.then_inc(full, 1)

                for k in range(4):
                    for s in range(SLOTS):
                        if ph.block(k, 2):
                            b, n = head(v, k, 2)
                            for c in range(11):
                                if CHUNK_SLOT[c] == s:
                                    scores(b, n, c)
                        if ph.att:
                            maxima(v, k, *MAX_TILES[s])
                        for t, at in enumerate(AV_SLOT):
                            lag = 2 + at // SLOTS
                            if at % SLOTS == s and ph.block(k, lag):
                                values(*head(v, k, lag), t)
                        side(k, s)

            run(pe, body)

        @block.scalar
        def _(act):
            act.wait_ge(w_in, 16 * N_W)

            def body(ph, v):
                def full(name, k):
                    bank, c = use_count(ph, v, name, k)
                    act.wait_ge(sh_full[bank], c + 1)
                    return SH[:, bank], sh_free[bank]

                def exps(b, n, c):
                    t, e0, ne = CHUNKS[c]
                    g = (b * 4 + n) * 11 + c
                    if c == 0:
                        wait(act, o_done, b * 4 + n - 1)
                    act.wait_ge(st_full, g + 1)
                    w = S - P * t
                    a = PT_OFF[t] + e0 * w
                    nc.scalar.activation(PT[:, n % 2, a:a + ne * w], ST[:, (11 * n + c) % 2, 0:ne * w], ACT.Exp,
                                         scale=SCALE).then_inc(exp_done, 1)

                def side(k, s):
                    for name, uk, us in USES:
                        if (uk, us) != (k, s) or not ph.has(name, k):
                            continue
                        read(name, k)

                def read(name, k):
                    if name == "mT":
                        b, n = head(v, k, 1)
                        src, free = full(name, k)
                        for m in range(NH):
                            if m == (n - 1) % 4:
                                wait(act, m_in[m], (b + 1) * 16 if n else b * 16)
                        nc.scalar.copy(mT[:], src.bitcast(F16)[0:2 * J, 0:P]).then_inc(free, 1)
                    elif name == "q":
                        b, n = (v, k + 1) if k < 3 else (v + 1, 0)
                        src, _ = full(name, k)
                        m = (n - 1) % 4
                        wait(act, q_in[m], ((b + 1) if n else b) * 16)
                        nc.scalar.copy(qhi[:], src).then_inc(qhi_done, 1)
                    elif name == "L":
                        src, free = full(name, k)
                        before = use_before(ph, v, "LT", k)
                        if before:
                            act.wait_ge(sh_full[before[0]], before[1])
                        nc.scalar.copy(Lsb[:], src).then_inc(free, 1)
                    elif name in ("nat0", "nat1"):
                        b, n = head(v, k, 3)
                        i = 2 * int(name[3])
                        src, free = full(name, k)
                        wait(act, x_pool.sem, x_pool.after(b - 1, f"prod{n}"))
                        nc.scalar.copy(nat[:, n, i:i + 2, :], src[:, 0:2 * NATW].rearrange("p (c w) -> p c w", c=2)).then_inc(free, 1)
                    elif name in ("xnT", "xn2T"):
                        src, free = full(name, k)
                        nc.scalar.copy(xnT[:], src).then_inc(free, 1)
                    elif name in ("hu0", "hu1"):
                        i = 2 * int(name[2])
                        src, _ = full(name, k)
                        nc.scalar.copy(hS[:, i:i + 2, 0:H], src.rearrange("p (c w) -> p c w", c=2)[:, :, 0:H]).then_inc(g_act.sem, 1)
                    elif name == "sxT":
                        src, free = full(name, k)
                        nc.scalar.activation(sxT[:], src, ACT.Identity, bias=hlb_s).then_inc(free, 1)
                    elif name == "kT":
                        src, _ = full(name, k)
                        wait(act, k_in[3], (v + 1) * 48)
                        nc.scalar.copy(khi[:], src).then_inc(khi_done, 1)
                    elif name == "v":
                        src, free = full(name, k)
                        wait(act, v_copied, 4 * (v + 1))
                        nc.scalar.copy(vnew[:].rearrange("p c f -> p (c f)"), src).then_inc(free, 1)
                    elif name in ("fxT", "h1T", "foT", "fxT_b", "h1T_b", "foT_b"):
                        t, b = tails(ph, v, tail_a, tail_b)[name.endswith("_b")]
                        src, free = full(name, k)
                        if name == t.use("fxT"):
                            nc.scalar.copy(t.fxT, src).then_inc(free, 1)
                        elif name == t.use("h1T"):
                            nc.scalar.activation(t.h1r, src, ACT.Relu, bias=fc1b_s).then_inc(free, 1)
                        else:
                            nc.scalar.copy(t.foT, src).then_inc(free, 1)

                for k in range(4):
                    for s in range(SLOTS):
                        if ph.block(k, 2):
                            b, n = head(v, k, 2)
                            for c in range(11):
                                if CHUNK_SLOT[c] == s:
                                    exps(b, n, c)
                        side(k, s)
                        at = (k, s)
                        if ph.prev and at == SCALAR_AT["lex"]:
                            b = v - 1
                            act.wait_ge(x_dve.sem, x_dve.after(b, "lsub"))
                            nc.scalar.activation(lex[:], lsub[:], ACT.Exp).then_inc(x_act.sem, 1)
                        for t, b in tails(ph, v, tail_a, tail_b):
                            if at == SCALAR_AT["sq"]:
                                act.wait_ge(t.dve.sem, t.dve.after(b, "xc"))
                                nc.scalar.activation(t.sq, t.xc, ACT.Square).then_inc(t.act.sem, 1)
                            if at == SCALAR_AT["sq2"]:
                                act.wait_ge(t.dve.sem, t.dve.after(b, "xc2"))
                                nc.scalar.activation(t.sq, t.xc, ACT.Square).then_inc(t.act.sem, 1)
                            if at == SCALAR_AT["fex"]:
                                act.wait_ge(t.dve.sem, t.dve.after(b, "fsub"))
                                nc.scalar.activation(t.fex, t.fsub, ACT.Exp).then_inc(t.act.sem, 1)

            run(act, body)

        @block.vector
        def _(dve):
            nc.vector.memset(KT[96:98], -MSCALE).then_inc(k_rows, 1)

            def place():
                dve.wait_ge(w_in, 16 * N_W)
                dve.wait_ge(c_done, 3)
                b4 = blocks[:].unsqueeze(2).to_broadcast([P, NH, D])
                for dst, src in ((wk_s, wp_s[:, WP["wk"]]), (wv_s, wp_s[:, WP["wv"]]), (fc1_s, wd_s[:, WD["fc1"]]),
                                 (fc2_s, wd_s[:, WD["fc2"]])):
                    nc.vector.tensor_tensor(dst[:].rearrange("p (n o) -> p n o", n=NH), src.unsqueeze(1).to_broadcast([P, NH, D]), b4,
                                            ALU.mult)
                nc.vector.tensor_tensor(wq_s[:], wp_s[:, WP["wq"]].unsqueeze(1).to_broadcast([P, NH, NE * D]),
                                        blocks[:].unsqueeze(2).to_broadcast([P, NH, NE * D]), ALU.mult)
                nc.vector.tensor_copy(fgT_s[:, 0:NH], wp_s[:, WP["fgate"]])
                gate = wp_s[:, WP["gate"]].rearrange("p (n e) -> p n e", n=NH)
                for n in range(NH):
                    i = nc.vector.tensor_tensor(nat_w[:, n, P:NATW].rearrange("p (f e) -> p f e", f=NE),
                                                gate[:, n].unsqueeze(1).to_broadcast([P, NE, NE]),
                                                blocks[:].unsqueeze(2).to_broadcast([P, NE, NE]), ALU.mult)
                i.then_inc(placed, 1)

            def body(ph, v):
                def full(name, k):
                    bank, c = use_count(ph, v, name, k)
                    dve.wait_ge(sh_full[bank], c + 1)
                    return SH[:, bank], sh_free[bank]

                def done(name, k):
                    bank, c = use_count(ph, v, name, k)
                    dve.wait_ge(sh_free[bank], c + 1)

                def reduce_max(b, n, j, pos):
                    dve.wait_ge(mx_full, (b * 4 + n) * J + pos + 1)
                    if pos == 0:
                        wait(dve, m2_done, (b * 4 + n - 1) * 2)
                    nc.vector.tensor_reduce(mx[:, n % 2, j:j + 1], MX[:, mx_bank(n, pos), 0:P * (j % C + 1)], AX.X,
                                            ALU.max).then_inc(mx_free, 1)

                def layernorm_stats(b, src, two):
                    for c in range(C):
                        st = nc.vector.bn_stats(bst[:, c, :], src[:, c, :])
                    st.then_inc(g_dve.sem, 1)
                    dve.wait_ge(g_dve.sem, g_dve.after(b, "stats" + two))
                    held(dve)
                    for c in range(C):
                        st = nc.vector.bn_aggr(mv[:, c, :], bst[:, c, :])
                    st.then_inc(g_dve.sem, 1)
                    dve.wait_ge(g_dve.sem, g_dve.after(b, "aggr" + two))
                    nc.vector.tensor_scalar(ve[:], mv[:, :, 1], EPS_GNN, None, ALU.add).then_inc(g_dve.sem, 1)

                def normalise(b, src, two):
                    dve.wait_ge(g_pool.sem, g_pool.after(b, "rs" + two))
                    for c in range(C):
                        i = nc.vector.tensor_scalar(xn[:, c, :], src[:, c, :], mv[:, c, 0:1], rs[:, c:c + 1],
                                                    ALU.subtract, ALU.mult)
                    i.then_inc(g_dve.sem, 1)

                def aggregate(b, i):
                    src, free = full(f"msg{i}", 1)
                    m = src[:, 0:260].rearrange("p (c w) -> p c w", c=2)
                    nc.vector.tensor_scalar(dmax[:], m[:, :, H], 1.0, None, ALU.max).then_inc(g_dve.sem, 1)
                    dve.wait_ge(g_dve.sem, g_dve.after(b, f"deg{i}"))
                    nc.vector.reciprocal(drec[:], dmax[:]).then_inc(g_dve.sem, 1)
                    dve.wait_ge(g_dve.sem, g_dve.after(b, f"rec{i}"))
                    nc.vector.scalar_tensor_tensor(out=dgs[:], in0=m[:, :, H], scalar=0.0, in1=drec[:], op0=ALU.is_gt,
                                                   op1=ALU.mult).then_inc(g_dve.sem, 1)
                    dve.wait_ge(g_dve.sem, g_dve.after(b, f"gs{i}"))
                    c = 2 * i
                    nc.vector.scalar_tensor_tensor(out=agg[:, c, :], in0=m[:, 0, 0:H], scalar=dgs[:, 0:1], in1=upd[:, c, :],
                                                   op0=ALU.mult, op1=ALU.add).then_inc(g_dve.sem, 1)
                    nc.vector.scalar_tensor_tensor(out=agg[:, c + 1, :], in0=m[:, 1, 0:H], scalar=dgs[:, 1:2],
                                                   in1=upd[:, c + 1, :], op0=ALU.mult, op1=ALU.add).then_inc(free, 1)

                def prep(b, at):
                    if at == VECTOR_AT["stats"]:
                        dve.wait_ge(x_in, (b + 1) * 16)
                        layernorm_stats(b, xin, "")
                    if at == VECTOR_AT["xn"]:
                        normalise(b, xin, "")
                    if at == VECTOR_AT["adj"]:
                        dve.wait_ge(adj_in, (b + 1) * 16)
                        nc.vector.tensor_copy(adj_f[:], adj_i[:]).then_inc(g_dve.sem, 1)
                    for i in range(2):
                        if at != VECTOR_AT[f"upd{i}"]:
                            continue
                        src, free = full(f"hu{i}", 0)
                        dve.wait_ge(g_act.sem, g_act.after(b, f"h{i}"))
                        nc.vector.tensor_tensor(upd[:, 2 * i:2 * i + 2, :], src.rearrange("p (c w) -> p c w", c=2)[:, :, H:2 * H],
                                                gnnb_s.unsqueeze(1).to_broadcast([P, 2, H]), ALU.add).then_inc(free, 1)
                    if at == VECTOR_AT["agg0"]:
                        aggregate(b, 0)
                    if at == VECTOR_AT["agg1"]:
                        aggregate(b, 1)
                    if at == VECTOR_AT["x2"]:
                        done("msg0", 1)
                        done("msg1", 1)
                        wait(dve, x2_kept, 16 * b)
                        nc.vector.scalar_tensor_tensor(out=x2[:], in0=agg[:], scalar=0.0, in1=xin[:], op0=ALU.max,
                                                       op1=ALU.add).then_inc(g_dve.sem, 1)
                    if at == VECTOR_AT["stats2"]:
                        dve.wait_ge(g_dve.sem, g_dve.after(b, "x2"))
                        layernorm_stats(b, x2, "2")
                    if at == VECTOR_AT["xn2"]:
                        normalise(b, x2, "2")
                    if at == VECTOR_AT["nz"]:
                        done("sxT", 3)
                        wait(dve, nz_out, b * 16)
                        nc.vector.tensor_scalar(nzT[:], sxT[:], 0.0, None, ALU.not_equal).then_inc(g_dve.sem, 1)

                def read(name, k):
                    if name == "q":
                        b, n = (v, k + 1) if k < 3 else (v + 1, 0)
                        src, free = full(name, k)
                        dve.wait_ge(qhi_done, b * 4 + n + 1)
                        nc.vector.tensor_tensor(qlo[:], src, qhi[:], ALU.subtract).then_inc(free, 1)
                    elif name == "kT":
                        src, free = full(name, k)
                        dve.wait_ge(khi_done, (v + 1) * 2 + 1)
                        nc.vector.tensor_tensor(klo[:], src, khi[:], ALU.subtract).then_inc(free, 1)
                        dve.wait_ge(free, use_count(ph, v, name, k)[1] + 1)
                        dve.sem_inc(khi_done, 1)
                    elif name == "LT":
                        b, n = head(v, k, 3)
                        src, free = full(name, k)
                        wait(dve, x_dve.sem, x_dve.after(b - 1, "lw2"))
                        nc.vector.reciprocal(rL[:, n], src.rearrange("p (c e r) -> p c e r", c=C, e=NE)[:, :, :, 0]).then_inc(free, 1)
                    elif name == "sxn":
                        b = v + 1
                        src, free = full(name, k)
                        nc.vector.tensor_copy(resid[:, :, b, :], src.rearrange("p (c n d) -> p c n d", c=C, n=NH)[:, :, b, :]).then_inc(free, 1)

                def mix(b, at):
                    z = nat[:].rearrange("p n c w -> p (n c) w")[:, :, P:NATW].rearrange("p g (f e) -> p g e f", f=NE)
                    r = rL[:].rearrange("p n c e -> p (n c) e")

                    def step(name, ins):
                        ins.then_inc(x_dve.sem, 1)
                        dve.wait_ge(x_dve.sem, x_dve.after(b, name))

                    if at == VECTOR_AT["gate"]:
                        for name in ("LT", "nat1"):
                            bank, c = use_count(ph, v, name, 2)
                            dve.wait_ge(sh_free[bank], c + 1)
                        wait(dve, x_pool.sem, x_pool.after(b - 1, "prod3"))
                        step("zr", nc.vector.tensor_tensor(zr[:], z, r.unsqueeze(2).to_broadcast([P, G16, NE, NE]), ALU.mult))
                        step("lg", nc.vector.tensor_reduce(lg[:], zr[:], AX.X, ALU.add))
                        step("lgb", nc.vector.tensor_tensor(lgb[:].rearrange("p (n c) e -> p n c e", n=NH),
                                                            lg[:].rearrange("p (n c) e -> p n c e", n=NH),
                                                            gb_s.unsqueeze(2).to_broadcast([P, NH, C, NE]), ALU.add))
                        step("lmax", nc.vector.tensor_reduce(lmax[:], lgb[:], AX.X, ALU.max))
                        nc.vector.tensor_tensor(lsub[:], lgb[:], lmax[:].unsqueeze(2).to_broadcast([P, G16, NE]),
                                                ALU.subtract).then_inc(x_dve.sem, 1)
                    if at == VECTOR_AT["gate2"]:
                        dve.wait_ge(x_act.sem, x_act.after(b, "lex"))
                        step("lsum", nc.vector.tensor_reduce(lsum[:], lex[:], AX.X, ALU.add))
                        step("lrec", nc.vector.reciprocal(lrec[:], lsum[:]))
                        step("lw", nc.vector.tensor_tensor(lw[:], lex[:], lrec[:].unsqueeze(2).to_broadcast([P, G16, NE]), ALU.mult))
                        step("lw2", nc.vector.tensor_tensor(lw2[:], lw[:], r, ALU.mult))

                def tail(t, b, at):
                    def step(name, ins):
                        ins.then_inc(t.dve.sem, 1)
                        dve.wait_ge(t.dve.sem, t.dve.after(b, name))

                    def slot(ring):
                        size = ring.shape[1]
                        return ring[:, b % size] if isinstance(b, int) else ring[:, bass.ds(b % size, 1)].rearrange("p a f -> p (a f)")

                    def mean(two):
                        step("sum" + two, nc.vector.tensor_reduce(t.sum, t.y, AX.X, ALU.add))
                        step("mean" + two, nc.vector.tensor_scalar(t.mean, t.sum, 1.0 / D, None, ALU.mult))

                    def centre(two):
                        step("xc" + two, nc.vector.tensor_tensor(t.xc, t.y, t.mean.unsqueeze(2).to_broadcast([P, G16, D]),
                                                                 ALU.subtract))

                    def variance(two):
                        dve.wait_ge(t.act.sem, t.act.after(b, "sq" + two))
                        step("vs" + two, nc.vector.tensor_reduce(t.vs, t.sq, AX.X, ALU.add))
                        step("ve" + two, nc.vector.tensor_scalar(t.ve, t.vs, 1.0 / D, EPS_FFN, ALU.mult, ALU.add))

                    def scaled(two):
                        dve.wait_ge(t.pool.sem, t.pool.after(b, "rs" + two))
                        step("xs" + two, nc.vector.tensor_tensor(t.xs, t.xc, t.rs.unsqueeze(2).to_broadcast([P, G16, D]),
                                                                 ALU.mult))

                    if at == VECTOR_AT["y"]:
                        dve.wait_ge(mix_kept, (b + 1) * 16)
                        step("y", nc.vector.tensor_tensor(t.y.rearrange("p g d -> p (g d)"), slot(mixring),
                                                          resid[:].rearrange("p c n d -> p (c n d)"), ALU.add))
                        mean("")
                    if at == VECTOR_AT["xc"]:
                        centre("")
                    if at == VECTOR_AT["var"]:
                        variance("")
                    if at == VECTOR_AT["xs"]:
                        scaled("")
                    if at == VECTOR_AT["nzf"]:
                        done(t.use("fxT"), 1)
                        step("nzf", nc.vector.tensor_scalar(t.nzf, t.fxT, 0.0, None, ALU.not_equal))
                    if at == VECTOR_AT["y2"]:
                        src, free = full(t.use("h2"), 2)
                        step("u", nc.vector.tensor_tensor(t.u, src.rearrange("p (g d) -> p g d", d=D),
                                                          fc2b_s.unsqueeze(1).to_broadcast([P, G16, D]), ALU.add))
                        dve.sem_inc(free, 1)
                        step("w", nc.vector.scalar_tensor_tensor(out=t.w, in0=t.fx, scalar=0.0, in1=t.u, op0=ALU.not_equal,
                                                                 op1=ALU.mult))
                        step("y2", nc.vector.tensor_tensor(t.y, t.w, t.fx, ALU.add))
                    if at == VECTOR_AT["mean2"]:
                        mean("2")
                    if at == VECTOR_AT["xc2"]:
                        centre("2")
                    if at == VECTOR_AT["var2"]:
                        variance("2")
                    if at == VECTOR_AT["xs2"]:
                        scaled("2")
                    if at == VECTOR_AT["head"]:
                        src, free = full(t.use("fg"), 3)
                        l4 = src[:, 0:C * FGW].rearrange("p (c n) -> p c n", c=C)[:, :, 0:NH]
                        step("fmax", nc.vector.tensor_reduce(t.fmax, l4, AX.X, ALU.max))
                        step("fsub", nc.vector.tensor_tensor(t.fsub, l4, t.fmax.unsqueeze(2).to_broadcast([P, C, NH]), ALU.subtract))
                        dve.sem_inc(free, 1)
                    if at == VECTOR_AT["head2"]:
                        dve.wait_ge(t.act.sem, t.act.after(b, "fex"))
                        step("fsum", nc.vector.tensor_reduce(t.fsum, t.fex, AX.X, ALU.add))
                        step("frec", nc.vector.reciprocal(t.frec, t.fsum))
                        step("fgs", nc.vector.tensor_tensor(t.fgs, t.fex, t.frec.unsqueeze(2).to_broadcast([P, C, NH]), ALU.mult))
                    if at == VECTOR_AT["out"]:
                        dve.wait_ge(t.pool.sem, t.pool.after(b, "fmul"))
                        dve.wait_ge(x2_kept, (b + 1) * 16)
                        if t is tail_a:
                            wait(dve, out_done, b * 16)
                        step("out", nc.vector.tensor_tensor(t.out, slot(x2ring), t.mul.rearrange("p g d -> p (g d)"), ALU.add))

                for k in range(4):
                    for s in range(SLOTS):
                        at = (k, s)
                        if ph.block(k, 1) and s == SPLIT_SLOT:
                            b, n = head(v, k, 1)
                            i = b * 4 + n
                            before = use_before(ph, v, "mT", k)
                            if before:
                                dve.wait_ge(sh_full[before[0]], before[1])
                            dve.wait_ge(mx_free, (i + 1) * J)
                            nc.vector.tensor_scalar(m2[:, 0:J], mx[:, n % 2, :], 1.0 / MSCALE, None, ALU.mult).then_inc(m2_done, 1)
                            dve.wait_ge(m2_done, i * 2 + 1)
                            nc.vector.scalar_tensor_tensor(out=m2[:, J:2 * J], in0=mx[:, n % 2, :], scalar=1.0 / MSCALE,
                                                           in1=m2[:, 0:J], op0=ALU.mult, op1=ALU.subtract).then_inc(m2_done, 1)
                        if ph.att and s == V_SLOT:
                            wait(dve, o_done, (v - 1) * 4 + k + 1)
                            if k == 0:
                                dve.wait_ge(sh_free[BANK["v", 3]], iteration_start(ph, v, BANK["v", 3]))
                            nc.vector.tensor_copy(V[:, k], vnew[:, :, D * k:D * k + D]).then_inc(v_copied, 1)
                        if ph.att:
                            reduce_max(v, k, *MAX_TILES[s])
                        if ph.block(k, 3) and s == OM_SLOT:
                            b, n = head(v, k, 3)
                            dve.wait_ge(o_done, b * 4 + n + 1)
                            dve.wait_ge(mask_in[n], (b + 1) * 16)
                            before = use_before(ph, v, "nat1", k)
                            if before:
                                dve.wait_ge(sh_full[before[0]], before[1])
                            nc.vector.tensor_tensor(Om[:], O[:], mrep[:, n, :], ALU.mult).then_inc(om_done, 1)
                        for name, uk, us in USES:
                            if (uk, us) == at and ph.has(name, k):
                                read(name, k)
                        if ph.prep:
                            prep(v + 1, at)
                        if ph is PHASES[0] and at == (0, 0):
                            place()
                        if ph.prev:
                            mix(v - 1, at)
                        for t, b in tails(ph, v, tail_a, tail_b):
                            tail(t, b, at)

            run(dve, body)


def kernel(x, adj, L0_gnn_W_msg, L0_gnn_W_upd, L0_gnn_bias, L0_ffn_hl_w, L0_ffn_hl_b, L0_ffn_wq, L0_ffn_wk, L0_ffn_wv,
           L0_ffn_gate_w, L0_ffn_gate_b, L0_ffn_ln_g, L0_ffn_ln_b, L0_ffn_fc1_w, L0_ffn_fc1_b, L0_ffn_fc2_w, L0_ffn_fc2_b,
           L0_ffn_fnorm_g, L0_ffn_fnorm_b, L0_ffn_fgate_w):
    import concourse.bacc as bacc
    from concourse.bass_utils import run_bass_kernel_spmd

    def lay(a, *shape, perm=None):
        a = np.asarray(a)
        if perm is not None:
            a = a.transpose(perm)
        return np.ascontiguousarray(a.reshape(shape) if shape else a)

    arrays = {
        "x": lay(x),
        "adj": lay(adj),
        "w_mu": np.stack([np.asarray(L0_gnn_W_msg), np.asarray(L0_gnn_W_upd)]),
        "w_p": np.concatenate([lay(L0_ffn_hl_w, H, H, perm=(2, 0, 1)), lay(L0_ffn_hl_b, H, 1),
                               lay(L0_ffn_wq, H, NE * D, perm=(0, 3, 1, 2)), lay(L0_ffn_wk, H, D, perm=(0, 2, 1)),
                               lay(L0_ffn_wv, H, D, perm=(0, 2, 1)),
                               lay(np.asarray(L0_ffn_gate_w).reshape(NH, NE, NE, D), H, NH * NE, perm=(2, 3, 0, 1)),
                               lay(L0_ffn_fgate_w, perm=(1, 0))], axis=1),
        "w_d": np.concatenate([lay(L0_ffn_fc1_w, perm=(1, 0)), lay(L0_ffn_fc2_w, perm=(1, 0)), lay(L0_ffn_fc1_b, D, 1)], axis=1),
        "w_r": np.concatenate([lay(a, 1, -1) for a in (L0_gnn_bias, L0_ffn_gate_b, L0_ffn_ln_g, L0_ffn_ln_b, L0_ffn_fc2_b,
                                                       L0_ffn_fnorm_g, L0_ffn_fnorm_b)], axis=1),
    }
    nc = bacc.Bacc("TRN2", target_bir_lowering=False, num_devices=1)
    args = [nc.dram_tensor(name, a.shape, mybir.dt.from_np(a.dtype), kind="ExternalInput").ap() for name, a in arrays.items()]
    out = nc.dram_tensor("out", (B, S, H), F32, kind="ExternalOutput").ap()
    build(nc, *args, out)
    r = run_bass_kernel_spmd(nc, [arrays], core_ids=[0])
    return r.results[0]["out"]
```

```python
from contextlib import ExitStack

import numpy as np
import concourse.bass as bass
from concourse import mybir

ALU = mybir.AluOpType
ACT = mybir.ActivationFunctionType
AX = mybir.AxisListType
F32 = mybir.dt.float32
F16 = mybir.dt.float16
BF16 = mybir.dt.bfloat16
I32 = mybir.dt.int32

B, S, H = 16, 512, 128
NH, NE = 4, 4
D = H // NH
P = 128
C = S // P
J = NE * C
EPS_GNN, EPS_FFN = 1e-5, 1e-8
SCALE = float(D) ** 0.5
MSCALE = 64.0
BIG = -1e30
NATW = P + NE * NE
FGW = 96
TAIL_LAG = 3
X2_RING, MIX_RING = 8, 4

SLOTS = 16
MX_BANKS = 3
MAX_TILES = [(2, 3, 1), (2, 0, 1), (3, 2, 1), (0, 0, 4), (3, 0, 1), (1, 2, 2), (2, 2, 1), (3, 3, 1),
             (3, 1, 1), (1, 0, 2), (2, 1, 1)]
MAX_SLOT = [0, 1, 3, 4, 5, 7, 8, 9, 12, 14, 15]
TILES = len(MAX_TILES)
CHUNKS = [(0, e, 1) for e in range(4)] + [(1, e, 1) for e in range(4)] + [(2, 0, 2), (2, 2, 2), (3, 0, 4)]
CHUNK_SLOT = [0, 1, 2, 3, 5, 5, 9, 9, 13, 14, 15]
PT_OFF = [0, 2048, 3584, 4608]
PT_W = 5120
LAST_CHUNK = [3, 7, 9, 10]
AV_SLOT = [6, 11, 16, 16]
ADD_SLOT = [10, 16, 19]

USES = [
    ("mT", 0, 0, 1), ("q", 0, 1, 0), ("nat0", 0, 1, 1), ("nat1", 0, 3, 1), ("xnT", 0, 7, 0), ("L", 0, 7, 1),
    ("LT", 0, 9, 0), ("hu0", 0, 10, 1), ("hu1", 0, 15, 0),
    ("mT", 1, 0, 1), ("q", 1, 2, 0), ("msg0", 1, 2, 1), ("msg1", 1, 2, 0), ("nat0", 1, 5, 1), ("nat1", 1, 6, 1),
    ("L", 1, 7, 0), ("fxT", 1, 9, 1), ("LT", 1, 9, 0), ("fxT_b", 1, 9, 0), ("h1T", 1, 14, 1), ("h1T_b", 1, 15, 0),
    ("h2", 2, 1, 1), ("q", 2, 3, 1), ("h2_b", 2, 3, 1), ("mT", 2, 4, 0), ("L", 2, 7, 1), ("nat0", 2, 7, 0),
    ("LT", 2, 8, 1), ("nat1", 2, 10, 0), ("xn2T", 2, 12, 1),
    ("mT", 3, 1, 0), ("sxT", 3, 2, 1), ("nat0", 3, 3, 0), ("q", 3, 4, 1), ("foT", 3, 7, 0), ("kT", 3, 7, 1),
    ("L", 3, 7, 0), ("foT_b", 3, 8, 1), ("v", 3, 9, 0), ("nat1", 3, 9, 1), ("sxn", 3, 11, 1), ("fg", 3, 13, 0),
    ("LT", 3, 14, 0), ("fg_b", 3, 15, 1),
]
SPLIT_SLOT, V_SLOT, OM_SLOT = 0, 7, 0
VECTOR_AT = {
    "stats": (0, 0), "xn": (0, 3), "upd0": (0, 12), "upd1": (0, 15), "agg0": (1, 2), "agg1": (1, 4), "x2": (1, 5),
    "stats2": (1, 5), "xn2": (1, 15), "nz": (3, 10), "gate": (2, 11), "gate2": (3, 1), "y": (0, 6), "xc": (0, 6),
    "var": (0, 10), "xs": (1, 1), "nzf": (1, 14), "y2": (2, 2), "mean2": (2, 3), "xc2": (2, 3), "var2": (2, 4),
    "xs2": (2, 13), "head": (3, 12), "head2": (3, 12), "out": (3, 15),
}
SCALAR_AT = {
    "adj": (0, 4), "lex": (2, 14), "sq": (0, 11), "sq2": (2, 4), "fex": (3, 11),
}
POOL_AT = {
    "rs": (0, 0), "rs2": (1, 13), "mix0": (3, 3), "mix1": (3, 4), "mix2": (3, 5), "mix3": (3, 15), "trs": (0, 12),
    "g": (1, 0), "fx": (1, 5), "h1m": (1, 15), "trs2": (2, 7), "g2": (2, 13), "fo": (2, 13), "fmul": (3, 12),
}
BANK = {(name, k): bank for name, k, _, bank in USES}


def mx_bank(n, pos):
    return (n * TILES + pos) % MX_BANKS


def mx_before(n, pos):
    g = n * TILES + pos
    if g >= MX_BANKS:
        return g - MX_BANKS
    return max(i for i in range(NH * TILES) if i % MX_BANKS == g) - NH * TILES


class Phase:

    def __init__(self, v0, count):
        self.v0, self.count = v0, count
        v = v0
        self.att = 0 <= v < B
        self.prep = v + 1 < B
        self.load = v + 2 < B
        self.prev = 1 <= v <= B
        self.tail = TAIL_LAG <= v < B + TAIL_LAG
        self.resid = v + 1 < NH
        self.ending = v >= B
        self.pair = v == B + 1
        self.uses = [(n, k) for n, k, _, _ in USES if self.has(n, k)]

    def has(self, name, k):
        if name in ("xnT", "hu0", "hu1", "msg0", "msg1", "xn2T", "sxT", "kT", "v"):
            return self.prep
        if name == "sxn":
            return self.prep and self.resid
        if name in ("fxT", "h1T", "h2", "foT", "fg"):
            return self.tail
        if name in ("fxT_b", "h1T_b", "h2_b", "foT_b", "fg_b"):
            return self.pair
        return {"q": self.query(k), "mT": self.block(k, 1), "nat0": self.block(k, 3), "nat1": self.block(k, 3),
                "L": self.block(k, 3), "LT": self.block(k, 3)}[name]

    def query(self, k):
        return self.att if k < 3 else self.prep

    def block(self, k, lag):
        return self.att if k >= lag else self.prev


PHASES = [Phase(-1, 1), Phase(0, 1), Phase(1, 1), Phase(2, 1), Phase(3, B - 5), Phase(B - 2, 1), Phase(B - 1, 1), Phase(B, 1),
          Phase(B + 1, 1)]


def use_count(ph, v, name, k):
    bank = BANK[name, k]
    base = 0
    for q in PHASES:
        mine = [u for u in q.uses if BANK[u] == bank]
        if q is ph:
            at = base + mine.index((name, k))
            return bank, (at if isinstance(v, int) else (v - ph.v0) * len(mine) + at)
        base += q.count * len(mine)


def use_before(ph, v, name, k):
    if k > 0:
        if not ph.has(name, k - 1):
            return None
        bank, c = use_count(ph, v, name, k - 1)
        return bank, c + 1
    if ph is PHASES[0] or not PHASES[PHASES.index(ph) - 1].has(name, 3):
        return None
    return BANK[name, 3], iteration_start(ph, v, BANK[name, 3])


def iteration_start(ph, v, bank):
    base = 0
    for q in PHASES:
        mine = len([u for u in q.uses if BANK[u] == bank])
        if q is ph:
            return base if isinstance(v, int) else (v - ph.v0) * mine + base
        base += q.count * mine


class Steps:

    def __init__(self, sem, names, first=0):
        self.sem, self.names, self.first = sem, names, first

    def after(self, b, name):
        return (b - self.first) * len(self.names) + self.names.index(name) + 1


class Tail:

    def __init__(self, first, sem, tile):
        self.first = first

        def groups(name):
            return tile(f"{name}_{first}", NH * C * D).rearrange("p (g d) -> p g d", d=D)

        def small(name):
            return tile(f"{name}_{first}", NH * C)

        self.y, self.xc, self.sq, self.xs = groups("ty"), groups("txc"), groups("tsq"), groups("txs")
        self.fx, self.fo, self.mul = groups("fx"), groups("fo"), groups("fmul")
        self.g, self.w, self.u = self.y, self.sq, self.xs
        self.sum, self.mean, self.vs, self.ve, self.rs = small("tsum"), small("tmean"), small("tvs"), small("tve"), small("trs")
        self.fxT, self.nzf, self.h1r, self.h1m, self.out = [
            tile(f"{name}_{first}", S) for name in ("fxT", "nzf", "h1r", "h1m", "outb")]
        self.foT = self.fxT
        self.fsub, self.fex, self.fgs = [small(name).rearrange("p (c n) -> p c n", n=NH) for name in ("fsub", "fex", "fgs")]
        self.fmax, self.fsum, self.frec = [tile(f"{name}_{first}", C) for name in ("fmax", "fsum", "frec")]
        self.dve = Steps(sem(f"tail_vector_{first}"), ("y", "sum", "mean", "xc", "vs", "ve", "xs", "nzf", "u", "w", "y2", "sum2",
                                                       "mean2", "xc2", "vs2", "ve2", "xs2", "fmax", "fsub", "fsum", "frec", "fgs",
                                                       "out"), first)
        self.act = Steps(sem(f"tail_scalar_{first}"), ("sq", "sq2", "fex"), first)
        self.pool = Steps(sem(f"tail_pool_{first}"), ("rs", "g", "fx", "h1m", "rs2", "g2", "fo", "fmul"), first)

    def use(self, name):
        return name + "_b" if self.first else name


def wait(eng, sem, value):
    if not isinstance(value, int) or value > 0:
        eng.wait_ge(sem, value)


def head(v, k, lag):
    return (v, k - lag) if k >= lag else (v - 1, k - lag + 4)


def columns(*parts):
    at, cols = 0, {}
    for name, w in parts:
        cols[name] = slice(at, at + w)
        at += w
    return cols, at


WP, WP_W = columns(("hlwT", H), ("hlb", 1), ("wq", NE * D), ("wk", D), ("wv", D), ("gate", NH * NE), ("fgate", NH))
WD, WD_W = columns(("fc1", D), ("fc2", D), ("fc1_b", 1))
WR, WR_W = columns(("gnn_b", H), ("gate_b", NH * NE), ("ln_g", D), ("ln_b", D), ("fc2_b", D), ("fn_g", D), ("fn_b", D))


def tails(ph, v, a, b):
    return ([(a, v - TAIL_LAG)] if ph.tail else []) + ([(b, v - TAIL_LAG + 1)] if ph.pair else [])


def build(nc, x, adj, w_mu, w_p, w_d, w_r, out):
    ctx = ExitStack()
    with ctx:
        def sb(name, shape, dt=F32):
            return ctx.enter_context(nc.sbuf_tensor(name, shape, dt))

        def sem(name):
            return ctx.enter_context(nc.semaphore(name))

        ident = sb("ident", [P, P])
        ident16 = sb("ident16", [P, P], F16)
        identb = sb("identb", [P, P], BF16)
        maskneg = sb("maskneg", [P, NE, P], BF16)
        masknegT = sb("masknegT", [P, NE, P], BF16)
        blocks = sb("blocks", [P, NH])
        ones = sb("ones", [P, D])
        warm = sb("warm", [P, 1])
        mhalf = sb("mhalf", [P, 16])
        w_mu_s = sb("w_mu_s", [P, 2, H])
        wp_s = sb("wp_s", [P, WP_W])
        wd_s = sb("wd_s", [P, WD_W])
        wr_s = sb("wr_s", [P, WR_W])
        hlwT_s, hlb_s, fc1b_s = wp_s[:, WP["hlwT"]], wp_s[:, WP["hlb"]], wd_s[:, WD["fc1_b"]]
        gnnb_s, fc2b_s = wr_s[:, WR["gnn_b"]], wr_s[:, WR["fc2_b"]]
        gb_s = wr_s[:, WR["gate_b"]].rearrange("p (n e) -> p n e", n=NH)
        wq_s = sb("wq_s", [P, NH, NE * D])
        wk_s = sb("wk_s", [P, H])
        wv_s = sb("wv_s", [P, H])
        fc1_s = sb("fc1_s", [P, H])
        fc2_s = sb("fc2_s", [P, H])
        nat_w = sb("nat_w", [P, NH, NATW])
        fgT_s = sb("fgT_s", [P, FGW])

        xin = sb("xin", [P, C, H])
        adj_i = sb("adj_i", [P, C, S], I32)
        adj_f = sb("adj_f", [P, C, S])
        bst = sb("bst", [P, C, 6])
        mv = sb("mv", [P, C, 2])
        ve = sb("ve", [P, C])
        rs = sb("rs", [P, C])
        xn = sb("xn", [P, C, H])
        xnT = sb("xnT", [P, S])
        hS = sb("hS", [P, C, 132])
        upd = sb("upd", [P, C, H])
        dmax = sb("dmax", [P, 2])
        drec = sb("drec", [P, 2])
        dgs = sb("dgs", [P, 2])
        agg = sb("agg", [P, C, H])
        x2 = sb("x2", [P, C, H])
        sxT = sb("sxT", [P, S])
        nzT = sb("nzT", [P, S], BF16)
        khi = sb("khi", [P, S], F16)
        klo = sb("klo", [P, S], F16)
        vnew = sb("vnew", [P, C, H])
        resid = sb("resid", [P, C, NH, D])
        x2ring = sb("x2ring", [P, X2_RING, C * H])
        mixring = sb("mixring", [P, MIX_RING, C * H])

        qhi = sb("qhi", [P, S], F16)
        qlo = sb("qlo", [P, S], F16)
        QT = sb("QT", [P, NH, NE, S], F16)
        KT = sb("KT", [98, NH, S], F16)
        V = sb("V", [P, NH, C, D])
        mx = sb("mx", [P, 2, NE, C])
        m2 = sb("m2", [P, 2 * J], F16)
        mT = sb("mT", [2 * J, P], F16)
        PT = sb("PT", [P, 2, PT_W])
        psum = sb("psum", [P, NE, S - P])
        mrep = sb("mrep", [P, NH, S], BF16)
        Om = sb("Om", [P, S])
        Lsb = sb("Lsb", [P, S])
        nat = sb("nat", [P, NH, C, NATW])
        rL = sb("rL", [P, NH, C, NE])

        G16 = NH * C
        zr = sb("zr", [P, G16, NE, NE])
        lg = sb("lg", [P, G16, NE])
        lgb = sb("lgb", [P, G16, NE])
        lmax = sb("lmax", [P, G16])
        lsub = sb("lsub", [P, G16, NE])
        lex = sb("lex", [P, G16, NE])
        lsum = sb("lsum", [P, G16])
        lrec = sb("lrec", [P, G16])
        lw = sb("lw", [P, G16, NE])
        lw2 = sb("lw2", [P, G16, NE])
        prod = sb("prod", [P, 2, C, NE, D])
        half = sb("half", [P, 2, C, 2, D])
        mixed = sb("mixed", [P, C, NH, D])

        tail_a = Tail(0, sem, lambda name, width: sb(name, [P, width])[:])
        spare = PT[:].rearrange("p a w -> p (a w)")
        taken = [0]

        def from_spare(name, width):
            taken[0] += width
            return spare[:, taken[0] - width:taken[0]]

        tail_b = Tail(B - 1, sem, from_spare)

        MX = ctx.enter_context(nc.psum_tensor("MX", [P, MX_BANKS, 512], F32))
        ST = ctx.enter_context(nc.psum_tensor("ST", [P, 2, 512], F32))
        O = ctx.enter_context(nc.psum_tensor("O", [P, 512], F32))
        SH = ctx.enter_context(nc.psum_tensor("SH", [P, 2, 512], F32))

        q_dram = nc.dram_tensor("q_scratch", (2, D, NE, S), F16, kind="Internal").ap()
        nz_dram = nc.dram_tensor("nonzero_scratch", (P, S), BF16, kind="Internal").ap()

        w_in = sem("weights_loaded")
        placed = sem("weights_placed")
        q_out = sem("q_in_scratch")
        nz_out = sem("nonzero_in_scratch")
        c_done = sem("constants_built")
        k_rows = sem("key_rows_set")
        passed = sem("waits_passed")
        x_in = sem("x_loaded")
        adj_in = sem("adj_loaded")
        x2_kept = sem("x2_kept")
        mix_kept = sem("mixed_kept")
        out_done = sem("out_stored")
        q_in = [sem(f"q_loaded{n}") for n in range(NH)]
        k_in = [sem(f"k_loaded{n}") for n in range(NH)]
        m_in = [sem(f"max_loaded{n}") for n in range(NH)]
        mask_in = [sem(f"mask_loaded{n}") for n in range(NH)]
        sh_full = [sem(f"shared_full{i}") for i in range(2)]
        sh_free = [sem(f"shared_free{i}") for i in range(2)]
        mx_full = sem("max_scores_full")
        mx_free = sem("max_scores_reduced")
        st_full = sem("scores_full")
        exp_done = sem("exp_done")
        added = sem("probabilities_added")
        o_done = sem("outputs_done")
        m2_done = sem("max_split")
        v_copied = sem("v_copied")
        om_done = sem("outputs_masked")
        qhi_done = sem("q_high")
        khi_done = sem("k_high")
        g_dve = Steps(sem("prep_vector"), ("stats", "aggr", "var", "xn", "deg0", "rec0", "gs0", "agg0", "deg1", "rec1",
                                           "gs1", "agg1", "x2", "stats2", "aggr2", "var2", "xn2", "nz"))
        g_act = Steps(sem("prep_scalar"), ("adj", "h0", "h1"))
        g_pool = Steps(sem("prep_pool"), ("rs", "rs2"))
        x_dve = Steps(sem("mix_vector"), ("zr", "lg", "lgb", "lmax", "lsub", "lsum", "lrec", "lw", "lw2"))
        x_act = Steps(sem("mix_scalar"), ("lex",))
        x_pool = Steps(sem("mix_pool"), tuple(f"{w}{n}" for n in range(NH) for w in ("prod", "half", "mixed")))

        block = ctx.enter_context(nc.Block())

        def held(eng):
            eng.sem_inc(passed, 1)

        def run(eng, body):
            for ph in PHASES:
                if ph.count == 1:
                    body(ph, ph.v0)
                else:
                    with eng.Fori(ph.v0, ph.v0 + ph.count) as v:
                        body(ph, v)

        @block.sync
        def _(sp):
            def ready(sem, value):
                if not isinstance(value, int) or value > 0:
                    sp.wait_ge(sem, value)
                    held(sp)

            def loads(b):
                if isinstance(b, int):
                    xb, ab = x[b], adj[b]
                else:
                    xb, ab = x[bass.ds(b, 1)].rearrange("a s f -> (a s) f"), adj[bass.ds(b, 1)].rearrange("a s f -> (a s) f")
                ready(g_dve.sem, g_dve.after(b - 1, "x2"))
                sp.dma_start(xin[:], xb.rearrange("(c p) f -> p c f", p=P)).then_inc(x_in, 16)
                ready(g_act.sem, g_act.after(b - 1, "adj"))
                sp.dma_start(adj_i[:], ab.rearrange("(c p) j -> p c j", p=P)).then_inc(adj_in, 16)

            loads(0)
            sp.dma_start(w_mu_s[:], w_mu.rearrange("t p f -> p t f")).then_inc(w_in, 16)
            sp.dma_start(wr_s[:], w_r.to_broadcast([P, WR_W])).then_inc(w_in, 16)
            sp.dma_start(wp_s[:], w_p).then_inc(w_in, 16)
            sp.dma_start(wd_s[:], w_d.unsqueeze(0).to_broadcast([NH, D, WD_W])).then_inc(w_in, 16)

            def body(ph, v):
                for k in range(4):
                    if k < 3 and ph.att:
                        load_keys(v, k + 1)
                    if ph.att:
                        ready(nz_out, (v + 1) * 16)
                        ready(om_done, (v - 1) * 4 + k + 1)
                        sp.dma_start(mrep[:, k, :], nz_dram[D * k:D * k + D].unsqueeze(0).to_broadcast([NE, D, S])
                                     ).then_inc(mask_in[k], 16)
                    if ph.block(k, 1):
                        b, n = head(v, k, 1)
                        bank, c = use_count(ph, v, "mT", k)
                        ready(sh_free[bank], c + 1)
                        sp.dma_start(QT[96:98, n].rearrange("r e (c s) -> r (e c) s", s=P), mT[:]).then_inc(m_in[n], 16)
                    if ph.query(k):
                        b, n = (v, k + 1) if k < 3 else (v + 1, 0)
                        bank, c = use_count(ph, v, "q", k)
                        ready(sh_free[bank], c + 1)
                        ready(st_full, (b - 1) * 44 + (n + 1) * 11)
                        for r, part in enumerate((qhi, qlo)):
                            sp.dma_start(q_dram[r].rearrange("d e s -> e d s"), part[:]).then_inc(q_out, 16)
                        ready(q_out, (b * 4 + n + 1) * 32)
                        sp.dma_start(QT[:, n].rearrange("p e s -> p (e s)"),
                                     q_dram.rearrange("r d e s -> (r d) (e s)").unsqueeze(0).to_broadcast([2, 2 * D, NE * S])
                                     ).then_inc(q_in[n], 16)
                    if k == 1 and ph.prep:
                        ready(g_dve.sem, g_dve.after(v + 1, "x2"))
                        keep(x2ring, v + 1, x2[:].rearrange("p c f -> p (c f)"), x2_kept)
                        if ph.load:
                            loads(v + 2)
                    if k == 3 and ph.prep:
                        load_keys(v + 1, 0)
                        ready(g_dve.sem, g_dve.after(v + 1, "nz"))
                        for m in range(NH):
                            ready(mask_in[m], (v + 1) * 16)
                        sp.dma_start(nz_dram, nzT[:]).then_inc(nz_out, 16)
                    if k == 3 and ph.prev:
                        ready(x_pool.sem, x_pool.after(v - 1, "mixed3"))
                        keep(mixring, v - 1, mixed[:].rearrange("p c n d -> p (c n d)"), mix_kept)
                    if k == 3:
                        for t, b in tails(ph, v, tail_a, tail_b):
                            ready(t.dve.sem, t.dve.after(b, "out"))
                            ob = out[b] if isinstance(b, int) else out[bass.ds(b, 1)].rearrange("a s f -> (a s) f")
                            sp.dma_start(ob.rearrange("(c p) f -> p c f", p=P), t.out.rearrange("p (c f) -> p c f", c=C)
                                         ).then_inc(out_done, 16)

            def keep(ring, b, src, done):
                size = ring.shape[1]
                dst = ring[:, b % size] if isinstance(b, int) else ring[:, bass.ds(b % size, 1)].rearrange("p a f -> p (a f)")
                sp.dma_start(dst, src).then_inc(done, 16)

            def load_keys(b, n):
                ready(khi_done, (b + 1) * 2)
                ready(st_full, (b - 1) * 44 + (n + 1) * 11)
                r = slice(D * n, D * n + D)
                sp.dma_start(KT[0:D, n, :], khi[r, :]).then_inc(k_in[n], 16)
                sp.dma_start(KT[D:2 * D, n, :], khi[r, :]).then_inc(k_in[n], 16)
                sp.dma_start(KT[2 * D:3 * D, n, :], klo[r, :]).then_inc(k_in[n], 16)

            run(sp, body)
            sp.wait_ge(out_done, 16 * B)

        N_W = 4

        def mix_head(eng, b, n):
            if n == 0:
                eng.wait_ge(x_dve.sem, x_dve.after(b, "lw2"))
            if n >= 2:
                eng.wait_ge(x_pool.sem, x_pool.after(b, f"half{n - 2}"))
            else:
                wait(eng, x_pool.sem, x_pool.after(b - 1, f"half{n + 2}"))
            w = lw2[:, n * C:n * C + C, :].unsqueeze(3).to_broadcast([P, C, NE, D])
            eng.tensor_tensor(prod[:, n % 2], nat[:, n, :, 0:P].rearrange("p c (e d) -> p c e d", d=D), w,
                              ALU.mult).then_inc(x_pool.sem, 1)
            eng.wait_ge(x_pool.sem, x_pool.after(b, f"prod{n}"))
            eng.tensor_tensor(half[:, n % 2], prod[:, n % 2, :, 0:2, :], prod[:, n % 2, :, 2:4, :],
                              ALU.add).then_inc(x_pool.sem, 1)
            eng.wait_ge(x_pool.sem, x_pool.after(b, f"half{n}"))
            if n == 0:
                wait(eng, mix_kept, b * 16)
            eng.tensor_tensor(mixed[:, :, n, :], half[:, n % 2, :, 0, :], half[:, n % 2, :, 1, :],
                              ALU.add).then_inc(x_pool.sem, 1)

        def add_chunk(eng, ph, v, k, b, n, t):
            i = b * 4 + n
            eng.wait_ge(exp_done, i * 11 + LAST_CHUNK[t] + 1)
            w = S - P * t
            new = PT[:, n % 2, PT_OFF[t]:PT_OFF[t] + NE * w].rearrange("p (e s) -> p e s", e=NE)
            if t == 1:
                if ph.has("L", k):
                    bank, c = use_count(ph, v, "L", k)
                    eng.wait_ge(sh_full[bank], c + 1)
                old = PT[:, n % 2, 0:NE * S].rearrange("p (e s) -> p e s", e=NE)[:, :, P:S]
            else:
                eng.wait_ge(added, i * 3 + t - 1)
                old = psum[:, :, P * (t - 1):S - P]
            eng.tensor_tensor(psum[:, :, P * (t - 1):S - P], old, new, ALU.add).then_inc(added, 1)

        def product(eng, ph, v, t, b, step):
            def row(name):
                return wr_s[:, WR[name]].unsqueeze(1).to_broadcast([P, G16, D])

            if step in ("g", "g2"):
                eng.wait_ge(w_in, 16 * N_W)
                eng.wait_ge(t.dve.sem, t.dve.after(b, "xs" if step == "g" else "xs2"))
                eng.tensor_tensor(t.g, t.xs, row("ln_g" if step == "g" else "fn_g"), ALU.mult).then_inc(t.pool.sem, 1)
            elif step == "fx":
                eng.wait_ge(t.pool.sem, t.pool.after(b, "g"))
                eng.tensor_tensor(t.fx, t.g, row("ln_b"), ALU.add).then_inc(t.pool.sem, 1)
            elif step == "fo":
                eng.wait_ge(t.pool.sem, t.pool.after(b, "g2"))
                eng.tensor_tensor(t.fo, t.g, row("fn_b"), ALU.add).then_inc(t.pool.sem, 1)
            elif step == "h1m":
                bank, c = use_count(ph, v, t.use("h1T"), 1)
                eng.wait_ge(sh_free[bank], c + 1)
                eng.wait_ge(t.dve.sem, t.dve.after(b, "nzf"))
                eng.tensor_tensor(t.h1m, t.h1r, t.nzf, ALU.mult).then_inc(t.pool.sem, 1)
            elif step == "fmul":
                eng.wait_ge(t.dve.sem, t.dve.after(b, "fgs"))
                gate = t.fgs.rearrange("p c n -> p (c n)").unsqueeze(2).to_broadcast([P, G16, D])
                eng.tensor_tensor(t.mul, t.fo, gate, ALU.mult).then_inc(t.pool.sem, 1)

        @block.gpsimd
        def _(pool):
            pool.memset(mhalf[:], -0.5)
            for t in (ident, ident16, identb, maskneg):
                pool.memset(t[:], 0.0)
            pool.memset(masknegT[:], 0.0)
            pool.memset(blocks[:], 1.0)
            pool.memset(nat_w[:, :, 0:P], 0.0)
            pool.memset(fgT_s[:], 0.0)
            pool.memset(ones[:], 1.0)
            pool.memset(hS[:, :, H:H + 1], 1.0)
            pool.memset(hS[:, :, H + 1:132], 0.0).then_inc(c_done, 1)
            pool.wait_ge(c_done, 1)
            for t in (ident, ident16, identb):
                pool.affine_select(out=t[:], in_=t[:], compare_op=ALU.not_equal, fill=1.0, base=0, pattern=[[-1, P]],
                                   channel_multiplier=1)
            for n in range(NH):
                pool.affine_select(out=nat_w[:, n, 0:P], in_=nat_w[:, n, 0:P], compare_op=ALU.not_equal, fill=1.0, base=0,
                                   pattern=[[-1, P]], channel_multiplier=1)
            pool.affine_select(out=masknegT[:], in_=masknegT[:], compare_op=ALU.is_ge, fill=BIG, base=0,
                               pattern=[[0, NE], [1, P]], channel_multiplier=-1)
            pool.affine_select(out=blocks[:], in_=blocks[:], compare_op=ALU.is_ge, fill=0.0, base=0,
                               pattern=[[-D, NH]], channel_multiplier=1)
            pool.affine_select(out=maskneg[:], in_=maskneg[:], compare_op=ALU.is_ge, fill=BIG, base=0,
                               pattern=[[0, NE], [-1, P]], channel_multiplier=1).then_inc(c_done, 1)
            pool.wait_ge(c_done, 2)
            pool.affine_select(out=blocks[:], in_=blocks[:], compare_op=ALU.is_ge, fill=0.0, base=D - 1,
                               pattern=[[D, NH]], channel_multiplier=-1).then_inc(c_done, 1)

            def power(steps, dst, src):
                pool.tensor_tensor(dst, src, mhalf[:, 0:src.shape[-1]], ALU.pow).then_inc(steps.sem, 1)

            def body(ph, v):
                for k in range(4):
                    for s in range(SLOTS):
                        at = (k, s)
                        for t, slot in enumerate(ADD_SLOT[0:2]):
                            lag = 2 + slot // SLOTS
                            if slot % SLOTS == s and ph.block(k, lag):
                                add_chunk(pool, ph, v, k, *head(v, k, lag), t + 1)
                        if ph.prep and at == POOL_AT["rs"]:
                            pool.wait_ge(g_dve.sem, g_dve.after(v + 1, "var"))
                            power(g_pool, rs[:], ve[:])
                        if ph.prep and at == POOL_AT["rs2"]:
                            pool.wait_ge(g_dve.sem, g_dve.after(v + 1, "var2"))
                            power(g_pool, rs[:], ve[:])
                        for n in range(NH):
                            if ph.prev and at == POOL_AT[f"mix{n}"] and not ph.ending:
                                mix_head(pool, v - 1, n)
                        for t, b in tails(ph, v, tail_a, tail_b):
                            tail(ph, v, t, b, at)

            def tail(ph, v, t, b, at):
                if at == POOL_AT["trs"]:
                    pool.wait_ge(t.dve.sem, t.dve.after(b, "ve"))
                    power(t.pool, t.rs, t.ve)
                if at == POOL_AT["trs2"]:
                    pool.wait_ge(t.dve.sem, t.dve.after(b, "ve2"))
                    power(t.pool, t.rs, t.ve)
                for step in ("g", "fx", "h1m", "g2", "fo", "fmul"):
                    if at == POOL_AT[step] and not ph.ending:
                        product(pool, ph, v, t, b, step)

            run(pool, body)

        @block.tensor
        def _(pe):
            pe.wait_ge(c_done, 2)
            pe.wait_ge(k_rows, 1)
            pe.wait_ge(w_in, 16 * N_W)

            def body(ph, v):
                def shared(name, k):
                    bank, c = use_count(ph, v, name, k)
                    wait(pe, sh_free[bank], c)
                    return SH[:, bank], sh_full[bank]

                def done(name, k):
                    bank, c = use_count(ph, v, name, k)
                    pe.wait_ge(sh_free[bank], c + 1)

                def maxima(b, n, pos):
                    if pos == 0:
                        pe.wait_ge(q_in[n], (b + 1) * 16)
                        pe.wait_ge(k_in[n], (b + 1) * 16 * 3)
                    wait(pe, mx_free, b * NH * TILES + mx_before(n, pos) + 1)
                    c, e0, ne = MAX_TILES[pos]
                    w = P * (c + 1)
                    for i in range(ne):
                        nc.tensor.matmul(MX[:, mx_bank(n, pos), i * w:i * w + w], QT[0:96, n, e0 + i, P * c:P * c + P],
                                         KT[0:96, n, 0:w], start=(i == 0), stop=False)
                    diag = MX[:, mx_bank(n, pos), 0:ne * w].rearrange("p (e s) -> p e s", e=ne)[:, :, P * c:w]
                    nc.tensor.matmul(diag, identb[:], maskneg[:, 0:ne, :], start=False, stop=True).then_inc(mx_full, 1)

                def scores(b, n, c):
                    t, e0, ne = CHUNKS[c]
                    g = (b * 4 + n) * 11 + c
                    if c == 0:
                        pe.wait_ge(m_in[n], (b + 1) * 16)
                    wait(pe, exp_done, g - 1)
                    w = S - P * t
                    bank = ST[:, (11 * n + c) % 2, 0:ne * w].rearrange("p (e s) -> p e s", e=ne)
                    nc.tensor.matmul(bank, KT[:, n, P * t:P * t + P], QT[0:98, n, e0:e0 + ne, P * t:S],
                                     start=True, stop=False)
                    nc.tensor.matmul(bank[:, :, 0:P], identb[:], masknegT[:, 0:ne, :], start=False,
                                     stop=True).then_inc(st_full, 1)

                def values(b, n, t):
                    pe.wait_ge(exp_done, (b * 4 + n) * 11 + LAST_CHUNK[t] + 1)
                    if t == 0:
                        pe.wait_ge(v_copied, b * 4 + n + 1)
                        wait(pe, om_done, b * 4 + n)
                    w = S - P * t
                    for e in range(NE):
                        a = PT_OFF[t] + e * w
                        mm = nc.tensor.matmul(O[D * e:D * e + D, P * t:S], V[:, n, t, :], PT[:, n % 2, a:a + w],
                                              start=(t == 0), stop=(t == C - 1))
                    if t == C - 1:
                        mm.then_inc(o_done, 1)

                def transposes(dst, src, full):
                    for c in range(C):
                        mm = nc.tensor.transpose(dst[:, c * P:c * P + P], src[:, c, :], ident[:])
                    mm.then_inc(full, 1)

                def side(k, s):
                    for name, uk, us, _ in USES:
                        if (uk, us) != (k, s) or not ph.has(name, k):
                            continue
                        shared_use(name, k)

                def shared_use(name, k):
                    if name == "mT":
                        b, n = head(v, k, 1)
                        pe.wait_ge(m2_done, (b * 4 + n + 1) * 2)
                        dst, full = shared(name, k)
                        nc.tensor.transpose(dst.bitcast(F16)[0:2 * J, 0:P], m2[:], ident16[:]).then_inc(full, 1)
                    elif name == "q":
                        n = (k + 1) % 4
                        if k == 3:
                            done("sxT", 3)
                        dst, full = shared(name, k)
                        nc.tensor.matmul(dst, wq_s[:, n, :], sxT[:], start=True, stop=True).then_inc(full, 1)
                    elif name in ("nat0", "nat1"):
                        b, n = head(v, k, 3)
                        if name == "nat0":
                            pe.wait_ge(om_done, b * 4 + n + 1)
                        dst, full = shared(name, k)
                        for i in range(2):
                            c = 2 * int(name[3]) + i
                            mm = nc.tensor.matmul(dst[:, i * NATW:i * NATW + NATW], Om[:, c * P:c * P + P], nat_w[:, n, :],
                                                  start=True, stop=True)
                        mm.then_inc(full, 1)
                    elif name == "L":
                        b, n = head(v, k, 3)
                        dst, full = shared(name, k)
                        for e in range(NE):
                            nc.tensor.matmul(dst[D * e:D * e + D, 0:P], ones[:], PT[:, n % 2, e * S:e * S + P],
                                             start=True, stop=True)
                        pe.wait_ge(added, (b * 4 + n + 1) * 3)
                        for e in range(NE):
                            mm = nc.tensor.matmul(dst[D * e:D * e + D, P:S], ones[:], psum[:, e, :], start=True, stop=True)
                        mm.then_inc(full, 1)
                    elif name == "LT":
                        b, n = head(v, k, 3)
                        done("L", k)
                        dst, full = shared(name, k)
                        transposes(dst, Lsb[:].rearrange("p (c s) -> p c s", c=C), full)
                    elif name == "xnT":
                        pe.wait_ge(g_dve.sem, g_dve.after(v + 1, "xn"))
                        dst, full = shared(name, k)
                        transposes(dst, xn, full)
                    elif name in ("hu0", "hu1"):
                        done("xnT", 0)
                        dst, full = shared(name, k)
                        for i in range(2):
                            c = 2 * int(name[2]) + i
                            mm = nc.tensor.matmul(dst[:, i * 256:i * 256 + 256], xnT[:, c * P:c * P + P],
                                                  w_mu_s[:].rearrange("p t f -> p (t f)"),
                                                  start=True, stop=True)
                        mm.then_inc(full, 1)
                    elif name in ("msg0", "msg1"):
                        if name == "msg0":
                            pe.wait_ge(g_act.sem, g_act.after(v + 1, "h1"))
                        dst, full = shared(name, k)
                        for i in range(2):
                            jc = 2 * int(name[3]) + i
                            for ic in range(C):
                                mm = nc.tensor.matmul(dst[:, i * 130:i * 130 + 130], adj_f[:, ic, jc * P:jc * P + P],
                                                      hS[:, ic, 0:130], start=(ic == 0), stop=(ic == C - 1))
                        mm.then_inc(full, 1)
                    elif name == "xn2T":
                        pe.wait_ge(g_dve.sem, g_dve.after(v + 1, "xn2"))
                        dst, full = shared(name, k)
                        transposes(dst, xn, full)
                    elif name == "sxT":
                        if ph is PHASES[0]:
                            pe.wait_ge(placed, 1)
                        done("xn2T", 2)
                        dst, full = shared(name, k)
                        nc.tensor.matmul(dst, hlwT_s, xnT[:], start=True, stop=True).then_inc(full, 1)
                    elif name == "kT":
                        done("sxT", 3)
                        dst, full = shared(name, k)
                        nc.tensor.matmul(dst, wk_s[:], sxT[:], start=True, stop=True).then_inc(full, 1)
                    elif name == "v":
                        dst, full = shared(name, k)
                        for c in range(C):
                            mm = nc.tensor.matmul(dst[:, c * P:c * P + P], sxT[:, c * P:c * P + P], wv_s[:],
                                                  start=True, stop=True)
                        mm.then_inc(full, 1)
                    elif name == "sxn":
                        dst, full = shared(name, k)
                        transposes(dst, sxT[:].rearrange("p (c s) -> p c s", c=C), full)
                    else:
                        t, b = tails(ph, v, tail_a, tail_b)[name.endswith("_b")]
                        tail_use(t, b, name.removesuffix("_b"), k)

                def tail_use(t, b, name, k):
                    if name == "fxT":
                        pe.wait_ge(t.pool.sem, t.pool.after(b, "fx"))
                        dst, full = shared(t.use(name), k)
                        transposes(dst, t.fx.rearrange("p (c n) d -> p c (n d)", c=C), full)
                    elif name == "h1T":
                        done(t.use("fxT"), 1)
                        dst, full = shared(t.use(name), k)
                        nc.tensor.matmul(dst, fc1_s[:], t.fxT, start=True, stop=True).then_inc(full, 1)
                    elif name == "h2":
                        pe.wait_ge(t.pool.sem, t.pool.after(b, "h1m"))
                        dst, full = shared(t.use(name), k)
                        for c in range(C):
                            mm = nc.tensor.matmul(dst[:, c * P:c * P + P], t.h1m[:, c * P:c * P + P], fc2_s[:],
                                                  start=True, stop=True)
                        mm.then_inc(full, 1)
                    elif name == "foT":
                        pe.wait_ge(t.pool.sem, t.pool.after(b, "fo"))
                        dst, full = shared(t.use(name), k)
                        transposes(dst, t.fo.rearrange("p (c n) d -> p c (n d)", c=C), full)
                    elif name == "fg":
                        done(t.use("foT"), 3)
                        dst, full = shared(t.use(name), k)
                        for c in range(C):
                            mm = nc.tensor.matmul(dst[:, c * FGW:c * FGW + FGW], t.foT[:, c * P:c * P + P], fgT_s[:],
                                                  start=True, stop=True)
                        mm.then_inc(full, 1)

                for k in range(4):
                    for s in range(SLOTS):
                        if ph.block(k, 2):
                            b, n = head(v, k, 2)
                            for c in range(11):
                                if CHUNK_SLOT[c] == s:
                                    scores(b, n, c)
                        if ph.att:
                            for pos in range(TILES):
                                if MAX_SLOT[pos] == s:
                                    maxima(v, k, pos)
                        for t, at in enumerate(AV_SLOT):
                            lag = 2 + at // SLOTS
                            if at % SLOTS == s and ph.block(k, lag):
                                values(*head(v, k, lag), t)
                        side(k, s)

            run(pe, body)

        @block.scalar
        def _(act):
            act.wait_ge(w_in, 16 * N_W)
            nc.scalar.activation(warm[:], wp_s[:, 0:1], ACT.Exp)

            def body(ph, v):
                def full(name, k):
                    bank, c = use_count(ph, v, name, k)
                    act.wait_ge(sh_full[bank], c + 1)
                    return SH[:, bank], sh_free[bank]

                def exps(b, n, c):
                    t, e0, ne = CHUNKS[c]
                    g = (b * 4 + n) * 11 + c
                    if c == 0:
                        wait(act, o_done, b * 4 + n - 1)
                    act.wait_ge(st_full, g + 1)
                    w = S - P * t
                    a = PT_OFF[t] + e0 * w
                    nc.scalar.activation(PT[:, n % 2, a:a + ne * w], ST[:, (11 * n + c) % 2, 0:ne * w], ACT.Exp,
                                         scale=SCALE).then_inc(exp_done, 1)

                def side(k, s):
                    for name, uk, us, _ in USES:
                        if (uk, us) != (k, s) or not ph.has(name, k):
                            continue
                        read(name, k)

                def read(name, k):
                    if name == "mT":
                        b, n = head(v, k, 1)
                        src, free = full(name, k)
                        for m in range(NH):
                            if m == (n - 1) % 4:
                                wait(act, m_in[m], (b + 1) * 16 if n else b * 16)
                        nc.scalar.copy(mT[:], src.bitcast(F16)[0:2 * J, 0:P]).then_inc(free, 1)
                    elif name == "q":
                        b, n = (v, k + 1) if k < 3 else (v + 1, 0)
                        src, _ = full(name, k)
                        m = (n - 1) % 4
                        wait(act, q_in[m], ((b + 1) if n else b) * 16)
                        nc.scalar.copy(qhi[:], src).then_inc(qhi_done, 1)
                    elif name == "L":
                        src, free = full(name, k)
                        before = use_before(ph, v, "LT", k)
                        if before:
                            act.wait_ge(sh_full[before[0]], before[1])
                        nc.scalar.copy(Lsb[:], src).then_inc(free, 1)
                    elif name in ("nat0", "nat1"):
                        b, n = head(v, k, 3)
                        i = 2 * int(name[3])
                        src, free = full(name, k)
                        wait(act, x_pool.sem, x_pool.after(b - 1, f"prod{n}"))
                        nc.scalar.copy(nat[:, n, i:i + 2, :], src[:, 0:2 * NATW].rearrange("p (c w) -> p c w", c=2)
                                       ).then_inc(free, 1)
                    elif name in ("xnT", "xn2T"):
                        src, free = full(name, k)
                        nc.scalar.copy(xnT[:], src).then_inc(free, 1)
                    elif name in ("hu0", "hu1"):
                        i = 2 * int(name[2])
                        src, _ = full(name, k)
                        nc.scalar.copy(hS[:, i:i + 2, 0:H], src.rearrange("p (c w) -> p c w", c=2)[:, :, 0:H]
                                       ).then_inc(g_act.sem, 1)
                    elif name == "sxT":
                        src, free = full(name, k)
                        nc.scalar.activation(sxT[:], src, ACT.Identity, bias=hlb_s).then_inc(free, 1)
                    elif name == "kT":
                        src, _ = full(name, k)
                        wait(act, k_in[3], (v + 1) * 48)
                        nc.scalar.copy(khi[:], src).then_inc(khi_done, 1)
                    elif name == "v":
                        src, free = full(name, k)
                        wait(act, v_copied, 4 * (v + 1))
                        nc.scalar.copy(vnew[:].rearrange("p c f -> p (c f)"), src).then_inc(free, 1)
                    elif name in ("fxT", "h1T", "foT", "fxT_b", "h1T_b", "foT_b"):
                        t, b = tails(ph, v, tail_a, tail_b)[name.endswith("_b")]
                        src, free = full(name, k)
                        if name == t.use("fxT"):
                            nc.scalar.copy(t.fxT, src).then_inc(free, 1)
                        elif name == t.use("h1T"):
                            nc.scalar.activation(t.h1r, src, ACT.Relu, bias=fc1b_s).then_inc(free, 1)
                        else:
                            nc.scalar.copy(t.foT, src).then_inc(free, 1)

                for k in range(4):
                    for s in range(SLOTS):
                        if ph.block(k, 2):
                            b, n = head(v, k, 2)
                            for c in range(11):
                                if CHUNK_SLOT[c] == s:
                                    exps(b, n, c)
                        if ph.att and s == V_SLOT:
                            wait(act, o_done, (v - 1) * 4 + k + 1)
                            if k == 0:
                                act.wait_ge(sh_free[BANK["v", 3]], iteration_start(ph, v, BANK["v", 3]))
                            nc.scalar.copy(V[:, k], vnew[:, :, D * k:D * k + D]).then_inc(v_copied, 1)
                        side(k, s)
                        at = (k, s)
                        if ph.prep and at == SCALAR_AT["adj"]:
                            act.wait_ge(adj_in, (v + 2) * 16)
                            wait(act, g_dve.sem, g_dve.after(v, "agg1"))
                            nc.scalar.copy(adj_f[:].rearrange("p c j -> p (c j)"), adj_i[:].rearrange("p c j -> p (c j)")
                                           ).then_inc(g_act.sem, 1)
                        if ph.prev and at == SCALAR_AT["lex"]:
                            b = v - 1
                            act.wait_ge(x_dve.sem, x_dve.after(b, "lsub"))
                            nc.scalar.activation(lex[:], lsub[:], ACT.Exp).then_inc(x_act.sem, 1)
                        for t, b in tails(ph, v, tail_a, tail_b):
                            if at == SCALAR_AT["sq"]:
                                act.wait_ge(t.dve.sem, t.dve.after(b, "xc"))
                                nc.scalar.activation(t.sq, t.xc, ACT.Square).then_inc(t.act.sem, 1)
                            if at == SCALAR_AT["sq2"]:
                                act.wait_ge(t.dve.sem, t.dve.after(b, "xc2"))
                                nc.scalar.activation(t.sq, t.xc, ACT.Square).then_inc(t.act.sem, 1)
                            if at == SCALAR_AT["fex"]:
                                act.wait_ge(t.dve.sem, t.dve.after(b, "fsub"))
                                nc.scalar.activation(t.fex, t.fsub, ACT.Exp).then_inc(t.act.sem, 1)

            run(act, body)

        @block.vector
        def _(dve):
            nc.vector.memset(KT[96:98], -MSCALE).then_inc(k_rows, 1)

            def place():
                dve.wait_ge(w_in, 16 * N_W)
                dve.wait_ge(c_done, 3)
                b4 = blocks[:].unsqueeze(2).to_broadcast([P, NH, D])
                for dst, src in ((wk_s, wp_s[:, WP["wk"]]), (wv_s, wp_s[:, WP["wv"]]), (fc1_s, wd_s[:, WD["fc1"]]),
                                 (fc2_s, wd_s[:, WD["fc2"]])):
                    nc.vector.tensor_tensor(dst[:].rearrange("p (n o) -> p n o", n=NH),
                                            src.unsqueeze(1).to_broadcast([P, NH, D]), b4, ALU.mult)
                nc.vector.tensor_tensor(wq_s[:], wp_s[:, WP["wq"]].unsqueeze(1).to_broadcast([P, NH, NE * D]),
                                        blocks[:].unsqueeze(2).to_broadcast([P, NH, NE * D]), ALU.mult)
                nc.vector.tensor_copy(fgT_s[:, 0:NH], wp_s[:, WP["fgate"]])
                gate = wp_s[:, WP["gate"]].rearrange("p (n e) -> p n e", n=NH)
                for n in range(NH):
                    i = nc.vector.tensor_tensor(nat_w[:, n, P:NATW].rearrange("p (f e) -> p f e", f=NE),
                                                gate[:, n].unsqueeze(1).to_broadcast([P, NE, NE]),
                                                blocks[:].unsqueeze(2).to_broadcast([P, NE, NE]), ALU.mult)
                i.then_inc(placed, 1)

            def body(ph, v):
                def full(name, k):
                    bank, c = use_count(ph, v, name, k)
                    dve.wait_ge(sh_full[bank], c + 1)
                    return SH[:, bank], sh_free[bank]

                def done(name, k):
                    bank, c = use_count(ph, v, name, k)
                    dve.wait_ge(sh_free[bank], c + 1)

                def reduce_max(b, n, pos):
                    dve.wait_ge(mx_full, (b * NH + n) * TILES + pos + 1)
                    if pos == 0:
                        wait(dve, m2_done, (b * 4 + n - 1) * 2)
                    c, e0, ne = MAX_TILES[pos]
                    w = P * (c + 1)
                    tile = MX[:, mx_bank(n, pos), 0:ne * w].rearrange("p (e t) -> p e t", e=ne)
                    nc.vector.tensor_reduce(mx[:, n % 2, e0:e0 + ne, c], tile, AX.X, ALU.max).then_inc(mx_free, 1)

                def layernorm_stats(b, src, two):
                    for c in range(C):
                        st = nc.vector.bn_stats(bst[:, c, :], src[:, c, :])
                    st.then_inc(g_dve.sem, 1)
                    dve.wait_ge(g_dve.sem, g_dve.after(b, "stats" + two))
                    held(dve)
                    for c in range(C):
                        st = nc.vector.bn_aggr(mv[:, c, :], bst[:, c, :])
                    st.then_inc(g_dve.sem, 1)
                    dve.wait_ge(g_dve.sem, g_dve.after(b, "aggr" + two))
                    nc.vector.tensor_scalar(ve[:], mv[:, :, 1], EPS_GNN, None, ALU.add).then_inc(g_dve.sem, 1)

                def normalise(b, src, two):
                    dve.wait_ge(g_pool.sem, g_pool.after(b, "rs" + two))
                    for c in range(C):
                        i = nc.vector.tensor_scalar(xn[:, c, :], src[:, c, :], mv[:, c, 0:1], rs[:, c:c + 1],
                                                    ALU.subtract, ALU.mult)
                    i.then_inc(g_dve.sem, 1)

                def aggregate(b, i):
                    src, free = full(f"msg{i}", 1)
                    m = src[:, 0:260].rearrange("p (c w) -> p c w", c=2)
                    nc.vector.tensor_scalar(dmax[:], m[:, :, H], 1.0, None, ALU.max).then_inc(g_dve.sem, 1)
                    dve.wait_ge(g_dve.sem, g_dve.after(b, f"deg{i}"))
                    nc.vector.reciprocal(drec[:], dmax[:]).then_inc(g_dve.sem, 1)
                    dve.wait_ge(g_dve.sem, g_dve.after(b, f"rec{i}"))
                    nc.vector.scalar_tensor_tensor(out=dgs[:], in0=m[:, :, H], scalar=0.0, in1=drec[:], op0=ALU.is_gt,
                                                   op1=ALU.mult).then_inc(g_dve.sem, 1)
                    dve.wait_ge(g_dve.sem, g_dve.after(b, f"gs{i}"))
                    c = 2 * i
                    nc.vector.scalar_tensor_tensor(out=agg[:, c, :], in0=m[:, 0, 0:H], scalar=dgs[:, 0:1], in1=upd[:, c, :],
                                                   op0=ALU.mult, op1=ALU.add).then_inc(g_dve.sem, 1)
                    nc.vector.scalar_tensor_tensor(out=agg[:, c + 1, :], in0=m[:, 1, 0:H], scalar=dgs[:, 1:2],
                                                   in1=upd[:, c + 1, :], op0=ALU.mult, op1=ALU.add).then_inc(free, 1)

                def prep(b, at):
                    if at == VECTOR_AT["stats"]:
                        dve.wait_ge(x_in, (b + 1) * 16)
                        layernorm_stats(b, xin, "")
                    if at == VECTOR_AT["xn"]:
                        normalise(b, xin, "")
                    for i in range(2):
                        if at != VECTOR_AT[f"upd{i}"]:
                            continue
                        src, free = full(f"hu{i}", 0)
                        dve.wait_ge(g_act.sem, g_act.after(b, f"h{i}"))
                        nc.vector.tensor_tensor(upd[:, 2 * i:2 * i + 2, :],
                                                src.rearrange("p (c w) -> p c w", c=2)[:, :, H:2 * H],
                                                gnnb_s.unsqueeze(1).to_broadcast([P, 2, H]), ALU.add).then_inc(free, 1)
                    if at == VECTOR_AT["agg0"]:
                        aggregate(b, 0)
                    if at == VECTOR_AT["agg1"]:
                        aggregate(b, 1)
                    if at == VECTOR_AT["x2"]:
                        done("msg0", 1)
                        done("msg1", 1)
                        wait(dve, x2_kept, 16 * b)
                        nc.vector.scalar_tensor_tensor(out=x2[:], in0=agg[:], scalar=0.0, in1=xin[:], op0=ALU.max,
                                                       op1=ALU.add).then_inc(g_dve.sem, 1)
                    if at == VECTOR_AT["stats2"]:
                        dve.wait_ge(g_dve.sem, g_dve.after(b, "x2"))
                        layernorm_stats(b, x2, "2")
                    if at == VECTOR_AT["xn2"]:
                        normalise(b, x2, "2")
                    if at == VECTOR_AT["nz"]:
                        done("sxT", 3)
                        wait(dve, nz_out, b * 16)
                        nc.vector.tensor_scalar(nzT[:], sxT[:], 0.0, None, ALU.not_equal).then_inc(g_dve.sem, 1)

                def read(name, k):
                    if name == "q":
                        b, n = (v, k + 1) if k < 3 else (v + 1, 0)
                        src, free = full(name, k)
                        dve.wait_ge(qhi_done, b * 4 + n + 1)
                        nc.vector.tensor_tensor(qlo[:], src, qhi[:], ALU.subtract).then_inc(free, 1)
                    elif name == "kT":
                        src, free = full(name, k)
                        dve.wait_ge(khi_done, (v + 1) * 2 + 1)
                        nc.vector.tensor_tensor(klo[:], src, khi[:], ALU.subtract).then_inc(free, 1)
                        dve.wait_ge(free, use_count(ph, v, name, k)[1] + 1)
                        dve.sem_inc(khi_done, 1)
                    elif name == "LT":
                        b, n = head(v, k, 3)
                        src, free = full(name, k)
                        wait(dve, x_dve.sem, x_dve.after(b - 1, "lw2"))
                        nc.vector.reciprocal(rL[:, n], src.rearrange("p (c e r) -> p c e r", c=C, e=NE)[:, :, :, 0]
                                             ).then_inc(free, 1)
                    elif name == "sxn":
                        b = v + 1
                        src, free = full(name, k)
                        nc.vector.tensor_copy(resid[:, :, b, :], src.rearrange("p (c n d) -> p c n d", c=C, n=NH)[:, :, b, :]
                                              ).then_inc(free, 1)

                def mix(b, at):
                    z = nat[:].rearrange("p n c w -> p (n c) w")[:, :, P:NATW].rearrange("p g (f e) -> p g e f", f=NE)
                    r = rL[:].rearrange("p n c e -> p (n c) e")

                    def step(name, ins):
                        ins.then_inc(x_dve.sem, 1)
                        dve.wait_ge(x_dve.sem, x_dve.after(b, name))

                    if at == VECTOR_AT["gate"]:
                        for name in ("LT", "nat1"):
                            bank, c = use_count(ph, v, name, 2)
                            dve.wait_ge(sh_free[bank], c + 1)
                        wait(dve, x_pool.sem, x_pool.after(b - 1, "prod3"))
                        step("zr", nc.vector.tensor_tensor(zr[:], z, r.unsqueeze(2).to_broadcast([P, G16, NE, NE]), ALU.mult))
                        step("lg", nc.vector.tensor_reduce(lg[:], zr[:], AX.X, ALU.add))
                        step("lgb", nc.vector.tensor_tensor(lgb[:].rearrange("p (n c) e -> p n c e", n=NH),
                                                            lg[:].rearrange("p (n c) e -> p n c e", n=NH),
                                                            gb_s.unsqueeze(2).to_broadcast([P, NH, C, NE]), ALU.add))
                        step("lmax", nc.vector.tensor_reduce(lmax[:], lgb[:], AX.X, ALU.max))
                        nc.vector.tensor_tensor(lsub[:], lgb[:], lmax[:].unsqueeze(2).to_broadcast([P, G16, NE]),
                                                ALU.subtract).then_inc(x_dve.sem, 1)
                    if at == VECTOR_AT["gate2"]:
                        dve.wait_ge(x_act.sem, x_act.after(b, "lex"))
                        step("lsum", nc.vector.tensor_reduce(lsum[:], lex[:], AX.X, ALU.add))
                        step("lrec", nc.vector.reciprocal(lrec[:], lsum[:]))
                        step("lw", nc.vector.tensor_tensor(lw[:], lex[:], lrec[:].unsqueeze(2).to_broadcast([P, G16, NE]),
                                                           ALU.mult))
                        step("lw2", nc.vector.tensor_tensor(lw2[:], lw[:], r, ALU.mult))
                        for n in range(NH if ph.ending else 0):
                            mix_head(dve, b, n)

                def tail(t, b, at):
                    def step(name, ins):
                        ins.then_inc(t.dve.sem, 1)
                        dve.wait_ge(t.dve.sem, t.dve.after(b, name))

                    def slot(ring):
                        size = ring.shape[1]
                        return ring[:, b % size] if isinstance(b, int) else ring[:, bass.ds(b % size, 1)].rearrange("p a f -> p (a f)")

                    def mean(two):
                        step("sum" + two, nc.vector.tensor_reduce(t.sum, t.y, AX.X, ALU.add))
                        step("mean" + two, nc.vector.tensor_scalar(t.mean, t.sum, 1.0 / D, None, ALU.mult))

                    def centre(two):
                        step("xc" + two, nc.vector.tensor_tensor(t.xc, t.y, t.mean.unsqueeze(2).to_broadcast([P, G16, D]),
                                                                 ALU.subtract))

                    def variance(two):
                        dve.wait_ge(t.act.sem, t.act.after(b, "sq" + two))
                        step("vs" + two, nc.vector.tensor_reduce(t.vs, t.sq, AX.X, ALU.add))
                        step("ve" + two, nc.vector.tensor_scalar(t.ve, t.vs, 1.0 / D, EPS_FFN, ALU.mult, ALU.add))

                    def scaled(two):
                        dve.wait_ge(t.pool.sem, t.pool.after(b, "rs" + two))
                        step("xs" + two, nc.vector.tensor_tensor(t.xs, t.xc, t.rs.unsqueeze(2).to_broadcast([P, G16, D]),
                                                                 ALU.mult))

                    def products(*steps):
                        for name in steps if ph.ending else ():
                            product(dve, ph, v, t, b, name)

                    if at == VECTOR_AT["y"]:
                        dve.wait_ge(mix_kept, (b + 1) * 16)
                        step("y", nc.vector.tensor_tensor(t.y.rearrange("p g d -> p (g d)"), slot(mixring),
                                                          resid[:].rearrange("p c n d -> p (c n d)"), ALU.add))
                        mean("")
                    if at == VECTOR_AT["xc"]:
                        centre("")
                    if at == VECTOR_AT["var"]:
                        variance("")
                    if at == VECTOR_AT["xs"]:
                        scaled("")
                        products("g", "fx")
                    if at == VECTOR_AT["nzf"]:
                        done(t.use("fxT"), 1)
                        step("nzf", nc.vector.tensor_scalar(t.nzf, t.fxT, 0.0, None, ALU.not_equal))
                        products("h1m")
                    if at == VECTOR_AT["y2"]:
                        src, free = full(t.use("h2"), 2)
                        step("u", nc.vector.tensor_tensor(t.u, src.rearrange("p (g d) -> p g d", d=D),
                                                          fc2b_s.unsqueeze(1).to_broadcast([P, G16, D]), ALU.add))
                        dve.sem_inc(free, 1)
                        step("w", nc.vector.scalar_tensor_tensor(out=t.w, in0=t.fx, scalar=0.0, in1=t.u, op0=ALU.not_equal,
                                                                 op1=ALU.mult))
                        step("y2", nc.vector.tensor_tensor(t.y, t.w, t.fx, ALU.add))
                    if at == VECTOR_AT["mean2"]:
                        mean("2")
                    if at == VECTOR_AT["xc2"]:
                        centre("2")
                    if at == VECTOR_AT["var2"]:
                        variance("2")
                    if at == VECTOR_AT["xs2"]:
                        scaled("2")
                        products("g2", "fo")
                    if at == VECTOR_AT["head"]:
                        src, free = full(t.use("fg"), 3)
                        l4 = src[:, 0:C * FGW].rearrange("p (c n) -> p c n", c=C)[:, :, 0:NH]
                        step("fmax", nc.vector.tensor_reduce(t.fmax, l4, AX.X, ALU.max))
                        step("fsub", nc.vector.tensor_tensor(t.fsub, l4, t.fmax.unsqueeze(2).to_broadcast([P, C, NH]),
                                                             ALU.subtract))
                        dve.sem_inc(free, 1)
                    if at == VECTOR_AT["head2"]:
                        dve.wait_ge(t.act.sem, t.act.after(b, "fex"))
                        step("fsum", nc.vector.tensor_reduce(t.fsum, t.fex, AX.X, ALU.add))
                        step("frec", nc.vector.reciprocal(t.frec, t.fsum))
                        step("fgs", nc.vector.tensor_tensor(t.fgs, t.fex, t.frec.unsqueeze(2).to_broadcast([P, C, NH]),
                                                            ALU.mult))
                    if at == VECTOR_AT["out"]:
                        products("fmul")
                        dve.wait_ge(t.pool.sem, t.pool.after(b, "fmul"))
                        dve.wait_ge(x2_kept, (b + 1) * 16)
                        if t is tail_a:
                            wait(dve, out_done, b * 16)
                        step("out", nc.vector.tensor_tensor(t.out, slot(x2ring), t.mul.rearrange("p g d -> p (g d)"),
                                                            ALU.add))

                for k in range(4):
                    for s in range(SLOTS):
                        at = (k, s)
                        if ph.block(k, 1) and s == SPLIT_SLOT:
                            b, n = head(v, k, 1)
                            i = b * 4 + n
                            before = use_before(ph, v, "mT", k)
                            if before:
                                dve.wait_ge(sh_full[before[0]], before[1])
                            dve.wait_ge(mx_free, (i + 1) * TILES)
                            top = mx[:, n % 2].rearrange("p e c -> p (e c)")
                            nc.vector.tensor_scalar(m2[:, 0:J], top, 1.0 / MSCALE, None, ALU.mult).then_inc(m2_done, 1)
                            dve.wait_ge(m2_done, i * 2 + 1)
                            nc.vector.scalar_tensor_tensor(out=m2[:, J:2 * J], in0=top, scalar=1.0 / MSCALE, in1=m2[:, 0:J],
                                                           op0=ALU.mult, op1=ALU.subtract).then_inc(m2_done, 1)
                        if ph.att:
                            for pos in range(TILES):
                                if MAX_SLOT[pos] == s:
                                    reduce_max(v, k, pos)
                        lag = 2 + ADD_SLOT[2] // SLOTS
                        if ADD_SLOT[2] % SLOTS == s and ph.block(k, lag):
                            add_chunk(dve, ph, v, k, *head(v, k, lag), C - 1)
                        if ph.block(k, 3) and s == OM_SLOT:
                            b, n = head(v, k, 3)
                            dve.wait_ge(o_done, b * 4 + n + 1)
                            dve.wait_ge(mask_in[n], (b + 1) * 16)
                            before = use_before(ph, v, "nat1", k)
                            if before:
                                dve.wait_ge(sh_full[before[0]], before[1])
                            nc.vector.tensor_tensor(Om[:], O[:], mrep[:, n, :], ALU.mult).then_inc(om_done, 1)
                        for name, uk, us, _ in USES:
                            if (uk, us) == at and ph.has(name, k):
                                read(name, k)
                        if ph.prep:
                            prep(v + 1, at)
                        if ph is PHASES[0] and at == VECTOR_AT["xn"]:
                            place()
                        if ph.prev:
                            mix(v - 1, at)
                        for t, b in tails(ph, v, tail_a, tail_b):
                            tail(t, b, at)

            run(dve, body)


def kernel(x, adj, L0_gnn_W_msg, L0_gnn_W_upd, L0_gnn_bias, L0_ffn_hl_w, L0_ffn_hl_b, L0_ffn_wq, L0_ffn_wk, L0_ffn_wv,
           L0_ffn_gate_w, L0_ffn_gate_b, L0_ffn_ln_g, L0_ffn_ln_b, L0_ffn_fc1_w, L0_ffn_fc1_b, L0_ffn_fc2_w, L0_ffn_fc2_b,
           L0_ffn_fnorm_g, L0_ffn_fnorm_b, L0_ffn_fgate_w):
    import concourse.bacc as bacc
    from concourse.bass_utils import run_bass_kernel_spmd

    def lay(a, *shape, perm=None):
        a = np.asarray(a)
        if perm is not None:
            a = a.transpose(perm)
        return np.ascontiguousarray(a.reshape(shape) if shape else a)

    arrays = {
        "x": lay(x),
        "adj": lay(adj),
        "w_mu": np.stack([np.asarray(L0_gnn_W_msg), np.asarray(L0_gnn_W_upd)]),
        "w_p": np.concatenate([lay(L0_ffn_hl_w, H, H, perm=(2, 0, 1)), lay(L0_ffn_hl_b, H, 1),
                               lay(L0_ffn_wq, H, NE * D, perm=(0, 3, 1, 2)), lay(L0_ffn_wk, H, D, perm=(0, 2, 1)),
                               lay(L0_ffn_wv, H, D, perm=(0, 2, 1)),
                               lay(np.asarray(L0_ffn_gate_w).reshape(NH, NE, NE, D), H, NH * NE, perm=(2, 3, 0, 1)),
                               lay(L0_ffn_fgate_w, perm=(1, 0))], axis=1),
        "w_d": np.concatenate([lay(L0_ffn_fc1_w, perm=(1, 0)), lay(L0_ffn_fc2_w, perm=(1, 0)), lay(L0_ffn_fc1_b, D, 1)],
                              axis=1),
        "w_r": np.concatenate([lay(a, 1, -1) for a in (L0_gnn_bias, L0_ffn_gate_b, L0_ffn_ln_g, L0_ffn_ln_b, L0_ffn_fc2_b,
                                                       L0_ffn_fnorm_g, L0_ffn_fnorm_b)], axis=1),
    }
    nc = bacc.Bacc("TRN2", target_bir_lowering=False, num_devices=1)
    args = [nc.dram_tensor(name, a.shape, mybir.dt.from_np(a.dtype), kind="ExternalInput").ap() for name, a in arrays.items()]
    out = nc.dram_tensor("out", (B, S, H), F32, kind="ExternalOutput").ap()
    build(nc, *args, out)
    r = run_bass_kernel_spmd(nc, [arrays], core_ids=[0])
    return r.results[0]["out"]
```
